# Optimizing a Trainium2 kernel written in Bass

```python
import numpy as np
import jax
import jax.numpy as jnp

def _softmax(x, axis=-1):
    return jax.nn.softmax(x, axis=axis)

def _gelu(x):
    return jax.nn.gelu(x, approximate=True)

def _silu(x):
    return jax.nn.silu(x)

def _sigmoid(x):
    return jax.nn.sigmoid(x)

def _layernorm(x, axis=-1, eps=1e-05):
    m = jnp.mean(x, axis=axis, keepdims=True)
    v = jnp.var(x, axis=axis, keepdims=True)
    return (x - m) / jnp.sqrt(v + eps)

def _scatter_add(tgt, idx, src, axis=0):
    return tgt.at[idx].add(src)

def _segment_sum(src, seg, n):
    return jax.ops.segment_sum(src, seg, n)
kernel_name = 'mk_gps_d1_gnn_r8_55055e'

def setup_inputs(seed: int=0):
    np.random.seed(seed)
    _w = jnp.asarray

    def _rec_inputs():
        import jax
        import jax.numpy as jnp
        _gk = jax.random.key(seed)
        x = -8.776e-05 + 1 * jax.random.normal(jax.random.fold_in(_gk, 1), (6250, 512), jnp.float32)
        src = jax.random.randint(jax.random.fold_in(_gk, 2), (100000,), 0, 6250, jnp.int32)
        dst = jnp.minimum((6250 * jax.random.uniform(jax.random.fold_in(_gk, 3), (100000,)) ** 2.0).astype(jnp.int32), 49999)
        _o = jnp.argsort(dst, stable=True)
        src = src[_o]
        dst = dst[_o]
        return (x, src, dst)
    x, src, dst = _rec_inputs()

    def _L0_gnn_setup():
        import jax, jax.numpy as jnp
        import numpy as np
        N = 1250
        E = 20000
        DIN = 512
        DOUT = 512
        key = jax.random.key(seed)
        k1, k2, k3 = jax.random.split(key, 3)
        x = jax.random.normal(k1, (N, DIN), dtype=jnp.float32)
        edge_index = jax.random.randint(k2, (2, E), 0, N, dtype=jnp.int32)
        W = jax.random.normal(k3, (DIN, DOUT), dtype=jnp.float32) * (1.0 / np.sqrt(DIN))
        b = jnp.zeros((DOUT,), dtype=jnp.float32)
        return {'x': x, 'edge_index': edge_index, 'W': W, 'b': b}
    _L0_gnn_all = _L0_gnn_setup()
    _L0_gnn_in = {k: v for k, v in _L0_gnn_all.items() if k in ('W', 'b')}
    del _L0_gnn_all

    def _L0_mix_setup():
        import jax, jax.numpy as jnp
        import numpy as np
        DIM = 512
        HEADS = 8
        DIM_HEAD = 64
        INNER = HEADS * DIM_HEAD
        key = jax.random.key(seed)
        k1, k2, k3, k4 = jax.random.split(key, 4)
        x = jax.random.normal(k1, (4, 1024, DIM), dtype=jnp.float32)
        w_qkv = jax.random.normal(k2, (DIM, 3 * INNER), dtype=jnp.float32) / np.sqrt(DIM)
        w_out = jax.random.normal(k3, (INNER, DIM), dtype=jnp.float32) / np.sqrt(INNER)
        b_out = jax.random.normal(k4, (DIM,), dtype=jnp.float32) * 0.01
        return {'x': x, 'w_qkv': w_qkv, 'w_out': w_out, 'b_out': b_out}
    _L0_mix_all = _L0_mix_setup()
    _L0_mix_in = {k: v for k, v in _L0_mix_all.items() if k in ('w_qkv', 'w_out', 'b_out')}
    del _L0_mix_all

    def _L0_ffn_setup():
        import jax, jax.numpy as jnp
        import numpy as np
        K = 2
        EPS = 1e-06

        def _layernorm(x, gamma, beta):
            mu = jnp.mean(x, axis=-1, keepdims=True)
            var = jnp.mean(jnp.square(x - mu), axis=-1, keepdims=True)
            return (x - mu) * jax.lax.rsqrt(var + EPS) * gamma + beta
        key = jax.random.key(seed)
        ks = jax.random.split(key, 5)
        B, S, D, F, E = (8, 256, 512, 256, 8)
        x = jax.random.normal(ks[0], (B, S, D), dtype=jnp.float32)
        router_w = jax.random.normal(ks[1], (D, E), dtype=jnp.float32) * 0.02
        w1 = jax.random.normal(ks[2], (E, D, F), dtype=jnp.float32) * 0.02
        b1 = jnp.zeros((E, F), dtype=jnp.float32)
        w2 = jax.random.normal(ks[3], (E, F, D), dtype=jnp.float32) * 0.02
        b2 = jnp.zeros((E, D), dtype=jnp.float32)
        gamma = jnp.ones((E, D), dtype=jnp.float32)
        beta = jnp.zeros((E, D), dtype=jnp.float32)
        return {'x': x, 'router_w': router_w, 'w1': w1, 'b1': b1, 'w2': w2, 'b2': b2, 'gamma': gamma, 'beta': beta}
    _L0_ffn_all = _L0_ffn_setup()
    _L0_ffn_in = {k: v for k, v in _L0_ffn_all.items() if k in ('router_w', 'w1', 'b1', 'w2', 'b2', 'gamma', 'beta')}
    del _L0_ffn_all
    return {'x': x, 'src': src, 'dst': dst, 'L0_gnn_W': _L0_gnn_in['W'], 'L0_gnn_b': _L0_gnn_in['b'], 'L0_mix_w_qkv': _L0_mix_in['w_qkv'], 'L0_mix_w_out': _L0_mix_in['w_out'], 'L0_mix_b_out': _L0_mix_in['b_out'], 'L0_ffn_router_w': _L0_ffn_in['router_w'], 'L0_ffn_w1': _L0_ffn_in['w1'], 'L0_ffn_b1': _L0_ffn_in['b1'], 'L0_ffn_w2': _L0_ffn_in['w2'], 'L0_ffn_b2': _L0_ffn_in['b2'], 'L0_ffn_gamma': _L0_ffn_in['gamma'], 'L0_ffn_beta': _L0_ffn_in['beta']}

def reference(x, src, dst, L0_gnn_W, L0_gnn_b, L0_mix_w_qkv, L0_mix_w_out, L0_mix_b_out, L0_ffn_router_w, L0_ffn_w1, L0_ffn_b1, L0_ffn_w2, L0_ffn_b2, L0_ffn_gamma, L0_ffn_beta):
    import jax
    import jax.numpy as jnp

    def _L0_gnn_ref(x, edge_index, W, b):
        import jax, jax.numpy as jnp
        import numpy as np
        N = 1250
        E = 20000
        DIN = 512
        DOUT = 512
        n = x.shape[0]
        src, dst = (edge_index[0], edge_index[1])
        loop = jnp.arange(n, dtype=src.dtype)
        src = jnp.concatenate([src, loop])
        dst = jnp.concatenate([dst, loop])
        deg = jax.ops.segment_sum(jnp.ones_like(src, dtype=x.dtype), dst, num_segments=n)
        dinv = jnp.where(deg > 0, jax.lax.rsqrt(jnp.maximum(deg, 1e-12)), 0.0)
        norm = dinv[src] * dinv[dst]
        h = x @ W
        msg = h[src] * norm[:, None]
        out = jax.ops.segment_sum(msg, dst, num_segments=n) + b
        return jax.nn.relu(out)

    def _L0_mix_ref(x, w_qkv, w_out, b_out):
        import jax, jax.numpy as jnp
        import numpy as np
        DIM = 512
        HEADS = 8
        DIM_HEAD = 64
        INNER = HEADS * DIM_HEAD
        b, n, d = x.shape
        qkv = x @ w_qkv
        q, k, v = jnp.split(qkv, 3, axis=-1)

        def to_heads(t):
            return t.reshape(b, n, HEADS, DIM_HEAD).transpose(0, 2, 1, 3)
        q, k, v = map(to_heads, (q, k, v))
        q = jax.nn.elu(q) + 1.0
        k = jax.nn.elu(k) + 1.0
        kv = jnp.einsum('bhnd,bhnm->bhdm', k, v)
        z = 1.0 / (jnp.einsum('bhnd,bhd->bhn', q, k.sum(axis=2)) + 1e-06)
        out = jnp.einsum('bhnd,bhdm->bhnm', q, kv) * z[..., None]
        out = out.transpose(0, 2, 1, 3).reshape(b, n, INNER)
        return out @ w_out + b_out

    def _L0_ffn_ref(x, router_w, w1, b1, w2, b2, gamma, beta):
        import jax, jax.numpy as jnp
        import numpy as np
        K = 2
        EPS = 1e-06

        def _layernorm(x, gamma, beta):
            mu = jnp.mean(x, axis=-1, keepdims=True)
            var = jnp.mean(jnp.square(x - mu), axis=-1, keepdims=True)
            return (x - mu) * jax.lax.rsqrt(var + EPS) * gamma + beta
        B, S, D = x.shape
        E = w1.shape[0]
        xf = x.reshape(-1, D)
        logits = xf @ router_w
        gate_vals, idx = jax.lax.top_k(logits, K)
        gates = jax.nn.softmax(gate_vals, axis=-1)
        out = jnp.zeros_like(xf)
        for e in range(E):
            h = jax.nn.relu(xf @ w1[e] + b1[e]) @ w2[e] + b2[e]
            y = _layernorm(xf + h, gamma[e], beta[e])
            w = jnp.sum(jnp.where(idx == e, gates, 0.0), axis=-1)
            out = out + w[:, None] * y
        return out.reshape(B, S, D)
    edge_index = jnp.stack([src, dst])
    xn = _layernorm(x, axis=-1)
    x = x + _L0_gnn_ref(xn, edge_index, L0_gnn_W, L0_gnn_b) + _L0_mix_ref(xn[None], L0_mix_w_qkv, L0_mix_w_out, L0_mix_b_out)[0]
    x = x + _L0_ffn_ref(_layernorm(x, axis=-1)[None], L0_ffn_router_w, L0_ffn_w1, L0_ffn_b1, L0_ffn_w2, L0_ffn_b2, L0_ffn_gamma, L0_ffn_beta)[0]
    return x

_drawn_inputs = setup_inputs


def setup_inputs(seed=0):
    import zlib

    import numpy as np

    out = dict(_drawn_inputs(seed))
    spreads = {'L0_gnn_b': (0.0, 0.1),
     'L0_ffn_b1': (0.0, 0.8),
     'L0_ffn_b2': (0.0, 0.1),
     'L0_ffn_gamma': (1.0, 0.2),
     'L0_ffn_beta': (0.0, 0.1)}
    factors = {'L0_mix_w_qkv': 3.4, 'L0_mix_w_out': 3.579, 'L0_mix_b_out': 4.738}
    for name, (base, spread) in spreads.items():
        noise = np.random.default_rng([zlib.crc32(name.encode()), seed]).standard_normal(out[name].shape)
        drawn = base * np.exp(spread * noise) if base else spread * noise
        out[name] = jnp.asarray(drawn.astype(out[name].dtype))
    for name, factor in factors.items():
        out[name] = (out[name] * factor).astype(out[name].dtype)
    return out
```

```python
from contextlib import ExitStack

import concourse.bass as bass
from concourse import mybir

FP32 = mybir.dt.float32
BF16 = mybir.dt.bfloat16
I32 = mybir.dt.int32
U32 = mybir.dt.uint32
ALU = mybir.AluOpType
ACT = mybir.ActivationFunctionType

P = 128
N = 6250
D = 512
E = 100000
C = D // P
HEAD = 64
NX = 8
F = 256
FC = F // P
EPS_LN = 1e-5
EPS_MOE = 1e-6
EPS_Z = 1e-6

NT = 50
REAL = -(-N // P)
LAST = N - (REAL - 1) * P
WINDOWS = REAL
PAIR = 2 * P
BLOCKS = -(-E // PAIR)
BG = -(-BLOCKS // P)
STEPS = 8
TURNS = -(-(BLOCKS + WINDOWS - 1) // STEPS)
T = TURNS * STEPS
SLOTS = 2 * STEPS
MB = 106
ROWS = NT * P


class Mem:

    def __init__(self, tensor, size):
        self.t, self.size, self.at = tensor, size, 0

    def take(self, *shape, dt=FP32):
        n = 1
        for s in shape:
            n *= s
        words = n if dt in (FP32, I32, U32) else -(-n // 2)
        words = -(-words // 8) * 8
        assert self.at + words <= self.size, (self.at, words, self.size)
        v = self.t[:, self.at:self.at + words]
        self.at += words
        if dt != FP32:
            v = v.bitcast(dt)
        v = v[:, 0:n]
        if len(shape) == 2:
            v = v.rearrange("p (a b) -> p a b", b=shape[1])
        elif len(shape) == 3:
            v = v.rearrange("p (a b c) -> p a b c", b=shape[1], c=shape[2])
        return v


class Chain:

    def __init__(self, eng, sem):
        self.eng, self.sem, self.n = eng, sem, 0

    def __call__(self, ins):
        self.add(ins)
        self.wait()

    def add(self, ins):
        ins.then_inc(self.sem, 1)
        self.n = self.n + 1

    def wait(self):
        self.eng.wait_ge(self.sem, self.n)

    def loop(self, i, per):
        self.base, self.per, self.start = self.n, per, self.n
        self.n = per * i + self.n
        self.inside = 0

    def done(self, count):
        self.n = self.base + self.per * count


def tile_of(x, t):
    return x[:, bass.ds(t, 1), :].rearrange("p a n -> p (a n)")


def flat(v):
    return v.rearrange("p a b -> p (a b)")


def build(nc, x, src, dst, gW, gb, wqkv, wout, bout, rw, w1, b1, w2, b2, gamma, beta, out):
    with ExitStack() as ctx:
        uid = [0]

        retired = []

        def stage(run, *args):
            own = []

            def sem(name):
                uid[0] += 1
                own.append(nc.alloc_semaphore(name=f"{name}_{uid[0]}"))
                return own[-1]

            keep.at = mark
            run(nc, sem, d, k, X, keep, *args)
            for s in retired:
                nc.release_semaphore(s)
            retired[:] = own
            if run is not combine:
                for s in own:
                    nc.gpsimd.sem_clear(s)

        def dram(name, shape, dt=FP32):
            return nc.dram_tensor(name, shape, dt, kind="Internal").ap()

        d = dict(
            xnT=dram("xnT_scratch", (NT, P, D)),
            xb=dram("xb_scratch", (ROWS, D)),
            h=dram("h_scratch", (ROWS, D)),
            xm=dram("xm_scratch", (ROWS, D)),
            x1=dram("x1_scratch", (ROWS, D)),
            xs=dram("xs_scratch", (MB * P, D)),
            ys=dram("ys_scratch", (MB * P, D)),
        )
        big = ctx.enter_context(nc.sbuf_tensor("big", [P, NT * D], FP32))
        WORK = 26400
        work = ctx.enter_context(nc.sbuf_tensor("work", [P, WORK], FP32))
        X = big[:, :].rearrange("p (t n) -> p t n", n=D)
        keep = Mem(work, WORK)
        k = dict(
            ident=keep.take(P), tri=keep.take(P), ones=keep.take(P), bd=keep.take(P), iota=keep.take(P),
            pidx=keep.take(1), eps=keep.take(1), epsm=keep.take(1), epsz=keep.take(1),
            rowmask=keep.take(NT), stats=keep.take(NT, 6), rstd=keep.take(NT), nmr=keep.take(NT),
            sdeg=keep.take(NT), dinv=keep.take(NT), small=keep.take(8, NT),
            M1=keep.take(NT, NX), M2=keep.take(NT, NX), v12=keep.take(NT, 2),
            pos=keep.take(2, NT, dt=I32), gate=keep.take(2, NT),
            win=keep.take(T + STEPS, dt=I32), edge_src=keep.take(2 * (T + STEPS)), edge_dst=keep.take(2 * (T + STEPS)),
            expert=keep.take(MB, dt=I32), wr=keep.take(C, NX),
        )
        banks = [ctx.enter_context(nc.psum_tensor(f"bank{i}", [P, 512], FP32)) for i in range(8)]
        mark = keep.at
        stage(prepare, banks, x, src, dst, gW, bout)
        stage(mix, banks, wqkv, wout, gb)
        stage(route, banks, rw)
        stage(dispatch, banks)
        stage(experts, banks, w1, b1, w2, b2, gamma, beta)
        stage(combine, out)


def prepare(nc, sem, d, k, X, keep, banks, x, src, dst, gW, bout):
    W = keep.take(C, D)
    boutb = keep.take(D)
    xn = [keep.take(D) for _ in range(2)]
    xT = [keep.take(C, P) for _ in range(2)]
    xb = [keep.take(D) for _ in range(2)]
    nat_i = keep.take(BG, PAIR, dt=I32)
    nat_s = keep.take(BG, PAIR)
    nat_d = keep.take(BG, PAIR)
    dT = keep.take(2, BG * P, dt=I32)
    dT2 = keep.take(2, BG * P, dt=I32)
    lo = keep.take(2, BG * P, dt=BF16)
    hi = keep.take(2, BG * P, dt=BF16)
    HB = 16
    onelo = [keep.take(HB, P, dt=BF16) for _ in range(2)]
    onehi = [keep.take(HB, WINDOWS + 1, dt=BF16) for _ in range(2)]
    iota_b = keep.take(P, dt=BF16)
    iota_i = keep.take(T, dt=I32)
    iota_t = keep.take(T)
    zero = keep.take(D)
    onehot = keep.take(BG, T)
    spread = keep.take(2, P)
    block_of = keep.take(T)
    over_w = keep.take(T)
    S = k["small"]
    LOADS = 6
    per_load = (REAL - 1) // LOADS
    s_x = [sem(f"x_loaded{i}") for i in range(LOADS + 1)]
    s_xz, s_edges0, s_w = sem("x_pad_zeroed"), sem("edges_padded"), sem("weights_loaded")
    s_src, s_dst = sem("src_loaded"), sem("dst_loaded")
    s_iota, s_const = sem("iotas_made"), sem("constants_made")
    s_natd, s_dTp = sem("dst_converted"), sem("dst_transposed")
    s_var, s_sq, s_ln = sem("variances"), sem("std_done"), sem("ln_ready")
    s_xn, s_T, s_xT, s_h, s_hs = sem("xn_made"), sem("xn_transposed"), sem("xT_copied"), sem("h_made"), sem("h_kept")
    s_xb = sem("xb_made")
    s_xTst = [sem(f"xT_stored{u}") for u in range(2)]
    s_xbst = [sem(f"xb_stored{u}") for u in range(2)]
    s_lo, s_hist = sem("onehots_made"), sem("histogram_step")
    s_deg, s_sdeg, s_dinv = sem("degrees_done"), sem("sqrt_degree"), sem("dinv_made")
    s_sc = [sem(f"h_scaled{u}") for u in range(2)]
    s_hst, s_z, s_zst = sem("h_stored"), sem("zero_row"), sem("slots_zeroed")
    s_c, s_pe, s_sch = sem("vector_chain"), sem("schedule_products"), sem("schedule_tables")
    s_pc, s_ac = sem("pool_ordered"), sem("act_ordered")
    psT, psH, psD, psA, psB = banks[0:2], banks[2:4], banks[4], banks[5], banks[6]
    x_rows = x
    full = (BLOCKS - 1) // P * P
    rest = (E // PAIR) - full
    tail = E - (E // PAIR) * PAIR

    with nc.Block() as block:
        @block.sync
        def _(sp):
            sp.wait_ge(s_edges0, 2)
            for a, to, s in ((dst, nat_i, s_dst), (src, nat_s.bitcast(I32), s_src)):
                g = full // P
                sp.dma_start(to[:, 0:g, :], a[0:full * PAIR].rearrange("(g p j) -> p g j", p=P, j=PAIR)).then_inc(s, 16)
                sp.dma_start(to[0:rest, g, :], a[full * PAIR:(full + rest) * PAIR].rearrange("(p j) -> p j", j=PAIR)).then_inc(s, 16)
                sp.dma_start(to[rest:rest + 1, g, 0:tail], a[E - tail:E].rearrange("(p j) -> p j", p=1)).then_inc(s, 16)
            for i in range(LOADS):
                a = i * per_load
                sp.dma_start(X[:, a:a + per_load, :], x_rows[a * P:(a + per_load) * P, :].rearrange("(t p) n -> p t n", p=P)).then_inc(s_x[i], 16)
            sp.wait_ge(s_xz, 1)
            a = (REAL - 1) * P
            sp.dma_start(X[0:96, REAL - 1, :], x_rows[a:a + 96, :]).then_inc(s_x[LOADS], 16)
            sp.dma_start(X[96:LAST, REAL - 1, :], x_rows[a + 96:N, :]).then_inc(s_x[LOADS], 16)
            sp.dma_start(W, gW.rearrange("(c p) n -> p c n", p=P)).then_inc(s_w, 16)
            sp.dma_start(boutb, bout.rearrange("(a n) -> a n", a=1).broadcast_to([P, D])).then_inc(s_w, 16)
            sp.wait_ge(s_z, 1)
            sp.dma_start(d["xs"].rearrange("(b p) n -> p b n", p=P), zero.unsqueeze(1).to_broadcast([P, MB, D])).then_inc(s_zst, 16)
            with sp.Fori(0, NT // 2) as i:
                for u in range(2):
                    sp.wait_ge(s_xb, 2 * i + u + 1)
                    sp.dma_start(d["xb"][bass.ds((2 * i + u) * P, P), :], xb[u]).then_inc(s_xbst[u], 16)
                    sp.wait_ge(s_xT, 2 * i + u + 1)
                    sp.dma_start(d["xnT"][bass.ds(2 * i + u, 1), :, :].rearrange("a p n -> p (a n)"), flat(xT[u])).then_inc(s_xTst[u], 16)
            with sp.Fori(0, NT // 2) as i:
                sp.wait_ge(s_sc[0], i + 1)
                sp.wait_ge(s_sc[1], i + 1)
                sp.dma_start(d["h"][bass.ds(i * 2 * P, 2 * P), :].rearrange("(t p) n -> p t n", p=P), X[:, bass.ds(2 * i, 2), :]).then_inc(s_hst, 16)
            for u in range(2):
                sp.wait_ge(s_xTst[u], 16 * (NT // 2) + 16)
                sp.wait_ge(s_xbst[u], 16 * (NT // 2) + 16)
            sp.wait_ge(s_hst, 16 * (NT // 2))
            sp.wait_ge(s_zst, 16)

        @block.gpsimd
        def _(pool):
            nc.gpsimd.iota(iota_i, [[1, T]], base=0, channel_multiplier=0).then_inc(s_iota, 1)
            nc.gpsimd.iota(dT[:, 0, 0:1], [[1, 1]], base=0, channel_multiplier=1).then_inc(s_iota, 1)
            pool.wait_ge(s_w, 32)
            pool.wait_ge(s_x[LOADS], 32)
            for i in range(LOADS):
                pool.wait_ge(s_x[i], 16)
            pool.wait_ge(s_const, 1)
            with pool.Fori(0, NT // 2) as i:
                for u in range(2):
                    pool.wait_ge(s_xbst[u], 16 * i + 16)
                    pool.sem_inc(s_pc, 1)
                    nc.gpsimd.tensor_tensor(xb[u], tile_of(X, 2 * i + u), boutb, ALU.add).then_inc(s_xb, 1)

        @block.scalar
        def _(act):
            act.wait_ge(s_var, 1)
            nc.scalar.activation(S[:, 0, :], S[:, 1, :], ACT.Sqrt, bias=k["eps"]).then_inc(s_sq, 1)
            act.wait_ge(s_ln, 1)
            with act.Fori(0, NT // 2) as i:
                for u in range(2):
                    act.wait_ge(s_T, 2 * i + u + 1)
                    act.sem_inc(s_ac, 1)
                    nc.scalar.activation(xn[u], tile_of(X, 2 * i + u), ACT.Identity,
                                         bias=k["nmr"][:, bass.ds(2 * i + u, 1)], scale=k["rstd"][:, bass.ds(2 * i + u, 1)]).then_inc(s_xn, 1)
                    act.wait_ge(s_T, 2 * i + u + 3)
                    act.wait_ge(s_h, 2 * i + u + 1)
                    act.wait_ge(s_xTst[u], 16 * i + 16)
                    nc.scalar.copy(flat(xT[u]), psT[u][:, :]).then_inc(s_xT, 1)
            act.wait_ge(s_deg, 1)
            nc.scalar.activation(k["sdeg"], S[:, 2, :], ACT.Sqrt).then_inc(s_sdeg, 1)
            act.wait_ge(s_dinv, 1)
            act.wait_ge(s_hs, NT + 2)
            with act.Fori(0, NT // 2) as i:
                t = tile_of(X, 2 * i + 1)
                nc.scalar.activation(t, t, ACT.Identity, scale=k["dinv"][:, bass.ds(2 * i + 1, 1)]).then_inc(s_sc[1], 1)

        @block.vector
        def _(dve):
            link = Chain(dve, s_c)
            nc.vector.memset(nat_i, -1).then_inc(s_edges0, 1)
            nc.vector.memset(nat_s.bitcast(I32), 0).then_inc(s_edges0, 1)
            nc.vector.memset(X[:, REAL - 1:NT, :], 0.0).then_inc(s_xz, 1)
            nc.vector.memset(zero, 0.0).then_inc(s_z, 1)
            nc.vector.memset(k["bd"], 0.0)
            nc.vector.memset(k["ones"], 1.0)
            nc.vector.memset(k["eps"], EPS_LN)
            nc.vector.memset(k["epsm"], EPS_MOE)
            nc.vector.memset(k["epsz"], EPS_Z)
            link(nc.vector.memset(k["rowmask"], 1.0))
            nc.vector.memset(k["rowmask"][:, REAL:NT], 0.0)
            link(nc.vector.memset(k["bd"][0:HEAD, 0:HEAD], 1.0))
            link(nc.vector.memset(k["bd"][HEAD:P, HEAD:P], 1.0))
            dve.wait_ge(s_iota, 2)
            nc.vector.tensor_copy(k["iota"], iota_i[:, 0:P])
            nc.vector.tensor_copy(iota_t, iota_i)
            link(nc.vector.tensor_copy(k["pidx"], dT[:, 0, 0:1]))
            nc.vector.tensor_copy(iota_b, k["iota"])
            nc.vector.tensor_scalar(k["ident"], k["iota"], k["pidx"], None, ALU.is_equal)
            nc.vector.tensor_scalar(k["tri"], k["iota"], k["pidx"], None, ALU.is_gt)
            link(nc.vector.tensor_scalar(k["rowmask"][:, REAL - 1:REAL], k["pidx"], float(LAST), None, ALU.is_lt))
            dve.sem_inc(s_const, 1)
            dve.wait_ge(s_dst, 48)
            nc.vector.tensor_copy(flat(nat_d), flat(nat_i)).then_inc(s_natd, 1)
            dve.wait_ge(s_dTp, 1)
            for half in range(2):
                link.add(nc.vector.tensor_copy(dT[:, half, :], banks[5 + half][:, :]))
            link.wait()
            link(nc.vector.tensor_single_scalar(flat(dT2), flat(dT), P.bit_length() - 1, ALU.arith_shift_right))
            link(nc.vector.tensor_copy(flat(hi), flat(dT2)))
            link(nc.vector.tensor_single_scalar(flat(dT2), flat(dT), P - 1, ALU.bitwise_and))
            link(nc.vector.tensor_copy(flat(lo), flat(dT2)))
            for i in range(LOADS + 1):
                dve.wait_ge(s_x[i], 16 if i < LOADS else 32)
                for t in range(i * per_load, min((i + 1) * per_load, NT)):
                    last = nc.vector.bn_stats(k["stats"][:, t, :], X[:, t, :])
            link(last)
            ln_stats(nc, link, k, S)
            dve.sem_inc(s_var, 1)
            dve.wait_ge(s_sq, 1)
            ln_scales(nc, link, k, S)
            dve.sem_inc(s_ln, 1)
            with dve.Fori(0, NT // 2) as i:
                for u in range(2):
                    dve.wait_ge(s_hist, 2 * i + u + 1)
                    nc.vector.tensor_tensor(
                        onelo[u],
                        lo[:, u, bass.ds(i * HB, HB)].unsqueeze(2).to_broadcast([P, HB, P]),
                        iota_b.unsqueeze(1).to_broadcast([P, HB, P]),
                        ALU.is_equal)
                    nc.vector.tensor_tensor(
                        onehi[u],
                        hi[:, u, bass.ds(i * HB, HB)].unsqueeze(2).to_broadcast([P, HB, WINDOWS + 1]),
                        iota_b[:, 0:WINDOWS + 1].unsqueeze(1).to_broadcast([P, HB, WINDOWS + 1]),
                        ALU.is_equal).then_inc(s_lo, 1)
                for u in range(2):
                    dve.wait_ge(s_h, 2 * i + u + 3)
                    dve.wait_ge(s_xb, 2 * i + u + 1)
                    nc.vector.tensor_scalar(tile_of(X, 2 * i + u), psH[u][:, :], 1.0, None, ALU.mult).then_inc(s_hs, 1)
            dve.wait_ge(s_hist, 3 + NT)
            nc.vector.memset(S[:, 2, :], 1.0)
            link(nc.vector.tensor_copy(S[:, 3, :], psD[:, 0:NT]))
            link(nc.vector.tensor_scalar(S[:, 2, 0:WINDOWS], S[:, 3, 0:WINDOWS], 1.0, 1e-12, ALU.add, ALU.max))
            dve.sem_inc(s_deg, 1)
            dve.wait_ge(s_sdeg, 1)
            link(nc.vector.reciprocal(k["dinv"], k["sdeg"]))
            dve.sem_inc(s_dinv, 1)
            dve.wait_ge(s_hs, NT + 2)
            with dve.Fori(0, NT // 2) as i:
                t = tile_of(X, 2 * i)
                nc.vector.tensor_scalar(t, t, k["dinv"][:, bass.ds(2 * i, 1)], None, ALU.mult).then_inc(s_sc[0], 1)
            schedule_vector(nc, dve, link, k, S, nat_s, nat_d, nat_i, iota_t, onehot, over_w, spread, block_of, banks, s_src, s_pe, s_sch)

        @block.tensor
        def _(pe):
            pe.sem_inc(s_T, 2)
            pe.sem_inc(s_h, 2)
            pe.sem_inc(s_hs, 2)
            for u in range(2):
                pe.sem_inc(s_xTst[u], 16)
                pe.sem_inc(s_xbst[u], 16)
            pe.wait_ge(s_const, 1)
            pe.wait_ge(s_natd, 1)
            for half in range(2):
                for g in range(BG):
                    last = nc.tensor.transpose(banks[5 + half][:, g * P:(g + 1) * P], nat_d[:, g, half * P:(half + 1) * P], k["ident"])
            last.then_inc(s_dTp, 1)
            pe.wait_ge(s_z, 1)
            nc.tensor.matmul(psD[:, 0:WINDOWS + 1], zero[:, 0:P], zero[:, 0:WINDOWS + 1], start=True, stop=False).then_inc(s_hist, 2)
            pe.wait_ge(s_w, 32)
            with pe.Fori(0, NT // 2) as i:
                for u in range(2):
                    pe.wait_ge(s_xn, 2 * i + u + 1)
                    for c in range(C):
                        last = nc.tensor.transpose(psT[u][:, c * P:(c + 1) * P], xn[u][:, c * P:(c + 1) * P], k["ident"])
                    last.then_inc(s_T, 1)
                for u in range(2):
                    pe.wait_ge(s_lo, 2 * i + u + 1)
                    for j in range(HB):
                        last = nc.tensor.matmul(psD[:, 0:WINDOWS + 1], onelo[u][:, j, :], onehi[u][:, j, :], start=False, stop=False)
                    last.then_inc(s_hist, 1)
                    pe.wait_ge(s_xT, 2 * i + u + 1)
                    pe.wait_ge(s_hs, 2 * i + u + 1)
                    for c in range(C):
                        last = nc.tensor.matmul(psH[u][:, :], xT[u][:, c, :], W[:, c, :], start=c == 0, stop=c == C - 1)
                    last.then_inc(s_h, 1)
            nc.tensor.matmul(psD[:, 0:WINDOWS + 1], zero[:, 0:P], zero[:, 0:WINDOWS + 1], start=False, stop=True).then_inc(s_hist, 1)
            schedule_tensor(nc, pe, k, S, nat_i, nat_d, onehot, over_w, spread, banks, s_pe, s_sch)


def mix(nc, sem, d, k, X, keep, banks, wqkv, wout, gb):
    A = keep.take(2 * C, D)
    B = keep.take(C, D)
    G = keep.take(SLOTS, D)
    hot = keep.take(SLOTS, P)
    idx = keep.take(SLOTS, dt=I32)
    xT = keep.take(2, D)
    kvm = keep.at
    gbb = keep.take(D)
    ek, rk, kk, vv = (keep.take(D) for _ in range(4))
    zero = keep.take(P)
    keep.at = kvm
    eq = [keep.take(2, 2 * P) for _ in range(2)]
    rq = [keep.take(2, 2 * P) for _ in range(2)]
    sums = keep.take(P)
    xb = [B[:, u, :] for u in range(2)]
    xm = [B[:, 2 + u, :] for u in range(2)]
    Wk, Wv, M, Wq = A[:, 0:C, :], A[:, C:2 * C, :], A[:, 0:C, :], A[:, C:2 * C, :]
    kvT = keep.take(C, P)
    ksum = keep.take(C, P)
    agg_banks = 4
    s_wk, s_wv, s_wo, s_wq, s_gb = (sem(n) for n in ("wk_loaded", "wv_loaded", "wout_loaded", "wq_loaded", "b_loaded"))
    s_g = [sem(f"gathered{i}") for i in range(SLOTS)]
    s_idx, s_hot = sem("indices_ready"), sem("onehot_ready")
    s_agg, s_add, s_bg = sem("step_summed"), sem("step_added"), sem("bias_added")
    s_xT = [sem(f"xT_loaded{u}") for u in range(2)]
    s_K, s_kr, s_k, s_V, s_v, s_kv = (sem(n) for n in ("k_made", "k_read", "k_ready", "v_made", "v_ready", "kv_summed"))
    s_z, s_z1, s_rz = sem("zeros_ready"), sem("norm_read"), sem("norm_inverted")
    s_bd, s_Mp, s_M = sem("kv_blocks_ready"), sem("m_made"), sem("m_kept")
    s_xp, s_xb = sem("xT_pair_loaded"), [sem(f"xb_loaded{u}") for u in range(2)]
    s_Q, s_qr, s_q, s_D, s_qs, s_O, s_xm = (sem(n) for n in ("q_made", "q_read", "q_ready", "norm_made", "q_scaled", "attention_out", "xm_made"))
    s_xmst = [sem(f"xm_stored{u}") for u in range(2)]
    s_c, s_pc = sem("vector_chain"), sem("pool_ordered")
    HALF = STEPS // 2
    KV = NT // 2
    psA, psK, psV, psKV, psS = banks[0:4], banks[4], banks[5], banks[6], banks[7]
    psQ, psO = banks[4:6], banks[6:8]

    with nc.Block() as block:
        @block.sync
        def _(sp):
            w = wqkv.rearrange("(c p) n -> p c n", p=P)
            for u in range(2):
                sp.dma_start(xT[:, u, :], d["xnT"][u]).then_inc(s_xT[u], 16)
            sp.dma_start(Wk, w[:, :, D:2 * D]).then_inc(s_wk, 16)
            sp.dma_start(Wv, w[:, :, 2 * D:3 * D]).then_inc(s_wv, 16)
            sp.dma_start(gbb, gb.rearrange("(a n) -> a n", a=1).broadcast_to([P, D])).then_inc(s_gb, 16)
            sp.dma_start(B, wout.rearrange("(c p) n -> p c n", p=P)).then_inc(s_wo, 16)
            with sp.Fori(0, KV - 1) as i:
                for u in range(2):
                    sp.wait_ge(s_V, 2 * i + u + 1)
                    sp.dma_start(xT[:, u, :], d["xnT"][bass.ds(2 * i + 2 + u, 1), :, :].rearrange("a p n -> p (a n)")).then_inc(s_xT[u], 16)
            sp.wait_ge(s_V, NT)
            sp.dma_start(Wq, w[:, :, 0:D]).then_inc(s_wq, 16)
            sp.dma_start(xT, d["xnT"][0:2].rearrange("t p n -> p t n")).then_inc(s_xp, 16)
            sp.wait_ge(s_Mp, C)
            for u in range(2):
                sp.dma_start(xb[u], d["xb"][u * P:(u + 1) * P, :]).then_inc(s_xb[u], 16)
            with sp.Fori(0, KV - 1) as j:
                sp.wait_ge(s_Q, 2 * j + 2)
                sp.dma_start(xT, d["xnT"][bass.ds(2 * j + 2, 2)].rearrange("t p n -> p t n")).then_inc(s_xp, 16)
                for u in range(2):
                    sp.wait_ge(s_xm, 2 * j + u + 3)
                    sp.dma_start(d["xm"][bass.ds((2 * j + u) * P, P), :], xm[u]).then_inc(s_xmst[u], 16)
                    sp.dma_start(xb[u], d["xb"][bass.ds((2 * j + 2 + u) * P, P), :]).then_inc(s_xb[u], 16)
            for u in range(2):
                sp.wait_ge(s_xm, 2 * KV + 1 + u)
                sp.dma_start(d["xm"][(NT - 2 + u) * P:(NT - 1 + u) * P, :], xm[u]).then_inc(s_xmst[u], 16)
            for u in range(2):
                sp.wait_ge(s_xmst[u], 16 * KV + 16)

        @block.gpsimd
        def _(pool):
            with pool.Fori(0, TURNS) as i:
                for slot in range(SLOTS):
                    if slot % STEPS == 0:
                        pool.wait_ge(s_idx, 2 * i + slot // STEPS + 1)
                    pool.wait_ge(s_agg, STEPS * i + slot // 2 + 1)
                    pool.sem_inc(s_pc, 1)
                    pool.indirect_dma_start(G[:, slot, :], None, d["h"],
                                            bass.IndirectOffsetOnAxis(ap=idx[:, slot:slot + 1], axis=0)).then_inc(s_g[slot], 16)

        @block.scalar
        def _(act):
            with act.Fori(0, KV) as i:
                for u in range(2):
                    t = 2 * i + u
                    act.wait_ge(s_K, t + 1)
                    act.wait_ge(s_k, t + 1)
                    nc.scalar.activation(ek, psK[:, :], ACT.Exp)
                    nc.scalar.activation(rk, psK[:, :], ACT.Relu).then_inc(s_kr, 1)
                    act.wait_ge(s_V, t + 1)
                    act.wait_ge(s_kv, t + 1)
                    nc.scalar.copy(vv, psV[:, :]).then_inc(s_v, 1)
            for c in range(C):
                act.wait_ge(s_Mp, c + 1)
                nc.scalar.copy(M[:, c, :], psQ[c % 2][:, :]).then_inc(s_M, 1)
            with act.Fori(0, KV) as j:
                for b in range(2):
                    act.wait_ge(s_Q, 2 * j + b + 1)
                    act.wait_ge(s_O, 2 * j + 2)
                    nc.scalar.activation(flat(eq[b]), psQ[b][:, :], ACT.Exp)
                    nc.scalar.activation(flat(rq[b]), psQ[b][:, :], ACT.Relu).then_inc(s_qr, 1)
                for b in range(2):
                    act.wait_ge(s_D, 2 * j + b + 1)
                    nc.scalar.activation(flat(rq[b]), psQ[b][:, :], ACT.Identity, bias=k["epsz"]).then_inc(s_z1, 1)

        @block.vector
        def _(dve):
            link = Chain(dve, s_c)

            def refresh(half, turn):
                cols = bass.ds(turn * SLOTS + half * STEPS, STEPS)
                nc.vector.tensor_scalar(idx[:, half * STEPS:(half + 1) * STEPS], k["edge_src"][:, cols], 0.0, None, ALU.add).then_inc(s_idx, 1)
                nc.vector.tensor_tensor(
                    hot[:, half * STEPS:(half + 1) * STEPS, :],
                    k["edge_dst"][:, cols].unsqueeze(2).to_broadcast([P, STEPS, P]),
                    k["iota"].unsqueeze(1).to_broadcast([P, STEPS, P]),
                    ALU.is_equal).then_inc(s_hot, 1)

            def step(i, s):
                w = dve.value_load(k["win"][0:1, bass.ds(STEPS * i + s, 1)], min_val=0, max_val=WINDOWS - 1)
                dve.wait_ge(s_agg, STEPS * (i + 1) + s + 1)
                dve.wait_ge(s_add, STEPS * i + s + agg_banks)
                nc.vector.tensor_tensor(tile_of(X, w), tile_of(X, w), psA[s % agg_banks][:, :], ALU.add).then_inc(s_add, 1)

            nc.vector.memset(zero, 0.0).then_inc(s_z, 1)
            for half in range(2):
                refresh(half, 0)
            dve.sem_inc(s_k, 1)
            dve.wait_ge(s_gb, 16)
            with dve.Fori(0, KV) as i:
                for u in range(2):
                    t = 2 * i + u
                    dve.wait_ge(s_kr, t + 2)
                    dve.wait_ge(s_kv, t + 1)
                    nc.vector.scalar_tensor_tensor(kk, ek, 1.0, rk, ALU.min, ALU.add).then_inc(s_k, 1)
                    for s in range(HALF * u, HALF * u + HALF):
                        step(i, s)
                        if s == HALF * u:
                            dve.wait_ge(s_add, STEPS * i + s + agg_banks + 1)
                            nc.vector.scalar_tensor_tensor(tile_of(X, t), gbb, k["sdeg"][:, bass.ds(t, 1)], tile_of(X, t), ALU.mult, ALU.add).then_inc(s_bg, 1)
                            dve.wait_ge(s_bg, t + 1)
                    refresh(u, i + 1)
            dve.wait_ge(s_kv, NT + 2)
            nc.vector.tensor_tensor(kvT, psKV[:, :].rearrange("p (c n) -> p c n", n=P), k["bd"].unsqueeze(1).to_broadcast([P, C, P]), ALU.mult)
            link(nc.vector.tensor_copy(sums[:, 0:C], psS[:, 0:C]))
            for c in range(C):
                last = nc.vector.tensor_scalar(ksum[:, c, :], k["bd"], sums[:, c:c + 1], None, ALU.mult)
            last.then_inc(s_bd, 1)
            with dve.Fori(KV, 2 * KV) as i:
                def scaled(b):
                    dve.wait_ge(s_z1, 2 * i + b + 3 - 2 * KV)
                    nc.vector.reciprocal(flat(rq[b]), flat(rq[b])).then_inc(s_rz, 1)
                    dve.wait_ge(s_rz, 2 * i + b + 1 - 2 * KV)
                    nc.vector.tensor_tensor(flat(eq[b]), flat(eq[b]), flat(rq[b]), ALU.mult).then_inc(s_qs, 1)

                def out(u):
                    dve.wait_ge(s_O, 2 * i + u + 3 - 2 * KV)
                    dve.wait_ge(s_xb[u], 16 * i + 16 - 16 * KV)
                    dve.wait_ge(s_xmst[u], 16 * i + 16 - 16 * KV)
                    nc.vector.tensor_tensor(xm[u], psO[u][:, :], xb[u], ALU.add).then_inc(s_xm, 1)

                for b in range(2):
                    dve.wait_ge(s_qr, 2 * i + b + 1 - 2 * KV)
                    nc.vector.scalar_tensor_tensor(flat(eq[b]), flat(eq[b]), 1.0, flat(rq[b]), ALU.min, ALU.add).then_inc(s_q, 1)
                for s in range(STEPS):
                    step(i, s)
                    if s == 2:
                        dve.wait_ge(s_q, 2 * i + 2 - 2 * KV)
                        scaled(0)
                        scaled(1)
                    if s == 3:
                        refresh(0, i + 1)
                    if s == 4:
                        out(0)
                    if s == 5:
                        out(1)
                refresh(1, i + 1)
            with dve.Fori(2 * KV, TURNS) as i:
                for s in range(STEPS):
                    step(i, s)
                    if s == 3:
                        refresh(0, i + 1)
                refresh(1, i + 1)
            dve.wait_ge(s_add, T + agg_banks)

        @block.tensor
        def _(pe):
            def step(i, s):
                if s % HALF == 0:
                    pe.wait_ge(s_hot, 2 * i + s // HALF + 1)
                pe.wait_ge(s_add, STEPS * i + s + 1)
                for half in range(2):
                    slot = 2 * s + half
                    pe.wait_ge(s_g[slot], 16 * i + 16)
                    last = nc.tensor.matmul(psA[s % agg_banks][:, :], hot[:, slot, :], G[:, slot, :], start=half == 0, stop=half == 1)
                last.then_inc(s_agg, 1)

            pe.sem_inc(s_agg, STEPS)
            pe.sem_inc(s_add, agg_banks)
            pe.sem_inc(s_kr, 1)
            pe.sem_inc(s_v, 1)
            for u in range(2):
                pe.sem_inc(s_xmst[u], 16)
            pe.wait_ge(s_z, 1)
            for c in range(C):
                nc.tensor.matmul(psKV[:, c * P:(c + 1) * P], zero, zero, start=c == 0, stop=False)
            nc.tensor.matmul(psS[:, 0:C], zero, zero[:, 0:C], start=True, stop=False).then_inc(s_kv, 1)
            pe.wait_ge(s_wk, 16)
            pe.wait_ge(s_wv, 16)
            with pe.Fori(0, KV) as i:
                for u in range(2):
                    t = 2 * i + u
                    pe.wait_ge(s_xT[u], 16 * i + 16)
                    pe.wait_ge(s_kr, t + 1)
                    for c in range(C):
                        last = nc.tensor.matmul(psK[:, :], xT[:, u, c * P:(c + 1) * P], Wk[:, c, :], start=c == 0, stop=c == C - 1)
                    last.then_inc(s_K, 1)
                    pe.wait_ge(s_v, t + 1)
                    for c in range(C):
                        last = nc.tensor.matmul(psV[:, :], xT[:, u, c * P:(c + 1) * P], Wv[:, c, :], start=c == 0, stop=c == C - 1)
                    last.then_inc(s_V, 1)
                    for s in range(HALF * u, HALF * u + HALF):
                        step(i, s)
                    pe.wait_ge(s_k, t + 2)
                    pe.wait_ge(s_v, t + 2)
                    for c in range(C):
                        nc.tensor.matmul(psKV[:, c * P:(c + 1) * P], vv[:, c * P:(c + 1) * P], kk[:, c * P:(c + 1) * P], start=False, stop=False)
                    for c in range(C):
                        last = nc.tensor.matmul(psS[:, c:c + 1], kk[:, c * P:(c + 1) * P], k["rowmask"][:, bass.ds(t, 1)], start=False, stop=False)
                    last.then_inc(s_kv, 1)
            for c in range(C):
                nc.tensor.matmul(psKV[:, c * P:(c + 1) * P], zero, zero, start=False, stop=c == C - 1)
            nc.tensor.matmul(psS[:, 0:C], zero, zero[:, 0:C], start=False, stop=True).then_inc(s_kv, 1)
            pe.wait_ge(s_bd, 1)
            pe.wait_ge(s_wo, 16)
            pe.wait_ge(s_kr, NT + 1)
            pe.wait_ge(s_v, NT + 1)
            for c in range(C):
                if c >= 2:
                    pe.wait_ge(s_M, c - 1)
                nc.tensor.matmul(psQ[c % 2][:, :], kvT[:, c, :], B[:, c, :], start=True, stop=True).then_inc(s_Mp, 1)
            pe.sem_inc(s_O, 2)
            pe.sem_inc(s_xm, 2)
            pe.sem_inc(s_z1, 2)
            pe.wait_ge(s_M, C)
            pe.wait_ge(s_wq, 16)
            with pe.Fori(KV, 2 * KV) as i:
                pe.wait_ge(s_xp, 16 * i + 16 - 16 * KV)
                pe.wait_ge(s_z1, 2 * i + 2 - 2 * KV)
                for b in range(2):
                    for half in range(2):
                        c = 2 * b + half
                        for kc in range(C):
                            last = nc.tensor.matmul(psQ[b][:, half * 2 * P:(half + 1) * 2 * P], Wq[:, kc, c * P:(c + 1) * P],
                                                    xT.rearrange("p t (c r) -> p t c r", r=P)[:, :, kc, :], start=kc == 0, stop=kc == C - 1)
                    last.then_inc(s_Q, 1)
                for s in range(3):
                    step(i, s)
                for b in range(2):
                    pe.wait_ge(s_q, 2 * i + b + 1 - 2 * KV)
                    for half in range(2):
                        last = nc.tensor.matmul(psQ[b][:, half * 2 * P:(half + 1) * 2 * P], ksum[:, 2 * b + half, :], eq[b][:, half, :], start=True, stop=True)
                    last.then_inc(s_D, 1)
                for s in range(3, 5):
                    step(i, s)
                pe.wait_ge(s_qs, 2 * i + 2 - 2 * KV)
                for u in range(2):
                    if u == 1:
                        step(i, 5)
                    pe.wait_ge(s_xm, 2 * i + u + 1 - 2 * KV)
                    for c in range(C):
                        last = nc.tensor.matmul(psO[u][:, :], eq[c // 2][:, c % 2, u * P:(u + 1) * P], M[:, c, :], start=c == 0, stop=c == C - 1)
                    last.then_inc(s_O, 1)
                for s in range(6, 8):
                    step(i, s)
            with pe.Fori(2 * KV, TURNS) as i:
                for s in range(STEPS):
                    step(i, s)


def ln_stats(nc, link, k, S):
    st = k["stats"].rearrange("p t c -> p c t")
    link.add(nc.vector.tensor_tensor(S[:, 2, :], st[:, 1, :], st[:, 4, :], ALU.add))
    link.add(nc.vector.tensor_tensor(S[:, 3, :], st[:, 1, :], st[:, 4, :], ALU.subtract))
    link(nc.vector.tensor_tensor(S[:, 4, :], st[:, 2, :], st[:, 5, :], ALU.add))
    link.add(nc.vector.tensor_scalar(S[:, 2, :], S[:, 2, :], 0.5, None, ALU.mult))
    link(nc.vector.scalar_tensor_tensor(S[:, 3, :], S[:, 3, :], 0.25, S[:, 3, :], ALU.mult, ALU.mult))
    link(nc.vector.scalar_tensor_tensor(S[:, 1, :], S[:, 4, :], 1.0 / D, S[:, 3, :], ALU.mult, ALU.add))


def ln_scales(nc, link, k, S):
    link(nc.vector.reciprocal(k["rstd"], S[:, 0, :]))
    link(nc.vector.scalar_tensor_tensor(k["nmr"], S[:, 2, :], -1.0, k["rstd"], ALU.mult, ALU.mult))


def schedule_vector(nc, dve, link, k, S, nat_s, nat_d, nat_i, iota_t, onehot, over_w, spread, block_of, banks, s_src, s_pe, s_sch):
    W = WINDOWS + 1
    col = [S[0:W, 4, i:i + 1] for i in range(12)]
    cnt, start, end, first, last_, nb, t0, t1, bm, some = col[:10]
    ints = S[0:W, 5, 0:4].bitcast(I32)
    ps = banks[5]
    dve.wait_ge(s_src, 48)
    nc.vector.memset(k["edge_src"], 0.0)
    nc.vector.memset(k["edge_dst"], -1.0)
    nc.vector.memset(k["win"], 0)
    nc.vector.tensor_copy(nat_i.bitcast(FP32), nat_s.bitcast(I32)).then_inc(s_sch, 1)
    dve.wait_ge(s_pe, 1)
    link(nc.vector.tensor_copy(cnt, ps[0:W, 0:1]))
    dve.sem_inc(s_sch, 1)
    dve.wait_ge(s_pe, 2)
    link(nc.vector.tensor_copy(start, ps[0:W, 1:2]))
    link(nc.vector.tensor_tensor(end, start, cnt, ALU.add))
    link.add(nc.vector.tensor_copy(ints[:, 0:1], start))
    link(nc.vector.tensor_scalar(ints[:, 1:2], end, -1.0, None, ALU.add))
    link(nc.vector.tensor_single_scalar(ints[:, 2:4], ints[:, 0:2], PAIR.bit_length() - 1, ALU.arith_shift_right))
    link.add(nc.vector.tensor_copy(first, ints[:, 2:3]))
    link.add(nc.vector.tensor_copy(last_, ints[:, 3:4]))
    link(nc.vector.tensor_scalar(some, cnt, 0.0, None, ALU.is_gt))
    link(nc.vector.tensor_scalar(nb, last_, first, 1.0, ALU.subtract, ALU.add))
    link(nc.vector.tensor_tensor(nb, nb, some, ALU.mult))
    dve.sem_inc(s_sch, 1)
    dve.wait_ge(s_pe, 3)
    link(nc.vector.tensor_copy(t0, ps[0:W, 2:3]))
    link.add(nc.vector.tensor_tensor(t1, t0, nb, ALU.add))
    link(nc.vector.tensor_tensor(bm, first, t0, ALU.subtract))
    link.add(nc.vector.tensor_scalar(over_w[0:W, :], iota_t[0:W, :], t0, None, ALU.is_ge))
    link.add(nc.vector.tensor_scalar(spread[0:W, 0, :], k["ones"][0:W, :], bm, None, ALU.mult))
    link(nc.vector.tensor_scalar(spread[0:W, 1, :], k["ones"][0:W, :], k["pidx"][0:W, :], None, ALU.mult))
    link(nc.vector.scalar_tensor_tensor(over_w[0:W, :], iota_t[0:W, :], t1, over_w[0:W, :], ALU.is_lt, ALU.mult))
    dve.sem_inc(s_sch, 1)
    dve.wait_ge(s_pe, 4)
    link.add(nc.vector.tensor_tensor(block_of, ps[:, 0:T], iota_t, ALU.add))
    link.add(nc.vector.tensor_copy(k["win"][:, 0:T], banks[6][:, 0:T]))
    link(nc.vector.tensor_scalar(over_w, banks[6][:, 0:T], float(P), None, ALU.mult))
    for g in range(BG):
        last = nc.vector.tensor_scalar(onehot[:, g, :], block_of, float(-P * g), k["pidx"], ALU.add, ALU.is_equal)
    last.then_inc(s_sch, 1)
    for half in range(2):
        to = k["edge_src"].rearrange("p (t h) -> p h t", h=2)[:, half, 0:T]
        dve.wait_ge(s_pe, 5 + half)
        nc.vector.tensor_copy(to, banks[5 + half][:, 0:T])
    for half in range(2):
        to = k["edge_dst"].rearrange("p (t h) -> p h t", h=2)[:, half, 0:T]
        dve.wait_ge(s_pe, 7 + half)
        nc.vector.tensor_tensor(to, banks[2 + half][:, 0:T], over_w, ALU.subtract)


def schedule_tensor(nc, pe, k, S, nat_i, nat_d, onehot, over_w, spread, banks, s_pe, s_sch):
    W = WINDOWS + 1
    nat_f = nat_i.bitcast(FP32)
    ps = banks[5]
    pe.wait_ge(s_sch, 1)
    nc.tensor.matmul(ps[0:W, 0:1], S[:, 3, 0:W], k["ones"][:, 0:1], start=True, stop=True).then_inc(s_pe, 1)
    pe.wait_ge(s_sch, 2)
    nc.tensor.matmul(ps[0:W, 1:2], k["tri"][0:W, 0:W], S[0:W, 4, 0:1], start=True, stop=True).then_inc(s_pe, 1)
    pe.wait_ge(s_sch, 3)
    nc.tensor.matmul(ps[0:W, 2:3], k["tri"][0:W, 0:W], S[0:W, 4, 5:6], start=True, stop=True).then_inc(s_pe, 1)
    pe.wait_ge(s_sch, 4)
    nc.tensor.matmul(ps[:, 0:T], spread[0:W, 0, :], over_w[0:W, :], start=True, stop=True)
    nc.tensor.matmul(banks[6][:, 0:T], spread[0:W, 1, :], over_w[0:W, :], start=True, stop=True).then_inc(s_pe, 1)
    pe.wait_ge(s_sch, 5)
    for table, first in ((nat_f, 5), (nat_d, 2)):
        for half in range(2):
            for g in range(BG):
                last = nc.tensor.matmul(banks[first + half][:, 0:T], table[:, g, half * P:(half + 1) * P], onehot[:, g, :], start=g == 0, stop=g == BG - 1)
            last.then_inc(s_pe, 1)


def route(nc, sem, d, k, X, keep, banks, rw):
    V = 5
    g = [keep.take(D) for _ in range(V)]
    xm = [keep.take(D) for _ in range(V)]
    x2 = [keep.take(D) for _ in range(2)]
    xT = [keep.take(C, P) for _ in range(2)]
    lg = [keep.take(NX) for _ in range(2)]
    v8 = [keep.take(NX) for _ in range(2)]
    ix = [keep.take(NX, dt=U32) for _ in range(2)]
    ixf = [keep.take(NX) for _ in range(2)]
    S = k["small"]
    psT, psL = banks[0:2], banks[2:4]
    s_w = sem("router_loaded")
    s_xm = [sem(f"xm_loaded{v}") for v in range(V)]
    s_g, s_x1, s_st, s_x1st = sem("gcn_ready"), sem("x1_made"), sem("stats_made"), sem("x1_stored")
    s_var, s_sq, s_ln = sem("variances"), sem("std_done"), sem("ln_ready")
    s_x2, s_T, s_xT, s_L, s_lg = (sem(n) for n in ("x2_made", "x2_transposed", "xT_copied", "logits_made", "logits_kept"))
    s_norm, s_gate, s_e = sem("x_normed"), sem("gate_gaps"), sem("gate_exps")
    s_c, s_ac, s_vc, s_vo = sem("vector_chain"), sem("act_ordered"), sem("choice_chain"), sem("vector_ordered")

    with nc.Block() as block:
        @block.sync
        def _(sp):
            for v in range(V):
                sp.dma_start(xm[v], d["xm"][v * P:(v + 1) * P, :]).then_inc(s_xm[v], 16)
            sp.dma_start(k["wr"], rw.rearrange("(c p) e -> p c e", p=P)).then_inc(s_w, 16)

            def store(t):
                sp.dma_start(d["x1"][bass.ds(t * P, P), :], tile_of(X, t)).then_inc(s_x1st, 16)

            with sp.Fori(0, NT // V - 1) as i:
                for v in range(V):
                    sp.wait_ge(s_x1, V * i + v + 1)
                    store(V * i + v)
                    sp.dma_start(xm[v], d["xm"][bass.ds((V * i + V + v) * P, P), :]).then_inc(s_xm[v], 16)
            for v in range(V):
                sp.wait_ge(s_x1, NT - V + v + 1)
                store(NT - V + v)
            sp.wait_ge(s_x1st, 16 * NT)

        @block.scalar
        def _(act):
            with act.Fori(0, NT // V) as i:
                for v in range(V):
                    t = V * i + v
                    act.wait_ge(s_st, t + 1)
                    act.sem_inc(s_ac, 1)
                    nc.scalar.activation(g[v], tile_of(X, t), ACT.Relu, scale=k["dinv"][:, bass.ds(t, 1)]).then_inc(s_g, 1)
            act.wait_ge(s_var, 1)
            nc.scalar.activation(S[:, 0, :], S[:, 1, :], ACT.Sqrt, bias=k["eps"]).then_inc(s_sq, 1)
            act.wait_ge(s_ln, 1)
            with act.Fori(0, NT // 2) as i:
                for u in range(2):
                    t = 2 * i + u
                    act.wait_ge(s_T, t + 1)
                    act.sem_inc(s_ac, 1)
                    nc.scalar.activation(x2[u], tile_of(X, t), ACT.Identity, bias=k["nmr"][:, bass.ds(t, 1)], scale=k["rstd"][:, bass.ds(t, 1)]).then_inc(s_x2, 1)
                for u in range(2):
                    t = 2 * i + u
                    act.wait_ge(s_T, t + 3)
                    act.wait_ge(s_L, t + 1)
                    nc.scalar.copy(flat(xT[u]), psT[u][:, :]).then_inc(s_xT, 1)
            act.wait_ge(s_gate, 1)
            nc.scalar.activation(k["gate"][:, 1, :], k["gate"][:, 0, :], ACT.Exp).then_inc(s_e, 1)

        @block.vector
        def _(dve):
            link = Chain(dve, s_c)
            dve.sem_inc(s_st, V)
            with dve.Fori(0, NT // V) as i:
                for v in range(V):
                    t = V * i + v
                    dve.wait_ge(s_g, t + 1)
                    dve.wait_ge(s_xm[v], 16 * i + 16)
                    nc.vector.tensor_tensor(tile_of(X, t), g[v], xm[v], ALU.add).then_inc(s_x1, 1)
                    dve.wait_ge(s_x1, t + 1)
                    dve.sem_inc(s_vo, 1)
                    nc.vector.bn_stats(k["stats"][:, bass.ds(t, 1), :].rearrange("p a s -> p (a s)"), tile_of(X, t)).then_inc(s_st, 1)
            dve.wait_ge(s_st, NT + V)
            ln_stats(nc, link, k, S)
            dve.sem_inc(s_var, 1)
            dve.wait_ge(s_sq, 1)
            ln_scales(nc, link, k, S)
            dve.sem_inc(s_ln, 1)
            dve.wait_ge(s_x1st, 16 * NT)
            per = 7
            with dve.Fori(0, NT // 2) as i:
                for u in range(2):
                    t = 2 * i + u
                    dve.wait_ge(s_x2, t + 1)
                    nc.vector.tensor_scalar(tile_of(X, t), tile_of(X, t), k["rstd"][:, bass.ds(t, 1)], k["nmr"][:, bass.ds(t, 1)], ALU.mult, ALU.add).then_inc(s_norm, 1)
                chain = [0]

                def then(ins):
                    ins.then_inc(s_vc, 1)
                    chain[0] += 1

                def settle():
                    dve.wait_ge(s_vc, 2 * per * i + chain[0])

                for u in range(2):
                    dve.wait_ge(s_L, 2 * i + u + 3)
                    then(nc.vector.tensor_copy(lg[u], psL[u][:, 0:NX]))
                settle()
                for u in range(2):
                    dve.sem_inc(s_lg, 1)
                    then(nc.vector.max(v8[u], lg[u]))
                settle()
                for u in range(2):
                    dve.sem_inc(s_vo, 1)
                    then(nc.vector.max_index(ix[u], v8[u], lg[u]))
                settle()
                for u in range(2):
                    then(nc.vector.tensor_copy(ixf[u], ix[u]))
                settle()
                for u in range(2):
                    t = 2 * i + u
                    for m, M in enumerate((k["M1"], k["M2"])):
                        then(nc.vector.tensor_scalar(M[:, bass.ds(t, 1), :].rearrange("p a e -> p (a e)"), k["iota"][:, 0:NX], ixf[u][:, m:m + 1],
                                                     k["rowmask"][:, bass.ds(t, 1)], ALU.is_equal, ALU.mult))
                    then(nc.vector.tensor_copy(k["v12"][:, bass.ds(t, 1), :].rearrange("p a e -> p (a e)"), v8[u][:, 0:2]))
                settle()
            link(nc.vector.tensor_tensor(k["gate"][:, 0, :], k["v12"][:, :, 1], k["v12"][:, :, 0], ALU.subtract))
            dve.sem_inc(s_gate, 1)
            dve.wait_ge(s_e, 1)
            link(nc.vector.tensor_scalar(S[:, 3, :], k["gate"][:, 1, :], 1.0, None, ALU.add))
            link(nc.vector.reciprocal(k["gate"][:, 0, :], S[:, 3, :]))
            link(nc.vector.tensor_tensor(k["gate"][:, 1, :], k["gate"][:, 1, :], k["gate"][:, 0, :], ALU.mult))
            dve.wait_ge(s_norm, NT)

        @block.tensor
        def _(pe):
            pe.sem_inc(s_T, 2)
            pe.sem_inc(s_L, 2)
            pe.sem_inc(s_lg, 2)
            pe.wait_ge(s_w, 16)
            with pe.Fori(0, NT // 2) as i:
                for u in range(2):
                    pe.wait_ge(s_x2, 2 * i + u + 1)
                    for c in range(C):
                        last = nc.tensor.transpose(psT[u][:, c * P:(c + 1) * P], x2[u][:, c * P:(c + 1) * P], k["ident"])
                    last.then_inc(s_T, 1)
                for u in range(2):
                    pe.wait_ge(s_xT, 2 * i + u + 1)
                    pe.wait_ge(s_lg, 2 * i + u + 1)
                    for c in range(C):
                        last = nc.tensor.matmul(psL[u][:, 0:NX], xT[u][:, c, :], k["wr"][:, c, :], start=c == 0, stop=c == C - 1)
                    last.then_inc(s_L, 1)


def dispatch(nc, sem, d, k, X, keep, banks):
    both = keep.take(NT, NX)
    incl = keep.take(NT, NX)
    pos = keep.take(NT, NX)
    pick = keep.take(2, NT, NX)
    slot = keep.take(2, NT)
    zeros = keep.take(NT)
    cnt, nb, binc, bexc, base = (keep.take(NX) for _ in range(5))
    ni = keep.take(2, NX, dt=I32)
    iota_i = keep.take(P, dt=I32)
    ex = keep.take(MB)
    s_c, s_both, s_ps, s_pos, s_out = sem("vector_chain"), sem("choices_ready"), sem("ranks_made"), sem("slots_ready"), sem("rows_sent")

    with nc.Block() as block:
        @block.vector
        def _(dve):
            link = Chain(dve, s_c)
            nc.vector.memset(zeros, 0.0)
            link(nc.vector.tensor_tensor(flat(both), flat(k["M1"]), flat(k["M2"]), ALU.add))
            dve.sem_inc(s_both, 1)
            dve.wait_ge(s_ps, 1)
            rank = banks[0][:, 0:NT * NX].rearrange("p (t e) -> p t e", e=NX)
            total = banks[1][:, 0:NT * NX].rearrange("p (t e) -> p t e", e=NX)
            for e in range(NX):
                link.add(nc.vector.tensor_tensor_scan(incl[:, :, e], total[:, :, e], zeros, 0.0, ALU.add, ALU.add))
            link.wait()
            link.add(nc.vector.tensor_tensor(pos, incl, rank, ALU.add))
            link(nc.vector.tensor_scalar(ni[:, 0, :], incl[:, NT - 1, :], float(P - 1), None, ALU.add))
            link.add(nc.vector.tensor_tensor(pos, pos, total, ALU.subtract))
            link(nc.vector.tensor_single_scalar(ni[:, 1, :], ni[:, 0, :], P.bit_length() - 1, ALU.arith_shift_right))
            link(nc.vector.tensor_copy(nb, ni[:, 1, :]))
            link(nc.vector.tensor_tensor_scan(binc, nb, zeros[:, 0:NX], 0.0, ALU.add, ALU.add))
            link(nc.vector.tensor_tensor(bexc, binc, nb, ALU.subtract))
            link(nc.vector.tensor_scalar(base, bexc, float(P), None, ALU.mult))
            link(nc.vector.tensor_tensor(pos, pos, base.unsqueeze(1).to_broadcast([P, NT, NX]), ALU.add))
            for m, M in enumerate((k["M1"], k["M2"])):
                link(nc.vector.tensor_tensor(pick[:, m], M, pos, ALU.mult))
                link(nc.vector.tensor_reduce(slot[:, m, :], pick[:, m], mybir.AxisListType.X, ALU.add))
            link(nc.vector.tensor_copy(flat(k["pos"]), flat(slot)))
            dve.sem_inc(s_pos, 1)
            link(nc.vector.tensor_scalar(ex, k["iota"][:, 0:MB], bexc[:, 1:2], None, ALU.is_ge))
            for e in range(2, NX):
                link(nc.vector.scalar_tensor_tensor(ex, k["iota"][:, 0:MB], bexc[:, e:e + 1], ex, ALU.is_ge, ALU.add))
            link(nc.vector.tensor_copy(k["expert"], ex))

        @block.tensor
        def _(pe):
            pe.wait_ge(s_both, 1)
            nc.tensor.matmul(banks[0][:, 0:NT * NX], k["tri"], flat(both), start=True, stop=True)
            nc.tensor.matmul(banks[1][:, 0:NT * NX], k["ones"], flat(both), start=True, stop=True).then_inc(s_ps, 1)

        @block.gpsimd
        def _(pool):
            pool.wait_ge(s_pos, 1)
            for t in range(REAL):
                rows = P if t < REAL - 1 else LAST
                for m in range(2):
                    pool.indirect_dma_start(d["xs"], bass.IndirectOffsetOnAxis(ap=k["pos"][0:rows, m, t:t + 1], axis=0), X[0:rows, t, :], None).then_inc(s_out, 16)
            pool.wait_ge(s_out, 32 * REAL)


def experts(nc, sem, d, k, X, keep, banks, w1, b1, w2, b2, gamma, beta):
    W1 = keep.take(NX * C, F)
    W2 = keep.take(NX * FC, D)
    m = Mem(X.rearrange("p t n -> p (t n)"), NT * D)
    b1b, b2b, gab, beb = m.take(NX, F), m.take(NX, D), m.take(NX, D), m.take(NX, D)
    xs = [m.take(D) for _ in range(4)]
    xb = [m.take(D) for _ in range(4)]
    xsT, hb, hT, r, n, g, y = ([m.take(w) for _ in range(2)] for w in (D, F, F, D, D, D, D))
    st, mv, sd, rs, nm = ([m.take(w) for _ in range(2)] for w in (6, 2, 1, 1, 1))
    psX, psH, psG, psY = banks[0:2], banks[2:4], banks[4:6], banks[6:8]
    s_w1, s_w2, s_bb = sem("w1_loaded"), sem("w2_loaded"), sem("biases_loaded")
    s_xs = [sem(f"rows_loaded{u}") for u in range(4)]
    s_yst = [sem(f"y_stored{u}") for u in range(2)]
    s_T, s_xT, s_H, s_hb, s_G, s_hT, s_Y = (sem(n) for n in ("x_transposed", "xT_copied", "h_made", "h_biased", "h_transposed", "hT_copied", "y_made"))
    s_xb, s_r, s_v, s_sd, s_y, s_pc = (sem(n) for n in ("x_biased", "r_made", "var_made", "std_made", "y_ready", "pool_ordered"))
    s_st, s_rs, s_nm, s_n, s_g, s_vo = (sem(n) for n in ("stats_made", "rstd_made", "mean_scaled", "normed", "gamma_applied", "vector_ordered"))

    def pipeline(eng, turn, ahead, behind):
        lo, hi = 4 * -(-behind // 4), (MB - ahead) // 4 * 4
        for b in range(-ahead, lo):
            turn(b, b // 4, b % 4)
        with eng.Fori(lo // 4, hi // 4) as i:
            for u in range(4):
                turn(4 * i + u, i, u, middle=True)
        for b in range(hi, MB + behind):
            turn(b, b // 4, b % 4)

    def inside(b, middle):
        return middle or 0 <= b < MB

    with nc.Block() as block:
        @block.sync
        def _(sp):
            sp.dma_start(flat(b1b), b1.rearrange("(o e) n -> o (e n)", o=1).broadcast_to([P, NX * F])).then_inc(s_bb, 16)
            for to, a in ((b2b, b2), (gab, gamma), (beb, beta)):
                sp.dma_start(flat(to), a.rearrange("(o e) n -> o (e n)", o=1).broadcast_to([P, NX * D])).then_inc(s_bb, 16)
            sp.dma_start(W1, w1.rearrange("e (c p) f -> p (e c) f", p=P)).then_inc(s_w1, 16)
            sp.dma_start(W2, w2.rearrange("e (c p) n -> p (e c) n", p=P)).then_inc(s_w2, 16)

            def turn(b, i, u, middle=False):
                if inside(b + 4, middle):
                    rows = d["xs"][bass.ds((b + 4) * P, P), :]
                    if middle or b >= 0:
                        sp.wait_ge(s_T, b + 3)
                        sp.wait_ge(s_xb, b + 3)
                    sp.dma_start(xs[u], rows).then_inc(s_xs[u], 16)
                if inside(b - 3, middle):
                    rows = d["ys"][bass.ds((b - 3) * P, P), :]
                    sp.wait_ge(s_y, b - 2)
                    sp.dma_start(rows, y[(u + 1) % 2]).then_inc(s_yst[(u + 1) % 2], 16)

            pipeline(sp, turn, 4, 3)
            for v in range(2):
                sp.wait_ge(s_yst[v], 16 * (MB // 2) + 16)

        @block.gpsimd
        def _(pool):
            def turn(b, i, u, middle=False):
                v = u % 2
                if inside(b + 1, middle):
                    e = pool.value_load(k["expert"][0:1, bass.ds(b + 1, 1)], min_val=0, max_val=NX - 1)
                    w = (u + 1) % 4
                    pool.wait_ge(s_xs[w], 16 * (i + (u + 1) // 4) + 16)
                    if middle or b > 2:
                        pool.wait_ge(s_r, b - 2)
                    pool.sem_inc(s_pc, 1)
                    nc.gpsimd.tensor_tensor(xb[w], xs[w], tile_of(b2b, e), ALU.add).then_inc(s_xb, 1)
                if inside(b - 2, middle):
                    e = pool.value_load(k["expert"][0:1, bass.ds(b - 2, 1)], min_val=0, max_val=NX - 1)
                    pool.wait_ge(s_n, b + 1)
                    pool.sem_inc(s_pc, 1)
                    nc.gpsimd.tensor_tensor(g[v], n[v], tile_of(gab, e), ALU.mult).then_inc(s_g, 1)
                    pool.wait_ge(s_g, b + 1)
                    pool.wait_ge(s_yst[v], 16 * (2 * i + (u - 2) // 2) + 16)
                    pool.sem_inc(s_pc, 1)
                    nc.gpsimd.tensor_tensor(y[v], g[v], tile_of(beb, e), ALU.add).then_inc(s_y, 1)

            pool.sem_inc(s_xb, 2)
            pool.wait_ge(s_bb, 64)
            pipeline(pool, turn, 1, 2)

        @block.scalar
        def _(act):
            def turn(b, i, u, middle=False):
                v = u % 2
                if inside(b + 2, middle):
                    act.wait_ge(s_T, b + 5)
                    act.wait_ge(s_H, b + 3)
                    nc.scalar.copy(xsT[v], psX[v][:, :]).then_inc(s_xT, 1)
                if inside(b - 2, middle):
                    act.wait_ge(s_v, b - 1)
                    nc.scalar.activation(sd[v], mv[v][:, 1:2], ACT.Sqrt, bias=k["epsm"]).then_inc(s_sd, 1)
                    act.wait_ge(s_nm, b - 1)
                    act.wait_ge(s_g, b - 1)
                    nc.scalar.activation(n[v], r[v], ACT.Identity, bias=nm[v], scale=rs[v]).then_inc(s_n, 1)
                if inside(b, middle):
                    act.wait_ge(s_G, b + 3)
                    act.wait_ge(s_Y, b + 1)
                    nc.scalar.activation(hT[v], psG[v][:, 0:F], ACT.Relu).then_inc(s_hT, 1)

            pipeline(act, turn, 2, 2)

        @block.vector
        def _(dve):
            def turn(b, i, u, middle=False):
                v, w = u % 2, (u + 1) % 2
                if inside(b - 2, middle):
                    dve.wait_ge(s_Y, b + 1)
                    dve.wait_ge(s_xb, b + 1)
                    dve.wait_ge(s_n, b - 1)
                    nc.vector.tensor_tensor(r[v], psY[v][:, :], xb[(u + 2) % 4], ALU.add).then_inc(s_r, 1)
                    dve.wait_ge(s_r, b + 1)
                    nc.vector.bn_stats(st[v], r[v]).then_inc(s_st, 1)
                    dve.wait_ge(s_st, b - 1)
                    dve.sem_inc(s_vo, 1)
                    nc.vector.bn_aggr(mv[v], st[v]).then_inc(s_v, 1)
                    dve.wait_ge(s_sd, b - 1)
                    nc.vector.reciprocal(rs[v], sd[v]).then_inc(s_rs, 1)
                    dve.wait_ge(s_rs, b - 1)
                    nc.vector.scalar_tensor_tensor(nm[v], mv[v][:, 0:1], -1.0, rs[v], ALU.mult, ALU.mult).then_inc(s_nm, 1)
                if inside(b + 1, middle):
                    e = dve.value_load(k["expert"][0:1, bass.ds(b + 1, 1)], min_val=0, max_val=NX - 1)
                    dve.wait_ge(s_H, b + 4)
                    dve.wait_ge(s_G, b + 2)
                    nc.vector.tensor_tensor(hb[w], psH[w][:, 0:F], tile_of(b1b, e), ALU.add).then_inc(s_hb, 1)

            dve.sem_inc(s_r, 2)
            dve.wait_ge(s_bb, 64)
            pipeline(dve, turn, 1, 2)

        @block.tensor
        def _(pe):
            def turn(b, i, u, middle=False):
                v, w = u % 2, (u + 1) % 2
                if inside(b + 2, middle):
                    j = (u + 2) % 4
                    pe.wait_ge(s_xs[j], 16 * (i + (u + 2) // 4) + 16)
                    pe.wait_ge(s_xT, b + 3)
                    for c in range(C):
                        last = nc.tensor.transpose(psX[v][:, c * P:(c + 1) * P], xs[j][:, c * P:(c + 1) * P], k["ident"])
                    last.then_inc(s_T, 1)
                if inside(b + 1, middle):
                    e = pe.value_load(k["expert"][0:1, bass.ds(b + 1, 1)], min_val=0, max_val=NX - 1)
                    pe.wait_ge(s_xT, b + 4)
                    pe.wait_ge(s_hb, b + 2)
                    for c in range(C):
                        last = nc.tensor.matmul(psH[w][:, 0:F], xsT[w][:, c * P:(c + 1) * P], tile_of(W1, e * C + c), start=c == 0, stop=c == C - 1)
                    last.then_inc(s_H, 1)
                if inside(b, middle):
                    pe.wait_ge(s_hb, b + 3)
                    pe.wait_ge(s_hT, b + 1)
                    for c in range(FC):
                        last = nc.tensor.transpose(psG[v][:, c * P:(c + 1) * P], hb[v][:, c * P:(c + 1) * P], k["ident"])
                    last.then_inc(s_G, 1)
                if inside(b - 1, middle):
                    e = pe.value_load(k["expert"][0:1, bass.ds(b - 1, 1)], min_val=0, max_val=NX - 1)
                    pe.wait_ge(s_hT, b + 2)
                    pe.wait_ge(s_r, b)
                    for c in range(FC):
                        last = nc.tensor.matmul(psY[w][:, :], hT[w][:, c * P:(c + 1) * P], tile_of(W2, e * FC + c), start=c == 0, stop=c == FC - 1)
                    last.then_inc(s_Y, 1)

            for s in (s_T, s_xT, s_H, s_hb, s_G, s_hT, s_Y, s_g, s_n):
                pe.sem_inc(s, 2)
            for u in range(2):
                pe.sem_inc(s_yst[u], 16)
            pe.wait_ge(s_w1, 16)
            pe.wait_ge(s_w2, 16)
            pipeline(pe, turn, 2, 1)


def combine(nc, sem, d, k, X, keep, out):
    R = 4
    m = Mem(X.rearrange("p t n -> p (t n)"), NT * D)
    x1, y1, y2, o1, o = ([m.take(D) for _ in range(R)] for _ in range(5))
    s_x1, s_y1, s_y2, s_st = ([sem(f"{n}{r}") for r in range(R)] for n in ("x1_loaded", "y1_gathered", "y2_gathered", "out_stored"))
    s_o1, s_o = sem("first_added"), sem("out_made")
    turns = (REAL - 1) // R
    assert turns * R == REAL - 1

    with nc.Block() as block:
        @block.sync
        def _(sp):
            for r in range(R):
                sp.dma_start(x1[r], d["x1"][r * P:(r + 1) * P, :]).then_inc(s_x1[r], 16)
            def store(t, r):
                sp.wait_ge(s_o, t + 1)
                sp.dma_start(out[bass.ds(t * P, P), :], o[r]).then_inc(s_st[r], 16)

            with sp.Fori(0, turns - 1) as i:
                for r in range(R):
                    store(R * i + r, r)
                    sp.dma_start(x1[r], d["x1"][bass.ds((R * i + R + r) * P, P), :]).then_inc(s_x1[r], 16)
            for r in range(R):
                store(R * (turns - 1) + r, r)
                if r == 0:
                    sp.dma_start(x1[0], d["x1"][R * turns * P:(R * turns + 1) * P, :]).then_inc(s_x1[0], 16)
            sp.wait_ge(s_o, REAL)
            a = (REAL - 1) * P
            sp.dma_start(out[a:a + 96, :], o[0][0:96, :]).then_inc(s_st[0], 16)
            sp.dma_start(out[a + 96:N, :], o[0][96:LAST, :]).then_inc(s_st[0], 16)
            for r in range(R):
                sp.wait_ge(s_st[r], 16 * turns + 16 + (32 if r == 0 else 0))

        @block.gpsimd
        def _(pool):
            for t in range(REAL):
                r = t % R
                if t >= R:
                    pool.wait_ge(s_o, t - R + 1)
                rows = P if t < REAL - 1 else LAST
                for j, (y, s) in enumerate(((y1, s_y1), (y2, s_y2))):
                    pool.indirect_dma_start(y[r][0:rows, :], None, d["ys"], bass.IndirectOffsetOnAxis(ap=k["pos"][0:rows, j, t:t + 1], axis=0)).then_inc(s[r], 16)

        @block.vector
        def _(dve):
            def tile(t, i, r, rows):
                dve.wait_ge(s_x1[r], 16 * i + 16)
                dve.wait_ge(s_y1[r], 16 * i + 16)
                nc.vector.scalar_tensor_tensor(o1[r][0:rows, :], y1[r][0:rows, :], k["gate"][0:rows, 0, bass.ds(t, 1)], x1[r][0:rows, :], ALU.mult, ALU.add).then_inc(s_o1, 1)
                dve.wait_ge(s_y2[r], 16 * i + 16)
                dve.wait_ge(s_o1, t + 1)
                dve.wait_ge(s_st[r], 16 * i + 16)
                nc.vector.scalar_tensor_tensor(o[r][0:rows, :], y2[r][0:rows, :], k["gate"][0:rows, 1, bass.ds(t, 1)], o1[r][0:rows, :], ALU.mult, ALU.add).then_inc(s_o, 1)

            for r in range(R):
                dve.sem_inc(s_st[r], 16)
            with dve.Fori(0, turns) as i:
                for r in range(R):
                    tile(R * i + r, i, r, P)
            tile(REAL - 1, turns, 0, LAST)


_INS = ["x", "src", "dst", "L0_gnn_W", "L0_gnn_b", "L0_mix_w_qkv", "L0_mix_w_out", "L0_mix_b_out", "L0_ffn_router_w",
        "L0_ffn_w1", "L0_ffn_b1", "L0_ffn_w2", "L0_ffn_b2", "L0_ffn_gamma", "L0_ffn_beta"]


def kernel(**inputs):
    import concourse.bacc as bacc
    import numpy as np
    from concourse.bass_utils import run_bass_kernel_spmd

    nc = bacc.Bacc("TRN2", target_bir_lowering=False, num_devices=1)
    arrays, args = {}, []
    for name in _INS:
        a = np.ascontiguousarray(inputs[name])
        arrays[f"in_{name}"] = a
        args.append(nc.dram_tensor(f"in_{name}", a.shape, mybir.dt.from_np(a.dtype), kind="ExternalInput").ap())
    args.append(nc.dram_tensor("out_x", (N, D), FP32, kind="ExternalOutput").ap())
    build(nc, *args)
    r = run_bass_kernel_spmd(nc, [arrays], core_ids=[0])
    return r.results[0]["out_x"]
```

```python
from contextlib import ExitStack

import concourse.bass as bass
from concourse import mybir

FP32 = mybir.dt.float32
FP32R = mybir.dt.float32r
BF16 = mybir.dt.bfloat16
I32 = mybir.dt.int32
U32 = mybir.dt.uint32
ALU = mybir.AluOpType
ACT = mybir.ActivationFunctionType

P = 128
N = 6250
D = 512
E = 100000
C = D // P
HEAD = 64
HEADS = D // HEAD
NX = 8
F = 256
FC = F // P
EPS_LN = 1e-5
EPS_MOE = 1e-6
EPS_Z = 1e-6

NT = 50
REAL = -(-N // P)
LAST = N - (REAL - 1) * P
WINDOWS = REAL
PAIR = 2 * P
BLOCKS = -(-E // PAIR)
BG = -(-BLOCKS // P)
STEPS = 8
TURNS = -(-(BLOCKS + WINDOWS - 1) // STEPS)
T = TURNS * STEPS
SLOTS = 2 * STEPS
SPLIT = (0, 1, 3, 4, 5, 7)
TILE_SPLIT = len(SPLIT) // 2
MB = 106
ROWS = NT * P


class Mem:

    def __init__(self, tensor, size, dt=FP32):
        self.t, self.size, self.dt, self.at = tensor, size, dt, 0

    def take(self, *shape, dt=None):
        dt = dt or self.dt
        n = 1
        for s in shape:
            n *= s
        words = -(-n // 2) if dt == BF16 else n
        words = -(-words // 8) * 8
        assert self.at + words <= self.size, (self.at, words, self.size)
        v = self.t[:, self.at:self.at + words]
        self.at += words
        if dt != self.dt:
            v = v.bitcast(dt)
        v = v[:, 0:n]
        if len(shape) == 2:
            v = v.rearrange("p (a b) -> p a b", b=shape[1])
        elif len(shape) == 3:
            v = v.rearrange("p (a b c) -> p a b c", b=shape[1], c=shape[2])
        return v


class Chain:

    def __init__(self, eng, sem):
        self.eng, self.sem, self.n = eng, sem, 0

    def __call__(self, ins):
        self.add(ins)
        self.wait()

    def add(self, ins):
        ins.then_inc(self.sem, 1)
        self.n = self.n + 1

    def wait(self):
        self.eng.wait_ge(self.sem, self.n)

    def loop(self, i, per):
        self.base, self.per, self.start = self.n, per, self.n
        self.n = per * i + self.n
        self.inside = 0

    def done(self, count):
        self.n = self.base + self.per * count


def tile_of(x, t):
    return x[:, bass.ds(t, 1), :].rearrange("p a n -> p (a n)")


def flat(v):
    return v.rearrange("p a b -> p (a b)")


def build(nc, x, src, dst, gW, gb, wqkv, wout, bout, rw, w1, b1, w2, b2, gamma, beta, out):
    with ExitStack() as ctx:
        uid = [0]

        retired = []

        def stage(run, words, *args):
            own = []

            def sem(name):
                uid[0] += 1
                own.append(nc.alloc_semaphore(name=f"{name}_{uid[0]}"))
                return own[-1]

            uid[0] += 1
            with nc.sbuf_tensor(f"scratch_{uid[0]}", [P, words], FP32) as scratch:
                run(nc, sem, d, k, X, Mem(scratch, words), *args)
            for s in retired:
                nc.release_semaphore(s)
            retired[:] = own
            if run is not combine:
                for s in own:
                    nc.gpsimd.sem_clear(s)

        def dram(name, shape, dt=FP32):
            return nc.dram_tensor(name, shape, dt, kind="Internal").ap()

        d = dict(
            xnT=dram("xnT_scratch", (NT, P, D)),
            xb=dram("xb_scratch", (ROWS, D)),
            h=dram("h_scratch", (ROWS, D)),
            xm=dram("xm_scratch", (ROWS, D)),
            x1=dram("x1_scratch", (ROWS, D)),
            xs=dram("xs_scratch", (MB * P, D)),
            ys=dram("ys_scratch", (MB * P, D)),
        )
        big = ctx.enter_context(nc.sbuf_tensor("big", [P, NT * D], FP32))
        X = big[:, :].rearrange("p (t n) -> p t n", n=D)
        KEPT, LATE = 3912, 1264
        keep = Mem(ctx.enter_context(nc.sbuf_tensor("kept", [P, KEPT], FP32)), KEPT)
        k = dict(
            ident=keep.take(P), tri=keep.take(P), ones=keep.take(P), bd=keep.take(P), iota=keep.take(P),
            pidx=keep.take(1), eps=keep.take(1), epsm=keep.take(1), epsz=keep.take(1),
            rowmask=keep.take(NT), stats=keep.take(NT, 6), rstd=keep.take(NT), nmr=keep.take(NT),
            sdeg=keep.take(NT), dinv=keep.take(NT), small=keep.take(8, NT),
            win=keep.take(T + STEPS, dt=I32), edge_src=keep.take(2 * (T + STEPS)), edge_dst=keep.take(2 * (T + STEPS)),
        )
        banks = [ctx.enter_context(nc.psum_tensor(f"bank{i}", [P, 512], FP32)) for i in range(8)]
        stage(prepare, 23600, banks, x, src, dst, gW, bout)
        stage(mix, 11040, banks, wqkv, wout, gb)
        late = Mem(ctx.enter_context(nc.sbuf_tensor("late", [P, LATE], FP32)), LATE)
        k.update(
            M1=late.take(NT, NX), M2=late.take(NT, NX), v12=late.take(NT, 2),
            pos=late.take(2, NT, dt=I32), gate=late.take(2, NT),
            expert=late.take(MB, dt=I32), wr=late.take(C, NX),
        )
        stage(route, 20000, banks, rw)
        stage(dispatch, 20000, banks)
        stage(experts, 20000, banks, w1, b1, w2, b2, gamma, beta)
        stage(combine, 8, out)


def prepare(nc, sem, d, k, X, keep, banks, x, src, dst, gW, bout):
    W = keep.take(C, D)
    boutb = keep.take(D)
    xn = [keep.take(D) for _ in range(2)]
    xT = [keep.take(C, P) for _ in range(2)]
    xb = [keep.take(D) for _ in range(2)]
    nat_i = keep.take(BG, PAIR, dt=I32)
    nat_s = keep.take(BG, PAIR)
    nat_d = keep.take(BG, PAIR)
    dT = keep.take(2, BG * P, dt=I32)
    dT2 = keep.take(2, BG * P, dt=I32)
    lo = keep.take(2, BG * P, dt=BF16)
    hi = keep.take(2, BG * P, dt=BF16)
    HB = 16
    onelo = [keep.take(P, HB, dt=BF16) for _ in range(2)]
    onehi = [keep.take(WINDOWS + 1, HB, dt=BF16) for _ in range(2)]
    iota_b = keep.take(P, HB, dt=BF16)
    iota_i = keep.take(T, dt=I32)
    iota_t = keep.take(T)
    zero = keep.take(D)
    onehot = keep.take(BG, T)
    spread = keep.take(2, P)
    block_of = keep.take(T)
    over_w = keep.take(T)
    S = k["small"]
    L = keep.take(5, NT)
    TURNS_X = NT // 2
    GRAPH = -(-BLOCKS // HB) // 2
    assert 2 * GRAPH + 1 >= -(-BLOCKS // HB) and 2 * GRAPH <= TURNS_X
    STOPS = (0, 4, 8, GRAPH, 14, 16, 18, 20, TURNS_X - 1)
    SCHEDULE = {14: 1, 16: 2, 18: 3, 20: 4}
    X_LOADS = (0, 10, 18, 26, 34, 42, REAL - 1)
    LOADS = len(X_LOADS) - 1
    NORM = {4: 1, 8: 2, GRAPH: 3, 16: 4, 20: 5}
    s_x = [sem(f"x_loaded{i}") for i in range(LOADS + 1)]
    s_xz, s_edges0, s_w = sem("x_pad_zeroed"), sem("edges_padded"), sem("weights_loaded")
    s_src, s_dst = sem("src_loaded"), sem("dst_loaded")
    s_iota, s_const = sem("iotas_made"), sem("constants_made")
    s_natd, s_dTp = sem("dst_converted"), sem("dst_transposed")
    s_var, s_sq, s_ln = sem("variances"), sem("std_done"), sem("ln_ready")
    s_xn, s_T, s_xT, s_h, s_hs = sem("xn_made"), sem("xn_transposed"), sem("xT_copied"), sem("h_made"), sem("h_kept")
    s_xb = sem("xb_made")
    s_xTst = [sem(f"xT_stored{u}") for u in range(2)]
    s_xbst = [sem(f"xb_stored{u}") for u in range(2)]
    s_lo, s_hist = sem("onehots_made"), sem("histogram_step")
    s_deg, s_sdeg, s_dinv = sem("degrees_done"), sem("sqrt_degree"), sem("dinv_made")
    s_sc, s_vo = sem("h_scaled"), sem("vector_ordered")
    s_hst, s_z = sem("h_stored"), sem("zero_row")
    s_c, s_pe, s_sch = sem("vector_chain"), sem("schedule_products"), sem("schedule_tables")
    s_pc, s_ac = sem("pool_ordered"), sem("act_ordered")
    psT, psH, psD, psA, psB = banks[0:2], banks[2:4], banks[4], banks[5], banks[6]
    s_bout = sem("b_out_loaded")
    full = (BLOCKS - 1) // P * P
    rest = (E // PAIR) - full
    tail = E - (E // PAIR) * PAIR

    def norm_tiles(n):
        return slice(X_LOADS[n], X_LOADS[n + 1] if n < LOADS - 1 else NT)

    def edges(eng, a, to, s):
        g = full // P
        eng.dma_start(to[:, 0:g, :], a[0:full * PAIR].rearrange("(g p j) -> p g j", p=P, j=PAIR)).then_inc(s, 16)
        eng.dma_start(to[0:rest, g, :], a[full * PAIR:(full + rest) * PAIR].rearrange("(p j) -> p j", j=PAIR)).then_inc(s, 16)
        eng.dma_start(to[rest:rest + 1, g, 0:tail], a[E - tail:E].rearrange("(p j) -> p j", p=1)).then_inc(s, 16)

    def rows(eng, i):
        a, b = X_LOADS[i], X_LOADS[i + 1]
        eng.dma_start(X[:, a:b, :], x[a * P:b * P, :].rearrange("(t p) n -> p t n", p=P)).then_inc(s_x[i], 16)

    with nc.Block() as block:
        @block.sync
        def _(sp):
            sp.wait_ge(s_edges0, 2)
            edges(sp, dst, nat_i, s_dst)
            rows(sp, 0)
            sp.dma_start(W, gW.rearrange("(c p) n -> p c n", p=P)).then_inc(s_w, 16)
            sp.dma_start(boutb, bout.rearrange("(a n) -> a n", a=1).broadcast_to([P, D])).then_inc(s_bout, 16)

            def stores(i):
                for u in range(2):
                    sp.wait_ge(s_xb, 2 * i + u + 1)
                    sp.dma_start(d["xb"][bass.ds((2 * i + u) * P, P), :], xb[u]).then_inc(s_xbst[u], 16)
                    sp.wait_ge(s_xT, 2 * i + u + 1)
                    sp.dma_start(d["xnT"][bass.ds(2 * i + u, 1), :, :].rearrange("a p n -> p (a n)"), flat(xT[u])).then_inc(s_xTst[u], 16)

            def store_h(i):
                sp.dma_start(d["h"][bass.ds(i * 2 * P, 2 * P), :].rearrange("(t p) n -> p t n", p=P), X[:, bass.ds(2 * i, 2), :]).then_inc(s_hst, 16)

            with sp.Fori(0, GRAPH + 1) as i:
                stores(i)
            with sp.Fori(GRAPH + 1, TURNS_X) as i:
                stores(i)
                sp.wait_ge(s_hs, 2 * i + 2)
                store_h(i - 1)
                sp.wait_ge(s_sc, 2 * i - 2 * GRAPH)
                store_h(i - GRAPH - 1)
            sp.wait_ge(s_hs, NT + 2)
            store_h(TURNS_X - 1)
            for u in range(2):
                sp.wait_ge(s_xTst[u], 16 * TURNS_X + 16)
                sp.wait_ge(s_xbst[u], 16 * TURNS_X + 16)
            sp.wait_ge(s_hst, 16 * TURNS_X)

        @block.gpsimd
        def _(pool):
            nc.gpsimd.iota(iota_i, [[1, T]], base=0, channel_multiplier=0).then_inc(s_iota, 1)
            nc.gpsimd.iota(dT[:, 0, 0:1], [[1, 1]], base=0, channel_multiplier=1).then_inc(s_iota, 1)
            pool.wait_ge(s_bout, 16)

            def biased(i):
                for u in range(2):
                    pool.wait_ge(s_xbst[u], 16 * i + 16)
                    pool.sem_inc(s_pc, 1)
                    nc.gpsimd.tensor_tensor(xb[u], tile_of(X, 2 * i + u), boutb, ALU.add).then_inc(s_xb, 1)

            for n in range(LOADS):
                pool.wait_ge(s_x[n], 16)
                with pool.Fori(X_LOADS[n] // 2, X_LOADS[n + 1] // 2) as i:
                    biased(i)
            pool.wait_ge(s_x[LOADS], 32)
            biased(TURNS_X - 1)

        @block.scalar
        def _(act):
            def std(n):
                act.wait_ge(s_var, n + 1)
                t = norm_tiles(n)
                nc.scalar.activation(L[:, 0, t], L[:, 1, t], ACT.Sqrt, bias=k["eps"]).then_inc(s_sq, 1)
                act.wait_ge(s_ln, n + 1)

            def pair(i):
                for u in range(2):
                    act.wait_ge(s_T, 2 * i + u + 1)
                    act.sem_inc(s_ac, 1)
                    nc.scalar.activation(xn[u], tile_of(X, 2 * i + u), ACT.Identity,
                                         bias=k["nmr"][:, bass.ds(2 * i + u, 1)], scale=k["rstd"][:, bass.ds(2 * i + u, 1)]).then_inc(s_xn, 1)
                for u in range(2):
                    act.wait_ge(s_T, 2 * i + u + 3)
                    act.wait_ge(s_h, 2 * i + u + 1)
                    act.wait_ge(s_xTst[u], 16 * i + 16)
                    nc.scalar.copy(flat(xT[u]), psT[u][:, :]).then_inc(s_xT, 1)

            act.wait_ge(s_x[0], 16)
            for i in range(1, LOADS):
                rows(act, i)
            act.wait_ge(s_xz, 1)
            a = (REAL - 1) * P
            act.dma_start(X[0:96, REAL - 1, :], x[a:a + 96, :]).then_inc(s_x[LOADS], 16)
            act.dma_start(X[96:LAST, REAL - 1, :], x[a + 96:N, :]).then_inc(s_x[LOADS], 16)
            act.wait_ge(s_edges0, 2)
            edges(act, src, nat_s.bitcast(I32), s_src)
            std(0)
            pair(0)
            for a, b in zip(STOPS[:-1], STOPS[1:]):
                if a in NORM:
                    std(NORM[a])
                if a == GRAPH:
                    act.wait_ge(s_deg, 1)
                    nc.scalar.activation(k["sdeg"], S[:, 2, :], ACT.Sqrt).then_inc(s_sdeg, 1)
                    act.wait_ge(s_dinv, 1)
                    act.wait_ge(s_hs, 2 * GRAPH + 2)
                with act.Fori(a, b) as i:
                    pair(i + 1)
                    if a >= GRAPH:
                        for u in range(2):
                            t = tile_of(X, 2 * i + u - 2 * GRAPH)
                            nc.scalar.activation(t, t, ACT.Identity, scale=k["dinv"][:, bass.ds(2 * i + u - 2 * GRAPH, 1)]).then_inc(s_sc, 1)

        @block.vector
        def _(dve):
            link = Chain(dve, s_c)
            nc.vector.memset(nat_i, -1).then_inc(s_edges0, 1)
            nc.vector.memset(nat_s.bitcast(I32), 0).then_inc(s_edges0, 1)
            nc.vector.memset(X[:, REAL - 1:NT, :], 0.0).then_inc(s_xz, 1)
            nc.vector.memset(zero, 0.0).then_inc(s_z, 1)
            nc.vector.memset(k["bd"], 0.0)
            nc.vector.memset(k["ones"], 1.0)
            nc.vector.memset(k["eps"], EPS_LN)
            nc.vector.memset(k["epsm"], EPS_MOE)
            nc.vector.memset(k["epsz"], EPS_Z)
            link(nc.vector.memset(k["rowmask"], 1.0))
            nc.vector.memset(k["rowmask"][:, REAL:NT], 0.0)
            link(nc.vector.memset(k["bd"][0:HEAD, 0:HEAD], 1.0))
            link(nc.vector.memset(k["bd"][HEAD:P, HEAD:P], 1.0))
            dve.wait_ge(s_iota, 2)
            nc.vector.tensor_copy(k["iota"], iota_i[:, 0:P])
            nc.vector.tensor_copy(iota_t, iota_i)
            link(nc.vector.tensor_copy(k["pidx"], dT[:, 0, 0:1]))
            nc.vector.tensor_copy(iota_b, k["iota"].unsqueeze(2).to_broadcast([P, P, HB]))
            nc.vector.tensor_scalar(k["ident"], k["iota"], k["pidx"], None, ALU.is_equal)
            nc.vector.tensor_scalar(k["tri"], k["iota"], k["pidx"], None, ALU.is_gt)
            link(nc.vector.tensor_scalar(k["rowmask"][:, REAL - 1:REAL], k["pidx"], float(LAST), None, ALU.is_lt))
            dve.sem_inc(s_const, 1)
            dve.wait_ge(s_dst, 48)
            nc.vector.tensor_copy(flat(nat_d), flat(nat_i)).then_inc(s_natd, 1)
            dve.wait_ge(s_dTp, 1)
            for half in range(2):
                link.add(nc.vector.tensor_copy(dT[:, half, :], banks[5 + half][:, :]))
            link.wait()
            link(nc.vector.tensor_single_scalar(flat(dT2), flat(dT), P.bit_length() - 1, ALU.arith_shift_right))
            link(nc.vector.tensor_copy(flat(hi), flat(dT2)))
            link(nc.vector.tensor_single_scalar(flat(dT2), flat(dT), P - 1, ALU.bitwise_and))
            link(nc.vector.tensor_copy(flat(lo), flat(dT2)))
            def norm(n):
                t = norm_tiles(n)
                ln_stats(nc, link, k, L, t)
                dve.sem_inc(s_var, 1)
                dve.wait_ge(s_sq, n + 1)
                ln_scales(nc, link, k, L, t)
                dve.sem_inc(s_ln, 1)

            def onehots(n, r, u):
                dve.wait_ge(s_hist, n + 1)
                nc.vector.tensor_tensor(onelo[u], lo[:, u, bass.ds(r * HB, HB)].unsqueeze(1).to_broadcast([P, P, HB]), iota_b, ALU.is_equal)
                nc.vector.tensor_tensor(onehi[u], hi[:, u, bass.ds(r * HB, HB)].unsqueeze(1).to_broadcast([P, WINDOWS + 1, HB]),
                                        iota_b[:, 0:WINDOWS + 1, :], ALU.is_equal).then_inc(s_lo, 1)

            def keep_h(t, u, scaled):
                dve.wait_ge(s_h, t + 3)
                dve.wait_ge(s_xb, t + 1)
                nc.vector.tensor_scalar(tile_of(X, t), psH[u][:, :], k["dinv"][:, bass.ds(t, 1)] if scaled else 1.0, None, ALU.mult).then_inc(s_hs, 1)

            dve.wait_ge(s_x[0], 16)
            for t in range(X_LOADS[1]):
                last = nc.vector.bn_stats(k["stats"][:, t, :], X[:, t, :])
            link(last)
            norm(0)
            for half in range(2):
                onehots(half, 0, half)
            for a, b in zip(STOPS[:-1], STOPS[1:]):
                if a in NORM:
                    dve.wait_ge(s_vo, 2 * a)
                    norm(NORM[a])
                if a == GRAPH:
                    nc.vector.memset(S[:, 2, :], 1.0)
                    dve.wait_ge(s_hist, 3 + 4 * GRAPH + 2)
                    link(nc.vector.tensor_copy(S[:, 3, :], psD[:, 0:NT]))
                    link(nc.vector.tensor_scalar(S[:, 2, 0:WINDOWS], S[:, 3, 0:WINDOWS], 1.0, 1e-12, ALU.add, ALU.max))
                    dve.sem_inc(s_deg, 1)
                    dve.wait_ge(s_sdeg, 1)
                    link(nc.vector.reciprocal(k["dinv"], k["sdeg"]))
                    dve.sem_inc(s_dinv, 1)
                    schedule_vector(0, nc, dve, link, k, S, nat_s, nat_d, nat_i, iota_t, onehot, over_w, spread, block_of, banks, s_src, s_pe, s_sch)
                if a in SCHEDULE:
                    schedule_vector(SCHEDULE[a], nc, dve, link, k, S, nat_s, nat_d, nat_i, iota_t, onehot, over_w, spread, block_of, banks, s_src, s_pe, s_sch)
                if 2 * a + X_LOADS[1] in X_LOADS[:-1]:
                    n = X_LOADS.index(2 * a + X_LOADS[1])
                    dve.wait_ge(s_x[n], 16)
                    if n == LOADS - 1:
                        dve.wait_ge(s_x[LOADS], 32)
                with dve.Fori(a, b) as i:
                    for u in range(2):
                        if a < GRAPH:
                            for half in range(2):
                                onehots(4 * i + 2 * u + 2 + half, 2 * i + u + 1, half)
                        keep_h(2 * i + u, u, a >= GRAPH)
                    if a < 20:
                        for u in range(2):
                            nc.vector.bn_stats(k["stats"][:, bass.ds(2 * i + X_LOADS[1] + u, 1), :].rearrange("p a s -> p (a s)"), tile_of(X, 2 * i + X_LOADS[1] + u)).then_inc(s_vo, 1)
            for u in range(2):
                keep_h(NT - 2 + u, u, True)
            schedule_vector(5, nc, dve, link, k, S, nat_s, nat_d, nat_i, iota_t, onehot, over_w, spread, block_of, banks, s_src, s_pe, s_sch)

        @block.tensor
        def _(pe):
            pe.sem_inc(s_T, 2)
            pe.sem_inc(s_h, 2)
            pe.sem_inc(s_hs, 2)
            for u in range(2):
                pe.sem_inc(s_xTst[u], 16)
                pe.sem_inc(s_xbst[u], 16)
            pe.wait_ge(s_const, 1)
            pe.wait_ge(s_natd, 1)
            for half in range(2):
                for g in range(BG):
                    last = nc.tensor.transpose(banks[5 + half][:, g * P:(g + 1) * P], nat_d[:, g, half * P:(half + 1) * P], k["ident"])
            last.then_inc(s_dTp, 1)
            pe.wait_ge(s_z, 1)
            nc.tensor.matmul(psD[:, 0:WINDOWS + 1], zero[:, 0:P], zero[:, 0:WINDOWS + 1], start=True, stop=False).then_inc(s_hist, 2)
            pe.wait_ge(s_w, 16)

            def transpose(t, u):
                pe.wait_ge(s_xn, t + 1)
                for c in range(C):
                    last = nc.tensor.transpose(psT[u][:, c * P:(c + 1) * P], xn[u][:, c * P:(c + 1) * P], k["ident"])
                last.then_inc(s_T, 1)

            def count(n, u):
                pe.wait_ge(s_lo, n + 1)
                for j in range(HB):
                    last = nc.tensor.matmul(psD[:, 0:WINDOWS + 1], onelo[u][:, :, j], onehi[u][:, :, j], start=False, stop=False)
                last.then_inc(s_hist, 1)

            def product(t, u):
                pe.wait_ge(s_xT, t + 1)
                pe.wait_ge(s_hs, t + 1)
                for c in range(C):
                    last = nc.tensor.matmul(psH[u][:, :], xT[u][:, c, :], W[:, c, :], start=c == 0, stop=c == C - 1)
                last.then_inc(s_h, 1)

            for u in range(2):
                transpose(u, u)
            for a, b in zip(STOPS[:-1], STOPS[1:]):
                if a == GRAPH:
                    for u in range(2):
                        count(4 * GRAPH + u, u)
                    nc.tensor.matmul(psD[:, 0:WINDOWS + 1], zero[:, 0:P], zero[:, 0:WINDOWS + 1], start=False, stop=True).then_inc(s_hist, 1)
                if a in SCHEDULE:
                    schedule_tensor(SCHEDULE[a], nc, pe, k, S, nat_i, nat_d, onehot, over_w, spread, banks, s_pe, s_sch)
                with pe.Fori(a, b) as i:
                    for u in range(2):
                        if a < GRAPH:
                            for half in range(2):
                                count(4 * i + 2 * u + half, half)
                        product(2 * i + u, u)
                        transpose(2 * i + 2 + u, u)
            for u in range(2):
                product(NT - 2 + u, u)
            schedule_tensor(5, nc, pe, k, S, nat_i, nat_d, onehot, over_w, spread, banks, s_pe, s_sch)


def mix(nc, sem, d, k, X, keep, banks, wqkv, wout, gb):
    words = SLOTS * D + SLOTS * P + 4 * D
    with nc.sbuf_tensor("rounded", [P, words], FP32R) as tensor:
        mix_in(nc, sem, d, k, X, keep, Mem(tensor, words, FP32R), banks, wqkv, wout, gb)


def mix_in(nc, sem, d, k, X, keep, rounded, banks, wqkv, wout, gb):
    A = keep.take(2 * C, D)
    B = keep.take(C, D)
    Gr = rounded.take(SLOTS, D)
    hotr = rounded.take(SLOTS, P)
    high = rounded.take(4, D)
    G, hot = Gr.bitcast(FP32), hotr.bitcast(FP32)
    idx = keep.take(SLOTS, dt=I32)
    xT = keep.take(2, D)
    kvm = keep.at
    gbb = keep.take(D)
    ek, rk, kk, vv = (keep.take(D) for _ in range(4))
    zero = keep.take(P)
    keep.at = kvm
    eq = [keep.take(2, 2 * P) for _ in range(2)]
    rq = [keep.take(2, 2 * P) for _ in range(2)]
    sums = keep.take(P)
    xb = [B[:, u, :] for u in range(2)]
    xm = [B[:, 2 + u, :] for u in range(2)]
    Wk, Wv, M, Wq = A[:, 0:C, :], A[:, C:2 * C, :], A[:, 0:C, :], A[:, C:2 * C, :]
    kvT = keep.take(C, P)
    ksum = keep.take(C, HEADS)
    sel = keep.take(C, P)[0:HEADS]
    z = flat(rq[0])[0:HEADS, 0:2 * P]
    agg_banks = 4
    s_wk, s_wv, s_wo, s_wq, s_gb = (sem(n) for n in ("wk_loaded", "wv_loaded", "wout_loaded", "wq_loaded", "b_loaded"))
    s_g = [sem(f"gathered{i}") for i in range(SLOTS)]
    s_idx, s_hot = sem("indices_ready"), sem("onehot_ready")
    s_high, s_low = sem("high_parts"), sem("low_parts")
    s_agg, s_add, s_bg = sem("step_summed"), sem("step_added"), sem("bias_added")
    s_xT = [sem(f"xT_loaded{u}") for u in range(2)]
    s_K, s_kr, s_k, s_V, s_v, s_kv = (sem(n) for n in ("k_made", "k_read", "k_ready", "v_made", "v_ready", "kv_summed"))
    s_z, s_z1, s_rz = sem("zeros_ready"), sem("norm_read"), sem("norm_inverted")
    s_Z = sem("inverses_spread")
    s_bd, s_Mp, s_M = sem("kv_blocks_ready"), sem("m_made"), sem("m_kept")
    s_xp, s_xb = sem("xT_pair_loaded"), [sem(f"xb_loaded{u}") for u in range(2)]
    s_Q, s_qr, s_q, s_D, s_qs, s_O, s_xm = (sem(n) for n in ("q_made", "q_read", "q_ready", "norm_made", "q_scaled", "attention_out", "xm_made"))
    s_xmst = [sem(f"xm_stored{u}") for u in range(2)]
    s_c, s_pc = sem("vector_chain"), sem("pool_ordered")
    HALF = STEPS // 2
    KV = NT // 2
    psA, psK, psV, psKV, psS = banks[0:4], banks[4], banks[5], banks[6], banks[7]
    psQ, psO = banks[4:6], banks[6:8]

    with nc.Block() as block:
        @block.sync
        def _(sp):
            w = wqkv.rearrange("(c p) n -> p c n", p=P)
            for u in range(2):
                sp.dma_start(xT[:, u, :], d["xnT"][u]).then_inc(s_xT[u], 16)
            sp.dma_start(Wk, w[:, :, D:2 * D]).then_inc(s_wk, 16)
            sp.dma_start(Wv, w[:, :, 2 * D:3 * D]).then_inc(s_wv, 16)
            sp.dma_start(gbb, gb.rearrange("(a n) -> a n", a=1).broadcast_to([P, D])).then_inc(s_gb, 16)
            sp.dma_start(B, wout.rearrange("(c p) n -> p c n", p=P)).then_inc(s_wo, 16)
            with sp.Fori(0, KV - 1) as i:
                for u in range(2):
                    sp.wait_ge(s_V, 2 * i + u + 1)
                    sp.dma_start(xT[:, u, :], d["xnT"][bass.ds(2 * i + 2 + u, 1), :, :].rearrange("a p n -> p (a n)")).then_inc(s_xT[u], 16)
            sp.wait_ge(s_V, NT)
            sp.dma_start(Wq, w[:, :, 0:D]).then_inc(s_wq, 16)
            sp.dma_start(xT, d["xnT"][0:2].rearrange("t p n -> p t n")).then_inc(s_xp, 16)
            sp.wait_ge(s_Mp, C)
            for u in range(2):
                sp.dma_start(xb[u], d["xb"][u * P:(u + 1) * P, :]).then_inc(s_xb[u], 16)
            with sp.Fori(0, KV - 1) as j:
                sp.wait_ge(s_Q, 2 * j + 2)
                sp.dma_start(xT, d["xnT"][bass.ds(2 * j + 2, 2)].rearrange("t p n -> p t n")).then_inc(s_xp, 16)
                for u in range(2):
                    sp.wait_ge(s_xm, 2 * j + u + 3)
                    sp.dma_start(d["xm"][bass.ds((2 * j + u) * P, P), :], xm[u]).then_inc(s_xmst[u], 16)
                    sp.dma_start(xb[u], d["xb"][bass.ds((2 * j + 2 + u) * P, P), :]).then_inc(s_xb[u], 16)
            for u in range(2):
                sp.wait_ge(s_xm, 2 * KV + 1 + u)
                sp.dma_start(d["xm"][(NT - 2 + u) * P:(NT - 1 + u) * P, :], xm[u]).then_inc(s_xmst[u], 16)
            for u in range(2):
                sp.wait_ge(s_xmst[u], 16 * KV + 16)

        @block.gpsimd
        def _(pool):
            with pool.Fori(0, TURNS) as i:
                for slot in range(SLOTS):
                    if slot % STEPS == 0:
                        pool.wait_ge(s_idx, 2 * i + slot // STEPS + 1)
                    pool.wait_ge(s_agg, STEPS * i + slot // 2 + 1)
                    pool.sem_inc(s_pc, 1)
                    pool.indirect_dma_start(G[:, slot, :], None, d["h"],
                                            bass.IndirectOffsetOnAxis(ap=idx[:, slot:slot + 1], axis=0)).then_inc(s_g[slot], 16)

        @block.scalar
        def _(act):
            def split(i, m):
                s = SPLIT[m]
                for slot in (2 * s, 2 * s + 1):
                    act.wait_ge(s_g[slot], 16 * i + 16)
                act.wait_ge(s_agg, STEPS * i + (SPLIT[m - 2] + 1 + STEPS if m >= 2 else SPLIT[m - 2] + 1))
                nc.scalar.copy(high[:, 2 * (m % 2):2 * (m % 2) + 2, :], G[:, 2 * s:2 * s + 2, :]).then_inc(s_high, 1)

            with act.Fori(0, KV) as i:
                for u in range(2):
                    t = 2 * i + u
                    split(i, TILE_SPLIT * u)
                    split(i, TILE_SPLIT * u + 1)
                    act.wait_ge(s_K, t + 1)
                    act.wait_ge(s_k, t + 1)
                    nc.scalar.activation(ek, psK[:, :], ACT.Exp)
                    nc.scalar.activation(rk, psK[:, :], ACT.Relu).then_inc(s_kr, 1)
                    act.wait_ge(s_V, t + 1)
                    act.wait_ge(s_kv, t + 1)
                    nc.scalar.copy(vv, psV[:, :]).then_inc(s_v, 1)
                    for m in range(TILE_SPLIT * u + 2, TILE_SPLIT * (u + 1)):
                        split(i, m)
            for c in range(C):
                act.wait_ge(s_Mp, c + 1)
                nc.scalar.copy(M[:, c, :], psQ[c % 2][:, :]).then_inc(s_M, 1)
            with act.Fori(KV, 2 * KV) as i:
                split(i, 0)
                split(i, 1)
                for b in range(2):
                    act.wait_ge(s_Q, 2 * i + b + 1 - 2 * KV)
                    act.wait_ge(s_O, 2 * i + 2 - 2 * KV)
                    nc.scalar.activation(flat(eq[b]), psQ[b][:, :], ACT.Exp)
                    nc.scalar.activation(flat(rq[b]), psQ[b][:, :], ACT.Relu).then_inc(s_qr, 1)
                split(i, 2)
                act.wait_ge(s_D, i + 1 - KV)
                nc.scalar.activation(z, psQ[0][0:HEADS, 0:2 * P], ACT.Identity, bias=k["epsz"][0:HEADS, :]).then_inc(s_z1, 1)
                for m in range(3, len(SPLIT)):
                    split(i, m)
            with act.Fori(2 * KV, TURNS) as i:
                for m in range(len(SPLIT)):
                    split(i, m)

        @block.vector
        def _(dve):
            link = Chain(dve, s_c)

            def refresh(half, turn):
                cols = bass.ds(turn * SLOTS + half * STEPS, STEPS)
                nc.vector.tensor_scalar(idx[:, half * STEPS:(half + 1) * STEPS], k["edge_src"][:, cols], 0.0, None, ALU.add).then_inc(s_idx, 1)
                nc.vector.tensor_tensor(
                    hotr[:, half * STEPS:(half + 1) * STEPS, :],
                    k["edge_dst"][:, cols].unsqueeze(2).to_broadcast([P, STEPS, P]),
                    k["iota"].unsqueeze(1).to_broadcast([P, STEPS, P]),
                    ALU.is_equal).then_inc(s_hot, 1)

            def split(i, m):
                rows = slice(2 * SPLIT[m], 2 * SPLIT[m] + 2)
                dve.wait_ge(s_high, len(SPLIT) * i + m + 1)
                nc.vector.tensor_tensor(Gr[:, rows, :], G[:, rows, :], high[:, 2 * (m % 2):2 * (m % 2) + 2, :].bitcast(FP32), ALU.subtract).then_inc(s_low, 1)

            def step(i, s):
                w = dve.value_load(k["win"][0:1, bass.ds(STEPS * i + s, 1)], min_val=0, max_val=WINDOWS - 1)
                dve.wait_ge(s_agg, STEPS * (i + 1) + s + 1)
                dve.wait_ge(s_add, STEPS * i + s + agg_banks)
                nc.vector.tensor_tensor(tile_of(X, w), tile_of(X, w), psA[s % agg_banks][:, :], ALU.add).then_inc(s_add, 1)

            nc.vector.memset(zero, 0.0).then_inc(s_z, 1)
            link.add(nc.vector.memset(ksum, 0.0))
            link(nc.vector.tensor_scalar(sel[:, C - 1, :], k["iota"][0:HEADS, :], float(HEAD), None, ALU.is_ge))
            for c in range(C):
                link(nc.vector.tensor_scalar(sel[:, c, :], sel[:, C - 1, :], 2.0 * c, k["pidx"][0:HEADS, :], ALU.add, ALU.is_equal))
            for half in range(2):
                refresh(half, 0)
            dve.sem_inc(s_k, 1)
            dve.wait_ge(s_gb, 16)
            with dve.Fori(0, KV) as i:
                for u in range(2):
                    t = 2 * i + u
                    split(i, TILE_SPLIT * u)
                    split(i, TILE_SPLIT * u + 1)
                    dve.wait_ge(s_kr, t + 2)
                    dve.wait_ge(s_kv, t + 1)
                    nc.vector.scalar_tensor_tensor(kk, ek, 1.0, rk, ALU.min, ALU.add).then_inc(s_k, 1)
                    for s in range(HALF * u, HALF * u + HALF):
                        step(i, s)
                        if s in SPLIT[TILE_SPLIT * u:TILE_SPLIT * (u + 1) - 2]:
                            split(i, SPLIT.index(s) + 2)
                        if s == HALF * u:
                            dve.wait_ge(s_add, STEPS * i + s + agg_banks + 1)
                            nc.vector.scalar_tensor_tensor(tile_of(X, t), gbb, k["sdeg"][:, bass.ds(t, 1)], tile_of(X, t), ALU.mult, ALU.add).then_inc(s_bg, 1)
                            dve.wait_ge(s_bg, t + 1)
                    refresh(u, i + 1)
            dve.wait_ge(s_kv, NT + 2)
            nc.vector.tensor_tensor(kvT, psKV[:, :].rearrange("p (c n) -> p c n", n=P), k["bd"].unsqueeze(1).to_broadcast([P, C, P]), ALU.mult)
            link(nc.vector.tensor_copy(sums[:, 0:C], psS[:, 0:C]))
            for h in range(HEADS):
                last = nc.vector.tensor_tensor(ksum[:, h // 2, h:h + 1], k["bd"][:, h % 2 * HEAD:h % 2 * HEAD + 1], sums[:, h // 2:h // 2 + 1], ALU.mult)
            last.then_inc(s_bd, 1)
            with dve.Fori(KV, 2 * KV) as i:
                def out(u):
                    dve.wait_ge(s_O, 2 * i + u + 3 - 2 * KV)
                    dve.wait_ge(s_xb[u], 16 * i + 16 - 16 * KV)
                    dve.wait_ge(s_xmst[u], 16 * i + 16 - 16 * KV)
                    nc.vector.tensor_tensor(xm[u], psO[u][:, :], xb[u], ALU.add).then_inc(s_xm, 1)

                split(i, 0)
                split(i, 1)
                for b in range(2):
                    dve.wait_ge(s_qr, 2 * i + b + 1 - 2 * KV)
                    nc.vector.scalar_tensor_tensor(flat(eq[b]), flat(eq[b]), 1.0, flat(rq[b]), ALU.min, ALU.add).then_inc(s_q, 1)
                for s in range(STEPS):
                    step(i, s)
                    if s == 1:
                        dve.wait_ge(s_z1, i + 1 - KV)
                        nc.vector.reciprocal(z, z).then_inc(s_rz, 1)
                    if s in SPLIT[:-2]:
                        split(i, SPLIT.index(s) + 2)
                    if s == 3:
                        for b in range(2):
                            dve.wait_ge(s_Z, 2 * i + b + 1 - 2 * KV)
                            nc.vector.tensor_tensor(flat(eq[b]), flat(eq[b]), psQ[b][:, :], ALU.mult).then_inc(s_qs, 1)
                        refresh(0, i + 1)
                    if s == 6:
                        out(0)
                refresh(1, i + 1)
                out(1)
            with dve.Fori(2 * KV, TURNS) as i:
                split(i, 0)
                split(i, 1)
                for s in range(STEPS):
                    step(i, s)
                    if s in SPLIT[:-2]:
                        split(i, SPLIT.index(s) + 2)
                    if s == 3:
                        refresh(0, i + 1)
                refresh(1, i + 1)
            dve.wait_ge(s_add, T + agg_banks)

        @block.tensor
        def _(pe):
            def step(i, s):
                if s % HALF == 0:
                    pe.wait_ge(s_hot, 2 * i + s // HALF + 1)
                pe.wait_ge(s_add, STEPS * i + s + 1)
                if s in SPLIT:
                    m = SPLIT.index(s)
                    pe.wait_ge(s_low, len(SPLIT) * i + m + 1)
                    for half in range(2):
                        slot = 2 * s + half
                        nc.tensor.matmul(psA[s % agg_banks][:, :], hotr[:, slot, :], high[:, 2 * (m % 2) + half, :], start=half == 0, stop=False)
                        last = nc.tensor.matmul(psA[s % agg_banks][:, :], hotr[:, slot, :], Gr[:, slot, :], start=False, stop=half == 1)
                else:
                    for half in range(2):
                        slot = 2 * s + half
                        pe.wait_ge(s_g[slot], 16 * i + 16)
                        last = nc.tensor.matmul(psA[s % agg_banks][:, :], hot[:, slot, :], G[:, slot, :], start=half == 0, stop=half == 1)
                last.then_inc(s_agg, 1)

            pe.sem_inc(s_agg, STEPS)
            pe.sem_inc(s_add, agg_banks)
            pe.sem_inc(s_kr, 1)
            pe.sem_inc(s_v, 1)
            for u in range(2):
                pe.sem_inc(s_xmst[u], 16)
            pe.wait_ge(s_z, 1)
            for c in range(C):
                nc.tensor.matmul(psKV[:, c * P:(c + 1) * P], zero, zero, start=c == 0, stop=False)
            nc.tensor.matmul(psS[:, 0:C], zero, zero[:, 0:C], start=True, stop=False).then_inc(s_kv, 1)
            pe.wait_ge(s_wk, 16)
            pe.wait_ge(s_wv, 16)
            with pe.Fori(0, KV) as i:
                for u in range(2):
                    t = 2 * i + u
                    pe.wait_ge(s_xT[u], 16 * i + 16)
                    pe.wait_ge(s_kr, t + 1)
                    for c in range(C):
                        last = nc.tensor.matmul(psK[:, :], xT[:, u, c * P:(c + 1) * P], Wk[:, c, :], start=c == 0, stop=c == C - 1)
                    last.then_inc(s_K, 1)
                    pe.wait_ge(s_v, t + 1)
                    for c in range(C):
                        last = nc.tensor.matmul(psV[:, :], xT[:, u, c * P:(c + 1) * P], Wv[:, c, :], start=c == 0, stop=c == C - 1)
                    last.then_inc(s_V, 1)
                    for s in range(HALF * u, HALF * u + HALF):
                        step(i, s)
                    pe.wait_ge(s_k, t + 2)
                    pe.wait_ge(s_v, t + 2)
                    for c in range(C):
                        nc.tensor.matmul(psKV[:, c * P:(c + 1) * P], vv[:, c * P:(c + 1) * P], kk[:, c * P:(c + 1) * P], start=False, stop=False)
                    for c in range(C):
                        last = nc.tensor.matmul(psS[:, c:c + 1], kk[:, c * P:(c + 1) * P], k["rowmask"][:, bass.ds(t, 1)], start=False, stop=False)
                    last.then_inc(s_kv, 1)
            for c in range(C):
                nc.tensor.matmul(psKV[:, c * P:(c + 1) * P], zero, zero, start=False, stop=c == C - 1)
            nc.tensor.matmul(psS[:, 0:C], zero, zero[:, 0:C], start=False, stop=True).then_inc(s_kv, 1)
            pe.wait_ge(s_bd, 1)
            pe.wait_ge(s_wo, 16)
            pe.wait_ge(s_kr, NT + 1)
            pe.wait_ge(s_v, NT + 1)
            for c in range(C):
                if c >= 2:
                    pe.wait_ge(s_M, c - 1)
                nc.tensor.matmul(psQ[c % 2][:, :], kvT[:, c, :], B[:, c, :], start=True, stop=True).then_inc(s_Mp, 1)
            pe.sem_inc(s_O, 2)
            pe.sem_inc(s_xm, 2)
            pe.sem_inc(s_qs, 2)
            pe.wait_ge(s_M, C)
            pe.wait_ge(s_wq, 16)
            with pe.Fori(KV, 2 * KV) as i:
                pe.wait_ge(s_xp, 16 * i + 16 - 16 * KV)
                pe.wait_ge(s_qs, 2 * i + 2 - 2 * KV)
                for b in range(2):
                    for half in range(2):
                        c = 2 * b + half
                        for kc in range(C):
                            last = nc.tensor.matmul(psQ[b][:, half * 2 * P:(half + 1) * 2 * P], Wq[:, kc, c * P:(c + 1) * P],
                                                    xT.rearrange("p t (c r) -> p t c r", r=P)[:, :, kc, :], start=kc == 0, stop=kc == C - 1)
                    last.then_inc(s_Q, 1)
                step(i, 0)
                step(i, 1)
                pe.wait_ge(s_q, 2 * i + 2 - 2 * KV)
                for c in range(C):
                    last = nc.tensor.matmul(psQ[0][0:HEADS, 0:2 * P], ksum[:, c, :], eq[c // 2][:, c % 2, :], start=c == 0, stop=c == C - 1)
                last.then_inc(s_D, 1)
                step(i, 2)
                step(i, 3)
                pe.wait_ge(s_rz, i + 1 - KV)
                for b in range(2):
                    for half in range(2):
                        last = nc.tensor.matmul(psQ[b][:, half * 2 * P:(half + 1) * 2 * P], sel[:, 2 * b + half, :], z, start=True, stop=True)
                    last.then_inc(s_Z, 1)
                for s in range(4, 7):
                    step(i, s)
                pe.wait_ge(s_qs, 2 * i + 4 - 2 * KV)
                for u in range(2):
                    if u == 1:
                        step(i, 7)
                    pe.wait_ge(s_xm, 2 * i + u + 1 - 2 * KV)
                    for c in range(C):
                        last = nc.tensor.matmul(psO[u][:, :], eq[c // 2][:, c % 2, u * P:(u + 1) * P], M[:, c, :], start=c == 0, stop=c == C - 1)
                    last.then_inc(s_O, 1)
            with pe.Fori(2 * KV, TURNS) as i:
                for s in range(STEPS):
                    step(i, s)


def ln_stats(nc, link, k, S, t=slice(0, NT)):
    st = k["stats"].rearrange("p t c -> p c t")
    link.add(nc.vector.tensor_tensor(S[:, 2, t], st[:, 1, t], st[:, 4, t], ALU.add))
    link.add(nc.vector.tensor_tensor(S[:, 3, t], st[:, 1, t], st[:, 4, t], ALU.subtract))
    link(nc.vector.tensor_tensor(S[:, 4, t], st[:, 2, t], st[:, 5, t], ALU.add))
    link.add(nc.vector.tensor_scalar(S[:, 2, t], S[:, 2, t], 0.5, None, ALU.mult))
    link(nc.vector.scalar_tensor_tensor(S[:, 3, t], S[:, 3, t], 0.25, S[:, 3, t], ALU.mult, ALU.mult))
    link(nc.vector.scalar_tensor_tensor(S[:, 1, t], S[:, 4, t], 1.0 / D, S[:, 3, t], ALU.mult, ALU.add))


def ln_scales(nc, link, k, S, t=slice(0, NT)):
    link(nc.vector.reciprocal(k["rstd"][:, t], S[:, 0, t]))
    link(nc.vector.scalar_tensor_tensor(k["nmr"][:, t], S[:, 2, t], -1.0, k["rstd"][:, t], ALU.mult, ALU.mult))


def schedule_vector(part, nc, dve, link, k, S, nat_s, nat_d, nat_i, iota_t, onehot, over_w, spread, block_of, banks, s_src, s_pe, s_sch):
    W = WINDOWS + 1
    col = [S[0:W, 4, i:i + 1] for i in range(12)]
    cnt, start, end, first, last_, nb, t0, t1, bm, some = col[:10]
    ints = S[0:W, 5, 0:4].bitcast(I32)
    ps = banks[5]
    if part == 0:
        dve.wait_ge(s_src, 48)
        nc.vector.memset(k["edge_src"], 0.0)
        nc.vector.memset(k["edge_dst"], -1.0)
        nc.vector.memset(k["win"], 0)
        nc.vector.tensor_copy(nat_i.bitcast(FP32), nat_s.bitcast(I32)).then_inc(s_sch, 1)
    if part == 1:
        dve.wait_ge(s_pe, 1)
        link(nc.vector.tensor_copy(cnt, ps[0:W, 0:1]))
        dve.sem_inc(s_sch, 1)
    if part == 2:
        dve.wait_ge(s_pe, 2)
        link(nc.vector.tensor_copy(start, ps[0:W, 1:2]))
        link(nc.vector.tensor_tensor(end, start, cnt, ALU.add))
        link.add(nc.vector.tensor_copy(ints[:, 0:1], start))
        link(nc.vector.tensor_scalar(ints[:, 1:2], end, -1.0, None, ALU.add))
        link(nc.vector.tensor_single_scalar(ints[:, 2:4], ints[:, 0:2], PAIR.bit_length() - 1, ALU.arith_shift_right))
        link.add(nc.vector.tensor_copy(first, ints[:, 2:3]))
        link.add(nc.vector.tensor_copy(last_, ints[:, 3:4]))
        link(nc.vector.tensor_scalar(some, cnt, 0.0, None, ALU.is_gt))
        link(nc.vector.tensor_scalar(nb, last_, first, 1.0, ALU.subtract, ALU.add))
        link(nc.vector.tensor_tensor(nb, nb, some, ALU.mult))
        dve.sem_inc(s_sch, 1)
    if part == 3:
        dve.wait_ge(s_pe, 3)
        link(nc.vector.tensor_copy(t0, ps[0:W, 2:3]))
        link.add(nc.vector.tensor_tensor(t1, t0, nb, ALU.add))
        link(nc.vector.tensor_tensor(bm, first, t0, ALU.subtract))
        link.add(nc.vector.tensor_scalar(over_w[0:W, :], iota_t[0:W, :], t0, None, ALU.is_ge))
        link.add(nc.vector.tensor_scalar(spread[0:W, 0, :], k["ones"][0:W, :], bm, None, ALU.mult))
        link(nc.vector.tensor_scalar(spread[0:W, 1, :], k["ones"][0:W, :], k["pidx"][0:W, :], None, ALU.mult))
        link(nc.vector.scalar_tensor_tensor(over_w[0:W, :], iota_t[0:W, :], t1, over_w[0:W, :], ALU.is_lt, ALU.mult))
        dve.sem_inc(s_sch, 1)
    if part == 4:
        dve.wait_ge(s_pe, 4)
        link.add(nc.vector.tensor_tensor(block_of, ps[:, 0:T], iota_t, ALU.add))
        link.add(nc.vector.tensor_copy(k["win"][:, 0:T], banks[6][:, 0:T]))
        link(nc.vector.tensor_scalar(over_w, banks[6][:, 0:T], float(P), None, ALU.mult))
        for g in range(BG):
            last = nc.vector.tensor_scalar(onehot[:, g, :], block_of, float(-P * g), k["pidx"], ALU.add, ALU.is_equal)
        last.then_inc(s_sch, 1)
    if part == 5:
        for half in range(2):
            to = k["edge_src"].rearrange("p (t h) -> p h t", h=2)[:, half, 0:T]
            dve.wait_ge(s_pe, 5 + half)
            nc.vector.tensor_copy(to, banks[5 + half][:, 0:T])
        for half in range(2):
            to = k["edge_dst"].rearrange("p (t h) -> p h t", h=2)[:, half, 0:T]
            dve.wait_ge(s_pe, 7 + half)
            nc.vector.tensor_tensor(to, banks[(7, 4)[half]][:, 0:T], over_w, ALU.subtract)


def schedule_tensor(part, nc, pe, k, S, nat_i, nat_d, onehot, over_w, spread, banks, s_pe, s_sch):
    W = WINDOWS + 1
    nat_f = nat_i.bitcast(FP32)
    ps = banks[5]
    if part == 1:
        pe.wait_ge(s_sch, 1)
        nc.tensor.matmul(ps[0:W, 0:1], S[:, 3, 0:W], k["ones"][:, 0:1], start=True, stop=True).then_inc(s_pe, 1)
    if part == 2:
        pe.wait_ge(s_sch, 2)
        nc.tensor.matmul(ps[0:W, 1:2], k["tri"][0:W, 0:W], S[0:W, 4, 0:1], start=True, stop=True).then_inc(s_pe, 1)
    if part == 3:
        pe.wait_ge(s_sch, 3)
        nc.tensor.matmul(ps[0:W, 2:3], k["tri"][0:W, 0:W], S[0:W, 4, 5:6], start=True, stop=True).then_inc(s_pe, 1)
    if part == 4:
        pe.wait_ge(s_sch, 4)
        nc.tensor.matmul(ps[:, 0:T], spread[0:W, 0, :], over_w[0:W, :], start=True, stop=True)
        nc.tensor.matmul(banks[6][:, 0:T], spread[0:W, 1, :], over_w[0:W, :], start=True, stop=True).then_inc(s_pe, 1)
    if part == 5:
        pe.wait_ge(s_sch, 5)
        for table, first in ((nat_f, (5, 6)), (nat_d, (7, 4))):
            for half in range(2):
                for g in range(BG):
                    last = nc.tensor.matmul(banks[first[half]][:, 0:T], table[:, g, half * P:(half + 1) * P], onehot[:, g, :], start=g == 0, stop=g == BG - 1)
                last.then_inc(s_pe, 1)


def route(nc, sem, d, k, X, keep, banks, rw):
    V = 5
    g = [keep.take(D) for _ in range(V)]
    xm = [keep.take(D) for _ in range(V)]
    x2 = [keep.take(D) for _ in range(2)]
    xT = [keep.take(C, P) for _ in range(2)]
    lg = [keep.take(NX) for _ in range(2)]
    v8 = [keep.take(NX) for _ in range(2)]
    ix = [keep.take(NX, dt=U32) for _ in range(2)]
    ixf = [keep.take(NX) for _ in range(2)]
    S = k["small"]
    psT, psL = banks[0:2], banks[2:4]
    s_w = sem("router_loaded")
    s_xm = [sem(f"xm_loaded{v}") for v in range(V)]
    s_g, s_x1, s_st, s_x1st = sem("gcn_ready"), sem("x1_made"), sem("stats_made"), sem("x1_stored")
    s_var, s_sq, s_ln = sem("variances"), sem("std_done"), sem("ln_ready")
    s_x2, s_T, s_xT, s_L, s_lg = (sem(n) for n in ("x2_made", "x2_transposed", "xT_copied", "logits_made", "logits_kept"))
    s_norm, s_gate, s_e = sem("x_normed"), sem("gate_gaps"), sem("gate_exps")
    s_c, s_ac, s_vc, s_vo = sem("vector_chain"), sem("act_ordered"), sem("choice_chain"), sem("vector_ordered")

    with nc.Block() as block:
        @block.sync
        def _(sp):
            for v in range(V):
                sp.dma_start(xm[v], d["xm"][v * P:(v + 1) * P, :]).then_inc(s_xm[v], 16)
            sp.dma_start(k["wr"], rw.rearrange("(c p) e -> p c e", p=P)).then_inc(s_w, 16)

            def store(t):
                sp.dma_start(d["x1"][bass.ds(t * P, P), :], tile_of(X, t)).then_inc(s_x1st, 16)

            with sp.Fori(0, NT // V - 1) as i:
                for v in range(V):
                    sp.wait_ge(s_x1, V * i + v + 1)
                    store(V * i + v)
                    sp.dma_start(xm[v], d["xm"][bass.ds((V * i + V + v) * P, P), :]).then_inc(s_xm[v], 16)
            for v in range(V):
                sp.wait_ge(s_x1, NT - V + v + 1)
                store(NT - V + v)
            sp.wait_ge(s_x1st, 16 * NT)

        @block.scalar
        def _(act):
            with act.Fori(0, NT // V) as i:
                for v in range(V):
                    t = V * i + v
                    act.wait_ge(s_st, t + 1)
                    act.sem_inc(s_ac, 1)
                    nc.scalar.activation(g[v], tile_of(X, t), ACT.Relu, scale=k["dinv"][:, bass.ds(t, 1)]).then_inc(s_g, 1)
            act.wait_ge(s_var, 1)
            nc.scalar.activation(S[:, 0, :], S[:, 1, :], ACT.Sqrt, bias=k["eps"]).then_inc(s_sq, 1)
            act.wait_ge(s_ln, 1)
            with act.Fori(0, NT // 2) as i:
                for u in range(2):
                    t = 2 * i + u
                    act.wait_ge(s_T, t + 1)
                    act.sem_inc(s_ac, 1)
                    nc.scalar.activation(x2[u], tile_of(X, t), ACT.Identity, bias=k["nmr"][:, bass.ds(t, 1)], scale=k["rstd"][:, bass.ds(t, 1)]).then_inc(s_x2, 1)
                for u in range(2):
                    t = 2 * i + u
                    act.wait_ge(s_T, t + 3)
                    act.wait_ge(s_L, t + 1)
                    nc.scalar.copy(flat(xT[u]), psT[u][:, :]).then_inc(s_xT, 1)
            act.wait_ge(s_gate, 1)
            nc.scalar.activation(k["gate"][:, 1, :], k["gate"][:, 0, :], ACT.Exp).then_inc(s_e, 1)

        @block.vector
        def _(dve):
            link = Chain(dve, s_c)
            dve.sem_inc(s_st, V)
            with dve.Fori(0, NT // V) as i:
                for v in range(V):
                    t = V * i + v
                    dve.wait_ge(s_g, t + 1)
                    dve.wait_ge(s_xm[v], 16 * i + 16)
                    nc.vector.tensor_tensor(tile_of(X, t), g[v], xm[v], ALU.add).then_inc(s_x1, 1)
                    dve.wait_ge(s_x1, t + 1)
                    dve.sem_inc(s_vo, 1)
                    nc.vector.bn_stats(k["stats"][:, bass.ds(t, 1), :].rearrange("p a s -> p (a s)"), tile_of(X, t)).then_inc(s_st, 1)
            dve.wait_ge(s_st, NT + V)
            ln_stats(nc, link, k, S)
            dve.sem_inc(s_var, 1)
            dve.wait_ge(s_sq, 1)
            ln_scales(nc, link, k, S)
            dve.sem_inc(s_ln, 1)
            dve.wait_ge(s_x1st, 16 * NT)
            per = 7
            with dve.Fori(0, NT // 2) as i:
                for u in range(2):
                    t = 2 * i + u
                    dve.wait_ge(s_x2, t + 1)
                    nc.vector.tensor_scalar(tile_of(X, t), tile_of(X, t), k["rstd"][:, bass.ds(t, 1)], k["nmr"][:, bass.ds(t, 1)], ALU.mult, ALU.add).then_inc(s_norm, 1)
                chain = [0]

                def then(ins):
                    ins.then_inc(s_vc, 1)
                    chain[0] += 1

                def settle():
                    dve.wait_ge(s_vc, 2 * per * i + chain[0])

                for u in range(2):
                    dve.wait_ge(s_L, 2 * i + u + 3)
                    then(nc.vector.tensor_copy(lg[u], psL[u][:, 0:NX]))
                settle()
                for u in range(2):
                    dve.sem_inc(s_lg, 1)
                    then(nc.vector.max(v8[u], lg[u]))
                settle()
                for u in range(2):
                    dve.sem_inc(s_vo, 1)
                    then(nc.vector.max_index(ix[u], v8[u], lg[u]))
                settle()
                for u in range(2):
                    then(nc.vector.tensor_copy(ixf[u], ix[u]))
                settle()
                for u in range(2):
                    t = 2 * i + u
                    for m, M in enumerate((k["M1"], k["M2"])):
                        then(nc.vector.tensor_scalar(M[:, bass.ds(t, 1), :].rearrange("p a e -> p (a e)"), k["iota"][:, 0:NX], ixf[u][:, m:m + 1],
                                                     k["rowmask"][:, bass.ds(t, 1)], ALU.is_equal, ALU.mult))
                    then(nc.vector.tensor_copy(k["v12"][:, bass.ds(t, 1), :].rearrange("p a e -> p (a e)"), v8[u][:, 0:2]))
                settle()
            link(nc.vector.tensor_tensor(k["gate"][:, 0, :], k["v12"][:, :, 1], k["v12"][:, :, 0], ALU.subtract))
            dve.sem_inc(s_gate, 1)
            dve.wait_ge(s_e, 1)
            link(nc.vector.tensor_scalar(S[:, 3, :], k["gate"][:, 1, :], 1.0, None, ALU.add))
            link(nc.vector.reciprocal(k["gate"][:, 0, :], S[:, 3, :]))
            link(nc.vector.tensor_tensor(k["gate"][:, 1, :], k["gate"][:, 1, :], k["gate"][:, 0, :], ALU.mult))
            dve.wait_ge(s_norm, NT)

        @block.tensor
        def _(pe):
            pe.sem_inc(s_T, 2)
            pe.sem_inc(s_L, 2)
            pe.sem_inc(s_lg, 2)
            pe.wait_ge(s_w, 16)
            with pe.Fori(0, NT // 2) as i:
                for u in range(2):
                    pe.wait_ge(s_x2, 2 * i + u + 1)
                    for c in range(C):
                        last = nc.tensor.transpose(psT[u][:, c * P:(c + 1) * P], x2[u][:, c * P:(c + 1) * P], k["ident"])
                    last.then_inc(s_T, 1)
                for u in range(2):
                    pe.wait_ge(s_xT, 2 * i + u + 1)
                    pe.wait_ge(s_lg, 2 * i + u + 1)
                    for c in range(C):
                        last = nc.tensor.matmul(psL[u][:, 0:NX], xT[u][:, c, :], k["wr"][:, c, :], start=c == 0, stop=c == C - 1)
                    last.then_inc(s_L, 1)


def dispatch(nc, sem, d, k, X, keep, banks):
    both = keep.take(NT, NX)
    incl = keep.take(NT, NX)
    pos = keep.take(NT, NX)
    pick = keep.take(2, NT, NX)
    slot = keep.take(2, NT)
    zeros = keep.take(NT)
    cnt, nb, binc, bexc, base = (keep.take(NX) for _ in range(5))
    ni = keep.take(2, NX, dt=I32)
    iota_i = keep.take(P, dt=I32)
    ex = keep.take(MB)
    zero = keep.take(D)
    ends = keep.take(NX)
    ends_i = keep.take(NX, dt=I32)
    full = 2 * N // P
    s_c, s_both, s_ps, s_pos, s_out = sem("vector_chain"), sem("choices_ready"), sem("ranks_made"), sem("slots_ready"), sem("rows_sent")
    s_ends, s_zst = sem("last_blocks_known"), sem("spare_slots_zeroed")

    with nc.Block() as block:
        @block.sync
        def _(sp):
            sp.wait_ge(s_ends, 1)
            sp.dma_start(d["xs"][full * P:MB * P, :].rearrange("(b p) n -> p b n", p=P), zero.unsqueeze(1).to_broadcast([P, MB - full, D])).then_inc(s_zst, 16)
            sp.wait_ge(s_zst, 16)
            sp.wait_ge(s_ends, 2)
            for e in range(NX):
                b = sp.value_load(ends_i[0:1, e:e + 1], min_val=0, max_val=MB - 1)
                sp.dma_start(d["xs"][bass.ds(b * P, P), :], zero).then_inc(s_zst, 16)

        @block.vector
        def _(dve):
            link = Chain(dve, s_c)
            nc.vector.memset(zeros, 0.0)
            nc.vector.memset(zero, 0.0).then_inc(s_ends, 1)
            link(nc.vector.tensor_tensor(flat(both), flat(k["M1"]), flat(k["M2"]), ALU.add))
            dve.sem_inc(s_both, 1)
            dve.wait_ge(s_ps, 1)
            rank = banks[0][:, 0:NT * NX].rearrange("p (t e) -> p t e", e=NX)
            total = banks[1][:, 0:NT * NX].rearrange("p (t e) -> p t e", e=NX)
            for e in range(NX):
                link.add(nc.vector.tensor_tensor_scan(incl[:, :, e], total[:, :, e], zeros, 0.0, ALU.add, ALU.add))
            link.wait()
            link.add(nc.vector.tensor_tensor(pos, incl, rank, ALU.add))
            link(nc.vector.tensor_scalar(ni[:, 0, :], incl[:, NT - 1, :], float(P - 1), None, ALU.add))
            link.add(nc.vector.tensor_tensor(pos, pos, total, ALU.subtract))
            link(nc.vector.tensor_single_scalar(ni[:, 1, :], ni[:, 0, :], P.bit_length() - 1, ALU.arith_shift_right))
            link(nc.vector.tensor_copy(nb, ni[:, 1, :]))
            link(nc.vector.tensor_tensor_scan(binc, nb, zeros[:, 0:NX], 0.0, ALU.add, ALU.add))
            link(nc.vector.tensor_scalar(ends, binc, -1.0, 0.0, ALU.add, ALU.max))
            link(nc.vector.tensor_copy(ends_i, ends))
            dve.sem_inc(s_ends, 1)
            link(nc.vector.tensor_tensor(bexc, binc, nb, ALU.subtract))
            link(nc.vector.tensor_scalar(base, bexc, float(P), None, ALU.mult))
            link(nc.vector.tensor_tensor(pos, pos, base.unsqueeze(1).to_broadcast([P, NT, NX]), ALU.add))
            for m, M in enumerate((k["M1"], k["M2"])):
                link(nc.vector.tensor_tensor(pick[:, m], M, pos, ALU.mult))
                link(nc.vector.tensor_reduce(slot[:, m, :], pick[:, m], mybir.AxisListType.X, ALU.add))
            link(nc.vector.tensor_copy(flat(k["pos"]), flat(slot)))
            dve.sem_inc(s_pos, 1)
            link(nc.vector.tensor_scalar(ex, k["iota"][:, 0:MB], bexc[:, 1:2], None, ALU.is_ge))
            for e in range(2, NX):
                link(nc.vector.scalar_tensor_tensor(ex, k["iota"][:, 0:MB], bexc[:, e:e + 1], ex, ALU.is_ge, ALU.add))
            link(nc.vector.tensor_copy(k["expert"], ex))

        @block.tensor
        def _(pe):
            pe.wait_ge(s_both, 1)
            nc.tensor.matmul(banks[0][:, 0:NT * NX], k["tri"], flat(both), start=True, stop=True)
            nc.tensor.matmul(banks[1][:, 0:NT * NX], k["ones"], flat(both), start=True, stop=True).then_inc(s_ps, 1)

        @block.gpsimd
        def _(pool):
            pool.wait_ge(s_pos, 1)
            pool.wait_ge(s_zst, 16 * (NX + 1))
            for t in range(REAL):
                rows = P if t < REAL - 1 else LAST
                for m in range(2):
                    pool.indirect_dma_start(d["xs"], bass.IndirectOffsetOnAxis(ap=k["pos"][0:rows, m, t:t + 1], axis=0), X[0:rows, t, :], None).then_inc(s_out, 16)
            pool.wait_ge(s_out, 32 * REAL)


def experts(nc, sem, d, k, X, keep, banks, w1, b1, w2, b2, gamma, beta):
    W1 = keep.take(NX * C, F)
    W2 = keep.take(NX * FC, D)
    m = Mem(X.rearrange("p t n -> p (t n)"), NT * D)
    b1b, b2b, gab, beb = m.take(NX, F), m.take(NX, D), m.take(NX, D), m.take(NX, D)
    xs = [m.take(D) for _ in range(4)]
    xb = [m.take(D) for _ in range(4)]
    xsT, hb, hT, r, n, g, y = ([m.take(w) for _ in range(2)] for w in (D, F, F, D, D, D, D))
    st, mv, sd, rs, nm = ([m.take(w) for _ in range(2)] for w in (6, 2, 1, 1, 1))
    psX, psH, psG, psY = banks[0:2], banks[2:4], banks[4:6], banks[6:8]
    s_w1, s_w2, s_bb = sem("w1_loaded"), sem("w2_loaded"), sem("biases_loaded")
    s_xs = [sem(f"rows_loaded{u}") for u in range(4)]
    s_yst = [sem(f"y_stored{u}") for u in range(2)]
    s_T, s_xT, s_H, s_hb, s_G, s_hT, s_Y = (sem(n) for n in ("x_transposed", "xT_copied", "h_made", "h_biased", "h_transposed", "hT_copied", "y_made"))
    s_xb, s_r, s_v, s_sd, s_y, s_pc = (sem(n) for n in ("x_biased", "r_made", "var_made", "std_made", "y_ready", "pool_ordered"))
    s_st, s_rs, s_nm, s_n, s_g, s_vo = (sem(n) for n in ("stats_made", "rstd_made", "mean_scaled", "normed", "gamma_applied", "vector_ordered"))

    def pipeline(eng, turn, ahead, behind):
        lo, hi = 4 * -(-behind // 4), (MB - ahead) // 4 * 4
        for b in range(-ahead, lo):
            turn(b, b // 4, b % 4)
        with eng.Fori(lo // 4, hi // 4) as i:
            for u in range(4):
                turn(4 * i + u, i, u, middle=True)
        for b in range(hi, MB + behind):
            turn(b, b // 4, b % 4)

    def inside(b, middle):
        return middle or 0 <= b < MB

    with nc.Block() as block:
        @block.sync
        def _(sp):
            sp.dma_start(flat(b1b), b1.rearrange("(o e) n -> o (e n)", o=1).broadcast_to([P, NX * F])).then_inc(s_bb, 16)
            for to, a in ((b2b, b2), (gab, gamma), (beb, beta)):
                sp.dma_start(flat(to), a.rearrange("(o e) n -> o (e n)", o=1).broadcast_to([P, NX * D])).then_inc(s_bb, 16)
            sp.dma_start(W1, w1.rearrange("e (c p) f -> p (e c) f", p=P)).then_inc(s_w1, 16)
            sp.dma_start(W2, w2.rearrange("e (c p) n -> p (e c) n", p=P)).then_inc(s_w2, 16)

            def turn(b, i, u, middle=False):
                if inside(b + 4, middle):
                    rows = d["xs"][bass.ds((b + 4) * P, P), :]
                    if middle or b >= 0:
                        sp.wait_ge(s_T, b + 3)
                        sp.wait_ge(s_xb, b + 3)
                    sp.dma_start(xs[u], rows).then_inc(s_xs[u], 16)
                if inside(b - 3, middle):
                    rows = d["ys"][bass.ds((b - 3) * P, P), :]
                    sp.wait_ge(s_y, b - 2)
                    sp.dma_start(rows, y[(u + 1) % 2]).then_inc(s_yst[(u + 1) % 2], 16)

            pipeline(sp, turn, 4, 3)
            for v in range(2):
                sp.wait_ge(s_yst[v], 16 * (MB // 2) + 16)

        @block.gpsimd
        def _(pool):
            def turn(b, i, u, middle=False):
                v = u % 2
                if inside(b + 1, middle):
                    e = pool.value_load(k["expert"][0:1, bass.ds(b + 1, 1)], min_val=0, max_val=NX - 1)
                    w = (u + 1) % 4
                    pool.wait_ge(s_xs[w], 16 * (i + (u + 1) // 4) + 16)
                    if middle or b > 2:
                        pool.wait_ge(s_r, b - 2)
                    pool.sem_inc(s_pc, 1)
                    nc.gpsimd.tensor_tensor(xb[w], xs[w], tile_of(b2b, e), ALU.add).then_inc(s_xb, 1)
                if inside(b - 2, middle):
                    e = pool.value_load(k["expert"][0:1, bass.ds(b - 2, 1)], min_val=0, max_val=NX - 1)
                    pool.wait_ge(s_n, b + 1)
                    pool.sem_inc(s_pc, 1)
                    nc.gpsimd.tensor_tensor(g[v], n[v], tile_of(gab, e), ALU.mult).then_inc(s_g, 1)
                    pool.wait_ge(s_g, b + 1)
                    pool.wait_ge(s_yst[v], 16 * (2 * i + (u - 2) // 2) + 16)
                    pool.sem_inc(s_pc, 1)
                    nc.gpsimd.tensor_tensor(y[v], g[v], tile_of(beb, e), ALU.add).then_inc(s_y, 1)

            pool.sem_inc(s_xb, 2)
            pool.wait_ge(s_bb, 64)
            pipeline(pool, turn, 1, 2)

        @block.scalar
        def _(act):
            def turn(b, i, u, middle=False):
                v = u % 2
                if inside(b + 2, middle):
                    act.wait_ge(s_T, b + 5)
                    act.wait_ge(s_H, b + 3)
                    nc.scalar.copy(xsT[v], psX[v][:, :]).then_inc(s_xT, 1)
                if inside(b - 2, middle):
                    act.wait_ge(s_v, b - 1)
                    nc.scalar.activation(sd[v], mv[v][:, 1:2], ACT.Sqrt, bias=k["epsm"]).then_inc(s_sd, 1)
                    act.wait_ge(s_nm, b - 1)
                    act.wait_ge(s_g, b - 1)
                    nc.scalar.activation(n[v], r[v], ACT.Identity, bias=nm[v], scale=rs[v]).then_inc(s_n, 1)
                if inside(b, middle):
                    act.wait_ge(s_G, b + 3)
                    act.wait_ge(s_Y, b + 1)
                    nc.scalar.activation(hT[v], psG[v][:, 0:F], ACT.Relu).then_inc(s_hT, 1)

            pipeline(act, turn, 2, 2)

        @block.vector
        def _(dve):
            def turn(b, i, u, middle=False):
                v, w = u % 2, (u + 1) % 2
                if inside(b - 2, middle):
                    dve.wait_ge(s_Y, b + 1)
                    dve.wait_ge(s_xb, b + 1)
                    dve.wait_ge(s_n, b - 1)
                    nc.vector.tensor_tensor(r[v], psY[v][:, :], xb[(u + 2) % 4], ALU.add).then_inc(s_r, 1)
                    dve.wait_ge(s_r, b + 1)
                    nc.vector.bn_stats(st[v], r[v]).then_inc(s_st, 1)
                    dve.wait_ge(s_st, b - 1)
                    dve.sem_inc(s_vo, 1)
                    nc.vector.bn_aggr(mv[v], st[v]).then_inc(s_v, 1)
                    dve.wait_ge(s_sd, b - 1)
                    nc.vector.reciprocal(rs[v], sd[v]).then_inc(s_rs, 1)
                    dve.wait_ge(s_rs, b - 1)
                    nc.vector.scalar_tensor_tensor(nm[v], mv[v][:, 0:1], -1.0, rs[v], ALU.mult, ALU.mult).then_inc(s_nm, 1)
                if inside(b + 1, middle):
                    e = dve.value_load(k["expert"][0:1, bass.ds(b + 1, 1)], min_val=0, max_val=NX - 1)
                    dve.wait_ge(s_H, b + 4)
                    dve.wait_ge(s_G, b + 2)
                    nc.vector.tensor_tensor(hb[w], psH[w][:, 0:F], tile_of(b1b, e), ALU.add).then_inc(s_hb, 1)

            dve.sem_inc(s_r, 2)
            dve.wait_ge(s_bb, 64)
            pipeline(dve, turn, 1, 2)

        @block.tensor
        def _(pe):
            def turn(b, i, u, middle=False):
                v, w = u % 2, (u + 1) % 2
                if inside(b + 2, middle):
                    j = (u + 2) % 4
                    pe.wait_ge(s_xs[j], 16 * (i + (u + 2) // 4) + 16)
                    pe.wait_ge(s_xT, b + 3)
                    for c in range(C):
                        last = nc.tensor.transpose(psX[v][:, c * P:(c + 1) * P], xs[j][:, c * P:(c + 1) * P], k["ident"])
                    last.then_inc(s_T, 1)
                if inside(b + 1, middle):
                    e = pe.value_load(k["expert"][0:1, bass.ds(b + 1, 1)], min_val=0, max_val=NX - 1)
                    pe.wait_ge(s_xT, b + 4)
                    pe.wait_ge(s_hb, b + 2)
                    for c in range(C):
                        last = nc.tensor.matmul(psH[w][:, 0:F], xsT[w][:, c * P:(c + 1) * P], tile_of(W1, e * C + c), start=c == 0, stop=c == C - 1)
                    last.then_inc(s_H, 1)
                if inside(b, middle):
                    pe.wait_ge(s_hb, b + 3)
                    pe.wait_ge(s_hT, b + 1)
                    for c in range(FC):
                        last = nc.tensor.transpose(psG[v][:, c * P:(c + 1) * P], hb[v][:, c * P:(c + 1) * P], k["ident"])
                    last.then_inc(s_G, 1)
                if inside(b - 1, middle):
                    e = pe.value_load(k["expert"][0:1, bass.ds(b - 1, 1)], min_val=0, max_val=NX - 1)
                    pe.wait_ge(s_hT, b + 2)
                    pe.wait_ge(s_r, b)
                    for c in range(FC):
                        last = nc.tensor.matmul(psY[w][:, :], hT[w][:, c * P:(c + 1) * P], tile_of(W2, e * FC + c), start=c == 0, stop=c == FC - 1)
                    last.then_inc(s_Y, 1)

            for s in (s_T, s_xT, s_H, s_hb, s_G, s_hT, s_Y, s_g, s_n):
                pe.sem_inc(s, 2)
            for u in range(2):
                pe.sem_inc(s_yst[u], 16)
            pe.wait_ge(s_w1, 16)
            pe.wait_ge(s_w2, 16)
            pipeline(pe, turn, 2, 1)


def combine(nc, sem, d, k, X, keep, out):
    R = 4
    m = Mem(X.rearrange("p t n -> p (t n)"), NT * D)
    x1, y1, y2, o1, o = ([m.take(D) for _ in range(R)] for _ in range(5))
    s_x1, s_y1, s_y2, s_st = ([sem(f"{n}{r}") for r in range(R)] for n in ("x1_loaded", "y1_gathered", "y2_gathered", "out_stored"))
    s_o1, s_o = sem("first_added"), sem("out_made")
    turns = (REAL - 1) // R
    assert turns * R == REAL - 1

    with nc.Block() as block:
        @block.sync
        def _(sp):
            for r in range(R):
                sp.dma_start(x1[r], d["x1"][r * P:(r + 1) * P, :]).then_inc(s_x1[r], 16)
            def store(t, r):
                sp.wait_ge(s_o, t + 1)
                sp.dma_start(out[bass.ds(t * P, P), :], o[r]).then_inc(s_st[r], 16)

            with sp.Fori(0, turns - 1) as i:
                for r in range(R):
                    store(R * i + r, r)
                    sp.dma_start(x1[r], d["x1"][bass.ds((R * i + R + r) * P, P), :]).then_inc(s_x1[r], 16)
            for r in range(R):
                store(R * (turns - 1) + r, r)
                if r == 0:
                    sp.dma_start(x1[0], d["x1"][R * turns * P:(R * turns + 1) * P, :]).then_inc(s_x1[0], 16)
            sp.wait_ge(s_o, REAL)
            a = (REAL - 1) * P
            sp.dma_start(out[a:a + 96, :], o[0][0:96, :]).then_inc(s_st[0], 16)
            sp.dma_start(out[a + 96:N, :], o[0][96:LAST, :]).then_inc(s_st[0], 16)
            for r in range(R):
                sp.wait_ge(s_st[r], 16 * turns + 16 + (32 if r == 0 else 0))

        @block.gpsimd
        def _(pool):
            for t in range(REAL):
                r = t % R
                if t >= R:
                    pool.wait_ge(s_o, t - R + 1)
                rows = P if t < REAL - 1 else LAST
                for j, (y, s) in enumerate(((y1, s_y1), (y2, s_y2))):
                    pool.indirect_dma_start(y[r][0:rows, :], None, d["ys"], bass.IndirectOffsetOnAxis(ap=k["pos"][0:rows, j, t:t + 1], axis=0)).then_inc(s[r], 16)

        @block.vector
        def _(dve):
            def tile(t, i, r, rows):
                dve.wait_ge(s_x1[r], 16 * i + 16)
                dve.wait_ge(s_y1[r], 16 * i + 16)
                nc.vector.scalar_tensor_tensor(o1[r][0:rows, :], y1[r][0:rows, :], k["gate"][0:rows, 0, bass.ds(t, 1)], x1[r][0:rows, :], ALU.mult, ALU.add).then_inc(s_o1, 1)
                dve.wait_ge(s_y2[r], 16 * i + 16)
                dve.wait_ge(s_o1, t + 1)
                dve.wait_ge(s_st[r], 16 * i + 16)
                nc.vector.scalar_tensor_tensor(o[r][0:rows, :], y2[r][0:rows, :], k["gate"][0:rows, 1, bass.ds(t, 1)], o1[r][0:rows, :], ALU.mult, ALU.add).then_inc(s_o, 1)

            for r in range(R):
                dve.sem_inc(s_st[r], 16)
            with dve.Fori(0, turns) as i:
                for r in range(R):
                    tile(R * i + r, i, r, P)
            tile(REAL - 1, turns, 0, LAST)


_INS = ["x", "src", "dst", "L0_gnn_W", "L0_gnn_b", "L0_mix_w_qkv", "L0_mix_w_out", "L0_mix_b_out", "L0_ffn_router_w",
        "L0_ffn_w1", "L0_ffn_b1", "L0_ffn_w2", "L0_ffn_b2", "L0_ffn_gamma", "L0_ffn_beta"]


def kernel(**inputs):
    import concourse.bacc as bacc
    import numpy as np
    from concourse.bass_utils import run_bass_kernel_spmd

    nc = bacc.Bacc("TRN2", target_bir_lowering=False, num_devices=1)
    arrays, args = {}, []
    for name in _INS:
        a = np.ascontiguousarray(inputs[name])
        arrays[f"in_{name}"] = a
        args.append(nc.dram_tensor(f"in_{name}", a.shape, mybir.dt.from_np(a.dtype), kind="ExternalInput").ap())
    args.append(nc.dram_tensor("out_x", (N, D), FP32, kind="ExternalOutput").ap())
    build(nc, *args)
    r = run_bass_kernel_spmd(nc, [arrays], core_ids=[0])
    return r.results[0]["out_x"]
```

```python
from contextlib import ExitStack

import concourse.bass as bass
from concourse import mybir

FP32 = mybir.dt.float32
FP32R = mybir.dt.float32r
BF16 = mybir.dt.bfloat16
I32 = mybir.dt.int32
U32 = mybir.dt.uint32
ALU = mybir.AluOpType
ACT = mybir.ActivationFunctionType

P = 128
N = 6250
D = 512
E = 100000
C = D // P
HEAD = 64
HEADS = D // HEAD
NX = 8
F = 256
FC = F // P
EPS_LN = 1e-5
EPS_MOE = 1e-6
EPS_Z = 1e-6

NT = 50
REAL = -(-N // P)
LAST = N - (REAL - 1) * P
WINDOWS = REAL
PAIR = 2 * P
BLOCKS = -(-E // PAIR)
BG = -(-BLOCKS // P)
STEPS = 8
TURNS = -(-(BLOCKS + WINDOWS - 1) // STEPS)
T = TURNS * STEPS
SLOTS = 2 * STEPS
SPLIT = (0, 1, 3, 4, 5, 7)
TILE_SPLIT = len(SPLIT) // 2
MB = 106
ROWS = NT * P


class Mem:

    def __init__(self, tensor, size, dt=FP32):
        self.t, self.size, self.dt, self.at = tensor, size, dt, 0

    def take(self, *shape, dt=None):
        dt = dt or self.dt
        n = 1
        for s in shape:
            n *= s
        words = -(-n // 2) if dt == BF16 else n
        words = -(-words // 8) * 8
        assert self.at + words <= self.size, (self.at, words, self.size)
        v = self.t[:, self.at:self.at + words]
        self.at += words
        if dt != self.dt:
            v = v.bitcast(dt)
        v = v[:, 0:n]
        if len(shape) == 2:
            v = v.rearrange("p (a b) -> p a b", b=shape[1])
        elif len(shape) == 3:
            v = v.rearrange("p (a b c) -> p a b c", b=shape[1], c=shape[2])
        return v


class Chain:

    def __init__(self, eng, sem):
        self.eng, self.sem, self.n = eng, sem, 0

    def __call__(self, ins):
        self.add(ins)
        self.wait()

    def add(self, ins):
        ins.then_inc(self.sem, 1)
        self.n = self.n + 1

    def wait(self):
        self.eng.wait_ge(self.sem, self.n)


def tile_of(x, t):
    return x[:, bass.ds(t, 1), :].rearrange("p a n -> p (a n)")


def flat(v):
    return v.rearrange("p a b -> p (a b)")


def build(nc, x, src, dst, gW, gb, wqkv, wout, bout, rw, w1, b1, w2, b2, gamma, beta, out):
    with ExitStack() as ctx:
        uid = [0]

        retired = []

        def stage(run, words, *args):
            own = []

            def sem(name):
                uid[0] += 1
                own.append(nc.alloc_semaphore(name=f"{name}_{uid[0]}"))
                return own[-1]

            uid[0] += 1
            with nc.sbuf_tensor(f"scratch_{uid[0]}", [P, words], FP32) as scratch:
                run(nc, sem, d, k, X, Mem(scratch, words), *args)
            for s in retired:
                nc.release_semaphore(s)
            retired[:] = own
            if run is not combine:
                for s in own:
                    nc.gpsimd.sem_clear(s)

        def dram(name, shape, dt=FP32):
            return nc.dram_tensor(name, shape, dt, kind="Internal").ap()

        d = dict(
            xnT=dram("xnT_scratch", (NT, P, D)),
            xb=dram("xb_scratch", (ROWS, D)),
            h=dram("h_scratch", (ROWS, D)),
            xm=dram("xm_scratch", (ROWS, D)),
            x1=dram("x1_scratch", (ROWS, D)),
            x2=dram("x2_scratch", (ROWS, D)),
            ys=dram("ys_scratch", (MB * P, D)),
        )
        big = ctx.enter_context(nc.sbuf_tensor("big", [P, NT * D], FP32))
        X = big[:, :].rearrange("p (t n) -> p t n", n=D)
        KEPT, LATE = 3112, 1376
        keep = Mem(ctx.enter_context(nc.sbuf_tensor("kept", [P, KEPT], FP32)), KEPT)
        k = dict(
            ident=keep.take(P), tri=keep.take(P), ones=keep.take(P), bd=keep.take(P), iota=keep.take(P),
            pidx=keep.take(1), eps=keep.take(1), epsm=keep.take(1), epsz=keep.take(1),
            rowmask=keep.take(NT),
            covered=keep.take(1), fallback=keep.take(1, dt=I32),
            sdeg=keep.take(NT), dinv=keep.take(NT),
            win=keep.take(T + STEPS, dt=I32), edge_src=keep.take(2 * (T + STEPS)), edge_dst=keep.take(2 * (T + STEPS)),
        )
        banks = [ctx.enter_context(nc.psum_tensor(f"bank{i}", [P, 512], FP32)) for i in range(8)]
        stage(prepare, 24480, banks, x, src, dst, gW, bout)
        stage(mix, 11616, banks, wqkv, wout, gb)
        stage(unsorted, 16000, banks, src, dst, gb)
        late = Mem(ctx.enter_context(nc.sbuf_tensor("late", [P, LATE], FP32)), LATE)
        k.update(
            M1=late.take(NT, NX), M2=late.take(NT, NX), v12=late.take(2, NT),
            pos=late.take(2, NT, dt=I32), gate=late.take(2, NT),
            expert=late.take(MB, dt=I32), token=late.take(MB, dt=I32), wr=late.take(C, NX),
        )
        stage(route, 22400, banks, rw)
        late = Mem(ctx.enter_context(nc.sbuf_tensor("norms", [P, 2 * NX * D], FP32)), 2 * NX * D)
        m = Mem(big, NT * D)
        k.update(
            W1=m.take(NX * C, F), W2=m.take(NX * FC, D), b1T=m.take(NX, FC), b2b=m.take(NX, D),
            gab=late.take(NX, D), beb=late.take(NX, D),
        )
        stage(dispatch, 10000, banks, w1, b1, w2, b2, gamma, beta)
        stage(experts, 12000, banks)
        stage(combine, 8, out)


def norm_tables(k, keep):
    k.update(stats=keep.take(NT, 6), rstd=keep.take(NT), nmr=keep.take(NT), small=keep.take(8, NT))


def prepare(nc, sem, d, k, X, keep, banks, x, src, dst, gW, bout):
    norm_tables(k, keep)
    W = keep.take(C, D)
    boutb = keep.take(D)
    xn = [keep.take(D) for _ in range(2)]
    xT = [keep.take(C, P) for _ in range(2)]
    xb = [keep.take(D) for _ in range(2)]
    nat_i = keep.take(BG, PAIR, dt=I32)
    nat_s = keep.take(BG, PAIR)
    nat_d = keep.take(BG, PAIR)
    dT = keep.take(2, BG * P, dt=I32)
    dT2 = keep.take(2, BG * P, dt=I32)
    lo = keep.take(2, BG * P, dt=BF16)
    hi = keep.take(2, BG * P, dt=BF16)
    HB = 16
    onelo = [keep.take(P, HB, dt=BF16) for _ in range(2)]
    onehi = [keep.take(WINDOWS + 1, HB, dt=BF16) for _ in range(2)]
    iota_b = keep.take(P, HB, dt=BF16)
    iota_i = keep.take(T, dt=I32)
    iota_t = keep.take(T)
    zero = keep.take(D)
    onehot = keep.take(BG, T)
    spread = keep.take(2, P)
    block_of = keep.take(T)
    over_w = keep.take(T)
    S = k["small"]
    L = keep.take(5, NT)
    TURNS_X = NT // 2
    GRAPH = -(-BLOCKS // HB) // 2
    assert 2 * GRAPH + 1 >= -(-BLOCKS // HB) and 2 * GRAPH <= TURNS_X
    STOPS = (0, 4, 8, GRAPH, 14, 16, 18, 20, TURNS_X - 1)
    SCHEDULE = {14: 1, 16: 2, 18: 3, 20: 4}
    X_LOADS = (0, 10, 18, 26, 34, 42, REAL - 1)
    LOADS = len(X_LOADS) - 1
    NORM = {4: 1, 8: 2, GRAPH: 3, 16: 4, 20: 5}
    s_x = [sem(f"x_loaded{i}") for i in range(LOADS + 1)]
    s_xz, s_edges0, s_w = sem("x_pad_zeroed"), sem("edges_padded"), sem("weights_loaded")
    s_src, s_dst = sem("src_loaded"), sem("dst_loaded")
    s_iota, s_const = sem("iotas_made"), sem("constants_made")
    s_natd, s_dTp = sem("dst_converted"), sem("dst_transposed")
    s_var, s_sq, s_ln = sem("variances"), sem("std_done"), sem("ln_ready")
    s_xn, s_T, s_xT, s_h, s_hs = sem("xn_made"), sem("xn_transposed"), sem("xT_copied"), sem("h_made"), sem("h_kept")
    s_xb = sem("xb_made")
    s_xTst = [sem(f"xT_stored{u}") for u in range(2)]
    s_xbst = [sem(f"xb_stored{u}") for u in range(2)]
    s_lo, s_hist = sem("onehots_made"), sem("histogram_step")
    s_deg, s_sdeg, s_dinv = sem("degrees_done"), sem("sqrt_degree"), sem("dinv_made")
    s_sc, s_vo = sem("h_scaled"), sem("vector_ordered")
    s_hst, s_z = sem("h_stored"), sem("zero_row")
    s_c, s_pe, s_sch = sem("vector_chain"), sem("schedule_products"), sem("schedule_tables")
    s_pc, s_ac = sem("pool_ordered"), sem("act_ordered")
    psT, psH, psD = banks[0:2], banks[2:4], banks[4]
    s_bout = sem("b_out_loaded")
    full = (BLOCKS - 1) // P * P
    rest = (E // PAIR) - full
    tail = E - (E // PAIR) * PAIR

    def norm_tiles(n):
        return slice(X_LOADS[n], X_LOADS[n + 1] if n < LOADS - 1 else NT)

    def edges(eng, a, to, s):
        g = full // P
        eng.dma_start(to[:, 0:g, :], a[0:full * PAIR].rearrange("(g p j) -> p g j", p=P, j=PAIR)).then_inc(s, 16)
        eng.dma_start(to[0:rest, g, :], a[full * PAIR:(full + rest) * PAIR].rearrange("(p j) -> p j", j=PAIR)).then_inc(s, 16)
        eng.dma_start(to[rest:rest + 1, g, 0:tail], a[E - tail:E].rearrange("(p j) -> p j", p=1)).then_inc(s, 16)

    def rows(eng, i):
        a, b = X_LOADS[i], X_LOADS[i + 1]
        eng.dma_start(X[:, a:b, :], x[a * P:b * P, :].rearrange("(t p) n -> p t n", p=P)).then_inc(s_x[i], 16)

    with nc.Block() as block:
        @block.sync
        def _(sp):
            sp.wait_ge(s_edges0, 2)
            edges(sp, dst, nat_i, s_dst)
            rows(sp, 0)
            sp.dma_start(W, gW.rearrange("(c p) n -> p c n", p=P)).then_inc(s_w, 16)
            sp.dma_start(boutb, bout.rearrange("(a n) -> a n", a=1).broadcast_to([P, D])).then_inc(s_bout, 16)

            def stores(i):
                for u in range(2):
                    sp.wait_ge(s_xb, 2 * i + u + 1)
                    sp.dma_start(d["xb"][bass.ds((2 * i + u) * P, P), :], xb[u]).then_inc(s_xbst[u], 16)
                    sp.wait_ge(s_xT, 2 * i + u + 1)
                    sp.dma_start(d["xnT"][bass.ds(2 * i + u, 1), :, :].rearrange("a p n -> p (a n)"), flat(xT[u])).then_inc(s_xTst[u], 16)

            def store_h(i):
                sp.dma_start(d["h"][bass.ds(i * 2 * P, 2 * P), :].rearrange("(t p) n -> p t n", p=P), X[:, bass.ds(2 * i, 2), :]).then_inc(s_hst, 16)

            with sp.Fori(0, GRAPH + 1) as i:
                stores(i)
            with sp.Fori(GRAPH + 1, TURNS_X) as i:
                stores(i)
                sp.wait_ge(s_hs, 2 * i + 2)
                store_h(i - 1)
                sp.wait_ge(s_sc, 2 * i - 2 * GRAPH)
                store_h(i - GRAPH - 1)
            sp.wait_ge(s_hs, NT + 2)
            store_h(TURNS_X - 1)
            for u in range(2):
                sp.wait_ge(s_xTst[u], 16 * TURNS_X + 16)
                sp.wait_ge(s_xbst[u], 16 * TURNS_X + 16)
            sp.wait_ge(s_hst, 16 * TURNS_X)

        @block.gpsimd
        def _(pool):
            nc.gpsimd.iota(iota_i, [[1, T]], base=0, channel_multiplier=0).then_inc(s_iota, 1)
            nc.gpsimd.iota(dT[:, 0, 0:1], [[1, 1]], base=0, channel_multiplier=1).then_inc(s_iota, 1)
            pool.wait_ge(s_bout, 16)

            def biased(i):
                for u in range(2):
                    pool.wait_ge(s_xbst[u], 16 * i + 16)
                    pool.sem_inc(s_pc, 1)
                    nc.gpsimd.tensor_tensor(xb[u], tile_of(X, 2 * i + u), boutb, ALU.add).then_inc(s_xb, 1)

            for n in range(LOADS):
                pool.wait_ge(s_x[n], 16)
                with pool.Fori(X_LOADS[n] // 2, X_LOADS[n + 1] // 2) as i:
                    biased(i)
            pool.wait_ge(s_x[LOADS], 32)
            biased(TURNS_X - 1)

        @block.scalar
        def _(act):
            def std(n):
                act.wait_ge(s_var, n + 1)
                t = norm_tiles(n)
                nc.scalar.activation(L[:, 0, t], L[:, 1, t], ACT.Sqrt, bias=k["eps"]).then_inc(s_sq, 1)
                act.wait_ge(s_ln, n + 1)

            def pair(i):
                for u in range(2):
                    act.wait_ge(s_T, 2 * i + u + 1)
                    act.sem_inc(s_ac, 1)
                    nc.scalar.activation(xn[u], tile_of(X, 2 * i + u), ACT.Identity,
                                         bias=k["nmr"][:, bass.ds(2 * i + u, 1)], scale=k["rstd"][:, bass.ds(2 * i + u, 1)]).then_inc(s_xn, 1)
                for u in range(2):
                    act.wait_ge(s_T, 2 * i + u + 3)
                    act.wait_ge(s_h, 2 * i + u + 1)
                    act.wait_ge(s_xTst[u], 16 * i + 16)
                    nc.scalar.copy(flat(xT[u]), psT[u][:, :]).then_inc(s_xT, 1)

            def load(n):
                rows(act, n)
                if n == LOADS - 1:
                    act.wait_ge(s_xz, 1)
                    a = (REAL - 1) * P
                    act.dma_start(X[0:96, REAL - 1, :], x[a:a + 96, :]).then_inc(s_x[LOADS], 16)
                    act.dma_start(X[96:LAST, REAL - 1, :], x[a + 96:N, :]).then_inc(s_x[LOADS], 16)

            act.wait_ge(s_x[0], 16)
            load(1)
            load(2)
            std(0)
            pair(0)
            for a, b in zip(STOPS[:-1], STOPS[1:]):
                if a in NORM:
                    std(NORM[a])
                if a == GRAPH:
                    act.wait_ge(s_deg, 1)
                    nc.scalar.activation(k["sdeg"], S[:, 2, :], ACT.Sqrt).then_inc(s_sdeg, 1)
                    act.wait_ge(s_dinv, 1)
                    act.wait_ge(s_hs, 2 * GRAPH + 2)
                if a in (4, 8, GRAPH):
                    load({4: 3, 8: 4, GRAPH: 5}[a])
                if a == 4:
                    act.wait_ge(s_edges0, 2)
                    edges(act, src, nat_s.bitcast(I32), s_src)
                with act.Fori(a, b) as i:
                    pair(i + 1)
                    if a >= GRAPH:
                        for u in range(2):
                            t = tile_of(X, 2 * i + u - 2 * GRAPH)
                            nc.scalar.activation(t, t, ACT.Identity, scale=k["dinv"][:, bass.ds(2 * i + u - 2 * GRAPH, 1)]).then_inc(s_sc, 1)

        @block.vector
        def _(dve):
            link = Chain(dve, s_c)
            nc.vector.memset(nat_i, -1).then_inc(s_edges0, 1)
            nc.vector.memset(nat_s.bitcast(I32), 0).then_inc(s_edges0, 1)
            nc.vector.memset(X[:, REAL - 1:NT, :], 0.0).then_inc(s_xz, 1)
            nc.vector.memset(zero, 0.0).then_inc(s_z, 1)
            nc.vector.memset(k["bd"], 0.0)
            nc.vector.memset(k["ones"], 1.0)
            nc.vector.memset(k["eps"], EPS_LN)
            nc.vector.memset(k["epsm"], EPS_MOE)
            nc.vector.memset(k["epsz"], EPS_Z)
            link(nc.vector.memset(k["rowmask"], 1.0))
            nc.vector.memset(k["rowmask"][:, REAL:NT], 0.0)
            link(nc.vector.memset(k["bd"][0:HEAD, 0:HEAD], 1.0))
            link(nc.vector.memset(k["bd"][HEAD:P, HEAD:P], 1.0))
            dve.wait_ge(s_iota, 2)
            nc.vector.tensor_copy(k["iota"], iota_i[:, 0:P])
            nc.vector.tensor_copy(iota_t, iota_i)
            link(nc.vector.tensor_copy(k["pidx"], dT[:, 0, 0:1]))
            nc.vector.tensor_copy(iota_b, k["iota"].unsqueeze(2).to_broadcast([P, P, HB]))
            nc.vector.tensor_scalar(k["ident"], k["iota"], k["pidx"], None, ALU.is_equal)
            nc.vector.tensor_scalar(k["tri"], k["iota"], k["pidx"], None, ALU.is_gt)
            link(nc.vector.tensor_scalar(k["rowmask"][:, REAL - 1:REAL], k["pidx"], float(LAST), None, ALU.is_lt))
            dve.sem_inc(s_const, 1)
            dve.wait_ge(s_dst, 48)
            nc.vector.tensor_copy(flat(nat_d), flat(nat_i)).then_inc(s_natd, 1)
            dve.wait_ge(s_dTp, 1)
            for half in range(2):
                link.add(nc.vector.tensor_copy(dT[:, half, :], banks[5 + half][:, :]))
            link.wait()
            link(nc.vector.tensor_single_scalar(flat(dT2), flat(dT), P.bit_length() - 1, ALU.arith_shift_right))
            link(nc.vector.tensor_copy(flat(hi), flat(dT2)))
            link(nc.vector.tensor_single_scalar(flat(dT2), flat(dT), P - 1, ALU.bitwise_and))
            link(nc.vector.tensor_copy(flat(lo), flat(dT2)))
            def norm(n):
                t = norm_tiles(n)
                ln_stats(nc, link, k, L, t)
                dve.sem_inc(s_var, 1)
                dve.wait_ge(s_sq, n + 1)
                ln_scales(nc, link, k, L, t)
                dve.sem_inc(s_ln, 1)

            def onehots(n, r, u):
                dve.wait_ge(s_hist, n + 1)
                nc.vector.tensor_tensor(onelo[u], lo[:, u, bass.ds(r * HB, HB)].unsqueeze(1).to_broadcast([P, P, HB]), iota_b, ALU.is_equal)
                nc.vector.tensor_tensor(onehi[u], hi[:, u, bass.ds(r * HB, HB)].unsqueeze(1).to_broadcast([P, WINDOWS + 1, HB]),
                                        iota_b[:, 0:WINDOWS + 1, :], ALU.is_equal).then_inc(s_lo, 1)

            def keep_h(t, u, scaled):
                dve.wait_ge(s_h, t + 3)
                dve.wait_ge(s_xb, t + 1)
                nc.vector.tensor_scalar(tile_of(X, t), psH[u][:, :], k["dinv"][:, bass.ds(t, 1)] if scaled else 1.0, None, ALU.mult).then_inc(s_hs, 1)

            dve.wait_ge(s_x[0], 16)
            for t in range(X_LOADS[1]):
                last = nc.vector.bn_stats(k["stats"][:, t, :], X[:, t, :])
            link(last)
            norm(0)
            for half in range(2):
                onehots(half, 0, half)
            for a, b in zip(STOPS[:-1], STOPS[1:]):
                if a in NORM:
                    dve.wait_ge(s_vo, 2 * a)
                    norm(NORM[a])
                if a == GRAPH:
                    nc.vector.memset(S[:, 2, :], 1.0)
                    dve.wait_ge(s_hist, 3 + 4 * GRAPH + 2)
                    link(nc.vector.tensor_copy(S[:, 3, :], psD[:, 0:NT]))
                    link(nc.vector.tensor_scalar(S[:, 2, 0:WINDOWS], S[:, 3, 0:WINDOWS], 1.0, 1e-12, ALU.add, ALU.max))
                    dve.sem_inc(s_deg, 1)
                    dve.wait_ge(s_sdeg, 1)
                    link(nc.vector.reciprocal(k["dinv"], k["sdeg"]))
                    dve.sem_inc(s_dinv, 1)
                    schedule_vector(0, nc, dve, link, k, S, nat_s, nat_d, nat_i, iota_t, onehot, over_w, spread, block_of, banks, s_src, s_pe, s_sch)
                if a in SCHEDULE:
                    schedule_vector(SCHEDULE[a], nc, dve, link, k, S, nat_s, nat_d, nat_i, iota_t, onehot, over_w, spread, block_of, banks, s_src, s_pe, s_sch)
                if 2 * a + X_LOADS[1] in X_LOADS[:-1]:
                    n = X_LOADS.index(2 * a + X_LOADS[1])
                    dve.wait_ge(s_x[n], 16)
                    if n == LOADS - 1:
                        dve.wait_ge(s_x[LOADS], 32)
                with dve.Fori(a, b) as i:
                    for u in range(2):
                        if a < GRAPH:
                            for half in range(2):
                                onehots(4 * i + 2 * u + 2 + half, 2 * i + u + 1, half)
                        keep_h(2 * i + u, u, a >= GRAPH)
                    if a < 20:
                        for u in range(2):
                            nc.vector.bn_stats(k["stats"][:, bass.ds(2 * i + X_LOADS[1] + u, 1), :].rearrange("p a s -> p (a s)"), tile_of(X, 2 * i + X_LOADS[1] + u)).then_inc(s_vo, 1)
            for u in range(2):
                keep_h(NT - 2 + u, u, True)
            schedule_vector(5, nc, dve, link, k, S, nat_s, nat_d, nat_i, iota_t, onehot, over_w, spread, block_of, banks, s_src, s_pe, s_sch)

        @block.tensor
        def _(pe):
            pe.sem_inc(s_T, 2)
            pe.sem_inc(s_h, 2)
            pe.sem_inc(s_hs, 2)
            for u in range(2):
                pe.sem_inc(s_xTst[u], 16)
                pe.sem_inc(s_xbst[u], 16)
            pe.wait_ge(s_const, 1)
            pe.wait_ge(s_natd, 1)
            for half in range(2):
                for g in range(BG):
                    last = nc.tensor.transpose(banks[5 + half][:, g * P:(g + 1) * P], nat_d[:, g, half * P:(half + 1) * P], k["ident"])
            last.then_inc(s_dTp, 1)
            pe.wait_ge(s_z, 1)
            nc.tensor.matmul(psD[:, 0:WINDOWS + 1], zero[:, 0:P], zero[:, 0:WINDOWS + 1], start=True, stop=False).then_inc(s_hist, 2)
            pe.wait_ge(s_w, 16)

            def transpose(t, u):
                pe.wait_ge(s_xn, t + 1)
                for c in range(C):
                    last = nc.tensor.transpose(psT[u][:, c * P:(c + 1) * P], xn[u][:, c * P:(c + 1) * P], k["ident"])
                last.then_inc(s_T, 1)

            def count(n, u):
                pe.wait_ge(s_lo, n + 1)
                for j in range(HB):
                    last = nc.tensor.matmul(psD[:, 0:WINDOWS + 1], onelo[u][:, :, j], onehi[u][:, :, j], start=False, stop=False)
                last.then_inc(s_hist, 1)

            def product(t, u):
                pe.wait_ge(s_xT, t + 1)
                pe.wait_ge(s_hs, t + 1)
                for c in range(C):
                    last = nc.tensor.matmul(psH[u][:, :], xT[u][:, c, :], W[:, c, :], start=c == 0, stop=c == C - 1)
                last.then_inc(s_h, 1)

            for u in range(2):
                transpose(u, u)
            for a, b in zip(STOPS[:-1], STOPS[1:]):
                if a == GRAPH:
                    for u in range(2):
                        count(4 * GRAPH + u, u)
                    nc.tensor.matmul(psD[:, 0:WINDOWS + 1], zero[:, 0:P], zero[:, 0:WINDOWS + 1], start=False, stop=True).then_inc(s_hist, 1)
                if a in SCHEDULE:
                    schedule_tensor(SCHEDULE[a], nc, pe, k, S, nat_i, nat_d, onehot, over_w, spread, banks, s_pe, s_sch)
                with pe.Fori(a, b) as i:
                    for u in range(2):
                        if a < GRAPH:
                            for half in range(2):
                                count(4 * i + 2 * u + half, half)
                        product(2 * i + u, u)
                        transpose(2 * i + 2 + u, u)
            for u in range(2):
                product(NT - 2 + u, u)
            schedule_tensor(5, nc, pe, k, S, nat_i, nat_d, onehot, over_w, spread, banks, s_pe, s_sch)


def mix(nc, sem, d, k, X, keep, banks, wqkv, wout, gb):
    words = SLOTS * D + SLOTS * P + 4 * D
    with nc.sbuf_tensor("rounded", [P, words], FP32R) as tensor:
        mix_in(nc, sem, d, k, X, keep, Mem(tensor, words, FP32R), banks, wqkv, wout, gb)


def mix_in(nc, sem, d, k, X, keep, rounded, banks, wqkv, wout, gb):
    A = keep.take(2 * C, D)
    B = keep.take(C, D)
    Gr = rounded.take(SLOTS, D)
    hotr = rounded.take(SLOTS, P)
    high = rounded.take(4, D)
    G, hot = Gr.bitcast(FP32), hotr.bitcast(FP32)
    idx = keep.take(SLOTS, dt=I32)
    xT = keep.take(2, D)
    kvm = keep.at
    gbb = keep.take(D)
    ek, rk, kk, vv = (keep.take(D) for _ in range(4))
    zero = keep.take(P)
    keep.at = kvm
    eq = [keep.take(2, 2 * P) for _ in range(2)]
    rq = [keep.take(2, 2 * P) for _ in range(2)]
    sums = keep.take(P)
    xb = [B[:, u, :] for u in range(2)]
    xm = [B[:, 2 + u, :] for u in range(2)]
    Wk, Wv, M, Wq = A[:, 0:C, :], A[:, C:2 * C, :], A[:, 0:C, :], A[:, C:2 * C, :]
    kvT = keep.take(C, P)
    ksum = keep.take(C, HEADS)
    total = keep.take(D)
    pad = keep.take(NT)
    sel = keep.take(C, P)[0:HEADS]
    z = flat(rq[0])[0:HEADS, 0:2 * P]
    agg_banks = 4
    s_wk, s_wv, s_wo, s_wq, s_gb = (sem(n) for n in ("wk_loaded", "wv_loaded", "wout_loaded", "wq_loaded", "b_loaded"))
    s_g = [sem(f"gathered{i}") for i in range(SLOTS)]
    s_idx, s_hot = sem("indices_ready"), sem("onehot_ready")
    s_high, s_low = sem("high_parts"), sem("low_parts")
    s_agg, s_add, s_bg = sem("step_summed"), sem("step_added"), sem("bias_added")
    s_xT = [sem(f"xT_loaded{u}") for u in range(2)]
    s_K, s_kr, s_k, s_V, s_v, s_kv = (sem(n) for n in ("k_made", "k_read", "k_ready", "v_made", "v_ready", "kv_summed"))
    s_z, s_z1, s_rz = sem("zeros_ready"), sem("norm_read"), sem("norm_inverted")
    s_Z = sem("inverses_spread")
    s_bd, s_Mp, s_M = sem("kv_blocks_ready"), sem("m_made"), sem("m_kept")
    s_xp, s_xb = sem("xT_pair_loaded"), [sem(f"xb_loaded{u}") for u in range(2)]
    s_Q, s_qr, s_q, s_D, s_qs, s_O, s_xm = (sem(n) for n in ("q_made", "q_read", "q_ready", "norm_made", "q_scaled", "attention_out", "xm_made"))
    s_xmst = [sem(f"xm_stored{u}") for u in range(2)]
    s_tot, s_ao = sem("k_totalled"), sem("act_ordered")
    s_c, s_pc = sem("vector_chain"), sem("pool_ordered")
    HALF = STEPS // 2
    KV = NT // 2
    psA, psK, psV, psKV, psS = banks[0:4], banks[4], banks[5], banks[6], banks[7]
    psQ, psO = banks[4:6], banks[6:8]

    with nc.Block() as block:
        @block.sync
        def _(sp):
            w = wqkv.rearrange("(c p) n -> p c n", p=P)
            for u in range(2):
                sp.dma_start(xT[:, u, :], d["xnT"][u]).then_inc(s_xT[u], 16)
            sp.dma_start(Wk, w[:, :, D:2 * D]).then_inc(s_wk, 16)
            sp.dma_start(Wv, w[:, :, 2 * D:3 * D]).then_inc(s_wv, 16)
            sp.dma_start(gbb, gb.rearrange("(a n) -> a n", a=1).broadcast_to([P, D])).then_inc(s_gb, 16)
            sp.dma_start(B, wout.rearrange("(c p) n -> p c n", p=P)).then_inc(s_wo, 16)
            with sp.Fori(0, KV - 1) as i:
                for u in range(2):
                    sp.wait_ge(s_V, 2 * i + u + 1)
                    sp.dma_start(xT[:, u, :], d["xnT"][bass.ds(2 * i + 2 + u, 1), :, :].rearrange("a p n -> p (a n)")).then_inc(s_xT[u], 16)
            sp.wait_ge(s_V, NT)
            sp.dma_start(Wq, w[:, :, 0:D]).then_inc(s_wq, 16)
            sp.dma_start(xT, d["xnT"][0:2].rearrange("t p n -> p t n")).then_inc(s_xp, 16)
            sp.wait_ge(s_Mp, C)
            for u in range(2):
                sp.dma_start(xb[u], d["xb"][u * P:(u + 1) * P, :]).then_inc(s_xb[u], 16)
            with sp.Fori(0, KV - 1) as j:
                sp.wait_ge(s_Q, 2 * j + 2)
                sp.dma_start(xT, d["xnT"][bass.ds(2 * j + 2, 2)].rearrange("t p n -> p t n")).then_inc(s_xp, 16)
                for u in range(2):
                    sp.wait_ge(s_xm, 2 * j + u + 3)
                    sp.dma_start(d["xm"][bass.ds((2 * j + u) * P, P), :], xm[u]).then_inc(s_xmst[u], 16)
                    sp.dma_start(xb[u], d["xb"][bass.ds((2 * j + 2 + u) * P, P), :]).then_inc(s_xb[u], 16)
            for u in range(2):
                sp.wait_ge(s_xm, 2 * KV + 1 + u)
                sp.dma_start(d["xm"][(NT - 2 + u) * P:(NT - 1 + u) * P, :], xm[u]).then_inc(s_xmst[u], 16)
            for u in range(2):
                sp.wait_ge(s_xmst[u], 16 * KV + 16)

        @block.gpsimd
        def _(pool):
            def gather(i, half):
                pool.wait_ge(s_idx, 2 * i + half + 1)
                for slot in range(half * STEPS, (half + 1) * STEPS):
                    pool.wait_ge(s_agg, STEPS * i + slot // 2 + 1)
                    pool.sem_inc(s_pc, 1)
                    pool.indirect_dma_start(G[:, slot, :], None, d["h"],
                                            bass.IndirectOffsetOnAxis(ap=idx[:, slot:slot + 1], axis=0)).then_inc(s_g[slot], 16)

            pool.wait_ge(s_z, 1)
            for half in range(2):
                gather(0, half)
            with pool.Fori(1, KV + 1) as i:
                for half in range(2):
                    t = 2 * i - 2 + half
                    pool.wait_ge(s_k, t + 2)
                    pool.wait_ge(s_tot, t + 1)
                    nc.gpsimd.tensor_tensor(total, total, kk, ALU.add).then_inc(s_tot, 1)
                    gather(i, half)
            with pool.Fori(KV + 1, TURNS) as i:
                for half in range(2):
                    gather(i, half)

        @block.scalar
        def _(act):
            def split(i, m):
                s = SPLIT[m]
                for slot in (2 * s, 2 * s + 1):
                    act.wait_ge(s_g[slot], 16 * i + 16)
                act.wait_ge(s_agg, STEPS * i + (SPLIT[m - 2] + 1 + STEPS if m >= 2 else SPLIT[m - 2] + 1))
                nc.scalar.copy(high[:, 2 * (m % 2):2 * (m % 2) + 2, :], G[:, 2 * s:2 * s + 2, :]).then_inc(s_high, 1)

            act.wait_ge(s_z, 1)
            with act.Fori(0, KV) as i:
                for u in range(2):
                    t = 2 * i + u
                    split(i, TILE_SPLIT * u)
                    split(i, TILE_SPLIT * u + 1)
                    act.wait_ge(s_K, t + 1)
                    act.wait_ge(s_k, t + 1)
                    act.sem_inc(s_ao, 1)
                    nc.scalar.activation(ek, psK[:, :], ACT.Exp, bias=pad[:, bass.ds(t, 1)])
                    nc.scalar.activation(rk, psK[:, :], ACT.Relu).then_inc(s_kr, 1)
                    act.wait_ge(s_V, t + 1)
                    act.wait_ge(s_kv, t + 1)
                    nc.scalar.copy(vv, psV[:, :]).then_inc(s_v, 1)
                    for m in range(TILE_SPLIT * u + 2, TILE_SPLIT * (u + 1)):
                        split(i, m)
            for c in range(C):
                act.wait_ge(s_Mp, c + 1)
                nc.scalar.copy(M[:, c, :], psQ[c % 2][:, :]).then_inc(s_M, 1)
            with act.Fori(KV, 2 * KV) as i:
                split(i, 0)
                split(i, 1)
                for b in range(2):
                    act.wait_ge(s_Q, 2 * i + b + 1 - 2 * KV)
                    act.wait_ge(s_O, 2 * i + 2 - 2 * KV)
                    nc.scalar.activation(flat(eq[b]), psQ[b][:, :], ACT.Exp)
                    nc.scalar.activation(flat(rq[b]), psQ[b][:, :], ACT.Relu).then_inc(s_qr, 1)
                split(i, 2)
                act.wait_ge(s_D, i + 1 - KV)
                nc.scalar.activation(z, psQ[0][0:HEADS, 0:2 * P], ACT.Identity, bias=k["epsz"][0:HEADS, :]).then_inc(s_z1, 1)
                for m in range(3, len(SPLIT)):
                    split(i, m)
            with act.Fori(2 * KV, TURNS) as i:
                for m in range(len(SPLIT)):
                    split(i, m)

        @block.vector
        def _(dve):
            link = Chain(dve, s_c)

            def refresh(half, turn):
                cols = bass.ds(turn * SLOTS + half * STEPS, STEPS)
                nc.vector.tensor_scalar(idx[:, half * STEPS:(half + 1) * STEPS], k["edge_src"][:, cols], 0.0, None, ALU.add).then_inc(s_idx, 1)
                nc.vector.tensor_tensor(
                    hotr[:, half * STEPS:(half + 1) * STEPS, :],
                    k["edge_dst"][:, cols].unsqueeze(2).to_broadcast([P, STEPS, P]),
                    k["iota"].unsqueeze(1).to_broadcast([P, STEPS, P]),
                    ALU.is_equal).then_inc(s_hot, 1)

            def split(i, m):
                rows = slice(2 * SPLIT[m], 2 * SPLIT[m] + 2)
                dve.wait_ge(s_high, len(SPLIT) * i + m + 1)
                nc.vector.tensor_tensor(Gr[:, rows, :], G[:, rows, :], high[:, 2 * (m % 2):2 * (m % 2) + 2, :].bitcast(FP32), ALU.subtract).then_inc(s_low, 1)

            def step(i, s):
                w = dve.value_load(k["win"][0:1, bass.ds(STEPS * i + s, 1)], min_val=0, max_val=WINDOWS - 1)
                dve.wait_ge(s_agg, STEPS * (i + 1) + s + 1)
                dve.wait_ge(s_add, STEPS * i + s + agg_banks)
                nc.vector.tensor_tensor(tile_of(X, w), tile_of(X, w), psA[s % agg_banks][:, :], ALU.add).then_inc(s_add, 1)

            nc.vector.memset(total, 0.0)
            nc.vector.tensor_scalar(pad, k["rowmask"], -1.0, 1e4, ALU.add, ALU.mult)
            nc.vector.memset(zero, 0.0).then_inc(s_z, 1)
            link.add(nc.vector.memset(ksum, 0.0))
            link(nc.vector.tensor_scalar(sel[:, C - 1, :], k["iota"][0:HEADS, :], float(HEAD), None, ALU.is_ge))
            for c in range(C):
                link(nc.vector.tensor_scalar(sel[:, c, :], sel[:, C - 1, :], 2.0 * c, k["pidx"][0:HEADS, :], ALU.add, ALU.is_equal))
            for half in range(2):
                refresh(half, 0)
            dve.sem_inc(s_k, 1)
            dve.wait_ge(s_gb, 16)
            with dve.Fori(0, KV) as i:
                for u in range(2):
                    t = 2 * i + u
                    split(i, TILE_SPLIT * u)
                    split(i, TILE_SPLIT * u + 1)
                    dve.wait_ge(s_kr, t + 2)
                    dve.wait_ge(s_kv, t + 1)
                    dve.wait_ge(s_tot, t + 1)
                    nc.vector.scalar_tensor_tensor(kk, ek, 1.0, rk, ALU.min, ALU.add).then_inc(s_k, 1)
                    for s in range(HALF * u, HALF * u + HALF):
                        step(i, s)
                        if s in SPLIT[TILE_SPLIT * u:TILE_SPLIT * (u + 1) - 2]:
                            split(i, SPLIT.index(s) + 2)
                        if s == HALF * u:
                            dve.wait_ge(s_add, STEPS * i + s + agg_banks + 1)
                            nc.vector.scalar_tensor_tensor(tile_of(X, t), gbb, k["sdeg"][:, bass.ds(t, 1)], tile_of(X, t), ALU.mult, ALU.add).then_inc(s_bg, 1)
                            dve.wait_ge(s_bg, t + 1)
                    refresh(u, i + 1)
            dve.wait_ge(s_kv, NT + 2)
            nc.vector.tensor_tensor(kvT, psKV[:, :].rearrange("p (c n) -> p c n", n=P), k["bd"].unsqueeze(1).to_broadcast([P, C, P]), ALU.mult)
            link(nc.vector.tensor_copy(sums[:, 0:C], psS[:, 0:C]))
            for h in range(HEADS):
                last = nc.vector.tensor_tensor(ksum[:, h // 2, h:h + 1], k["bd"][:, h % 2 * HEAD:h % 2 * HEAD + 1], sums[:, h // 2:h // 2 + 1], ALU.mult)
            last.then_inc(s_bd, 1)
            with dve.Fori(KV, 2 * KV) as i:
                def out(u):
                    dve.wait_ge(s_O, 2 * i + u + 3 - 2 * KV)
                    dve.wait_ge(s_xb[u], 16 * i + 16 - 16 * KV)
                    dve.wait_ge(s_xmst[u], 16 * i + 16 - 16 * KV)
                    nc.vector.tensor_tensor(xm[u], psO[u][:, :], xb[u], ALU.add).then_inc(s_xm, 1)

                split(i, 0)
                split(i, 1)
                for b in range(2):
                    dve.wait_ge(s_qr, 2 * i + b + 1 - 2 * KV)
                    nc.vector.scalar_tensor_tensor(flat(eq[b]), flat(eq[b]), 1.0, flat(rq[b]), ALU.min, ALU.add).then_inc(s_q, 1)
                for s in range(STEPS):
                    step(i, s)
                    if s == 1:
                        dve.wait_ge(s_z1, i + 1 - KV)
                        nc.vector.reciprocal(z, z).then_inc(s_rz, 1)
                    if s in SPLIT[:-2]:
                        split(i, SPLIT.index(s) + 2)
                    if s == 3:
                        for b in range(2):
                            dve.wait_ge(s_Z, 2 * i + b + 1 - 2 * KV)
                            nc.vector.tensor_tensor(flat(eq[b]), flat(eq[b]), psQ[b][:, :], ALU.mult).then_inc(s_qs, 1)
                        refresh(0, i + 1)
                    if s == 6:
                        out(0)
                refresh(1, i + 1)
                out(1)
            with dve.Fori(2 * KV, TURNS) as i:
                split(i, 0)
                split(i, 1)
                for s in range(STEPS):
                    step(i, s)
                    if s in SPLIT[:-2]:
                        split(i, SPLIT.index(s) + 2)
                    if s == 3:
                        refresh(0, i + 1)
                refresh(1, i + 1)
            dve.wait_ge(s_add, T + agg_banks)
            within = flat(A[:, 0:2, :])[:, 0:2 * T]
            link(nc.vector.tensor_scalar(within, k["edge_dst"][:, 0:2 * T], 0.0, None, ALU.is_ge))
            link(nc.vector.scalar_tensor_tensor(within, k["edge_dst"][:, 0:2 * T], float(P), within, ALU.is_lt, ALU.mult))
            link(nc.vector.tensor_reduce(k["covered"], within, mybir.AxisListType.X, ALU.add))

        @block.tensor
        def _(pe):
            def step(i, s):
                if s % HALF == 0:
                    pe.wait_ge(s_hot, 2 * i + s // HALF + 1)
                pe.wait_ge(s_add, STEPS * i + s + 1)
                if s in SPLIT:
                    m = SPLIT.index(s)
                    pe.wait_ge(s_low, len(SPLIT) * i + m + 1)
                    for half in range(2):
                        slot = 2 * s + half
                        nc.tensor.matmul(psA[s % agg_banks][:, :], hotr[:, slot, :], high[:, 2 * (m % 2) + half, :], start=half == 0, stop=False)
                        last = nc.tensor.matmul(psA[s % agg_banks][:, :], hotr[:, slot, :], Gr[:, slot, :], start=False, stop=half == 1)
                else:
                    for half in range(2):
                        slot = 2 * s + half
                        pe.wait_ge(s_g[slot], 16 * i + 16)
                        last = nc.tensor.matmul(psA[s % agg_banks][:, :], hot[:, slot, :], G[:, slot, :], start=half == 0, stop=half == 1)
                last.then_inc(s_agg, 1)

            pe.sem_inc(s_agg, STEPS)
            pe.sem_inc(s_add, agg_banks)
            pe.sem_inc(s_kr, 1)
            pe.sem_inc(s_v, 1)
            for u in range(2):
                pe.sem_inc(s_xmst[u], 16)
            pe.wait_ge(s_z, 1)
            for c in range(C):
                nc.tensor.matmul(psKV[:, c * P:(c + 1) * P], zero, zero, start=c == 0, stop=False)
            pe.sem_inc(s_kv, 1)
            pe.sem_inc(s_tot, 1)
            pe.wait_ge(s_wk, 16)
            pe.wait_ge(s_wv, 16)
            with pe.Fori(0, KV) as i:
                for u in range(2):
                    t = 2 * i + u
                    pe.wait_ge(s_xT[u], 16 * i + 16)
                    pe.wait_ge(s_kr, t + 1)
                    for c in range(C):
                        last = nc.tensor.matmul(psK[:, :], xT[:, u, c * P:(c + 1) * P], Wk[:, c, :], start=c == 0, stop=c == C - 1)
                    last.then_inc(s_K, 1)
                    pe.wait_ge(s_v, t + 1)
                    for c in range(C):
                        last = nc.tensor.matmul(psV[:, :], xT[:, u, c * P:(c + 1) * P], Wv[:, c, :], start=c == 0, stop=c == C - 1)
                    last.then_inc(s_V, 1)
                    for s in range(HALF * u, HALF * u + HALF):
                        step(i, s)
                    pe.wait_ge(s_k, t + 2)
                    pe.wait_ge(s_v, t + 2)
                    for c in range(C):
                        last = nc.tensor.matmul(psKV[:, c * P:(c + 1) * P], vv[:, c * P:(c + 1) * P], kk[:, c * P:(c + 1) * P], start=False, stop=False)
                    last.then_inc(s_kv, 1)
            for c in range(C):
                nc.tensor.matmul(psKV[:, c * P:(c + 1) * P], zero, zero, start=False, stop=c == C - 1)
            pe.wait_ge(s_tot, NT + 1)
            for c in range(C):
                last = nc.tensor.matmul(psS[:, c:c + 1], total[:, c * P:(c + 1) * P], k["ones"][:, 0:1], start=True, stop=True)
            last.then_inc(s_kv, 1)
            pe.wait_ge(s_bd, 1)
            pe.wait_ge(s_wo, 16)
            pe.wait_ge(s_kr, NT + 1)
            pe.wait_ge(s_v, NT + 1)
            for c in range(C):
                if c >= 2:
                    pe.wait_ge(s_M, c - 1)
                nc.tensor.matmul(psQ[c % 2][:, :], kvT[:, c, :], B[:, c, :], start=True, stop=True).then_inc(s_Mp, 1)
            pe.sem_inc(s_O, 2)
            pe.sem_inc(s_xm, 2)
            pe.sem_inc(s_qs, 2)
            pe.wait_ge(s_M, C)
            pe.wait_ge(s_wq, 16)
            with pe.Fori(KV, 2 * KV) as i:
                pe.wait_ge(s_xp, 16 * i + 16 - 16 * KV)
                pe.wait_ge(s_qs, 2 * i + 2 - 2 * KV)
                for b in range(2):
                    for half in range(2):
                        c = 2 * b + half
                        for kc in range(C):
                            last = nc.tensor.matmul(psQ[b][:, half * 2 * P:(half + 1) * 2 * P], Wq[:, kc, c * P:(c + 1) * P],
                                                    xT.rearrange("p t (c r) -> p t c r", r=P)[:, :, kc, :], start=kc == 0, stop=kc == C - 1)
                    last.then_inc(s_Q, 1)
                step(i, 0)
                step(i, 1)
                pe.wait_ge(s_q, 2 * i + 2 - 2 * KV)
                for c in range(C):
                    last = nc.tensor.matmul(psQ[0][0:HEADS, 0:2 * P], ksum[:, c, :], eq[c // 2][:, c % 2, :], start=c == 0, stop=c == C - 1)
                last.then_inc(s_D, 1)
                step(i, 2)
                step(i, 3)
                pe.wait_ge(s_rz, i + 1 - KV)
                for b in range(2):
                    for half in range(2):
                        last = nc.tensor.matmul(psQ[b][:, half * 2 * P:(half + 1) * 2 * P], sel[:, 2 * b + half, :], z, start=True, stop=True)
                    last.then_inc(s_Z, 1)
                for s in range(4, 7):
                    step(i, s)
                pe.wait_ge(s_qs, 2 * i + 4 - 2 * KV)
                for u in range(2):
                    if u == 1:
                        step(i, 7)
                    pe.wait_ge(s_xm, 2 * i + u + 1 - 2 * KV)
                    for c in range(C):
                        last = nc.tensor.matmul(psO[u][:, :], eq[c // 2][:, c % 2, u * P:(u + 1) * P], M[:, c, :], start=c == 0, stop=c == C - 1)
                    last.then_inc(s_O, 1)
            with pe.Fori(2 * KV, TURNS) as i:
                for s in range(STEPS):
                    step(i, s)


def unsorted(nc, sem, d, k, X, keep, banks, src, dst, gb):
    EB = 125
    blocks = E // EB
    GW = 7
    groups = WINDOWS // GW
    assert blocks * EB == E and groups * GW == WINDOWS
    rows = keep.take(D)
    gbb = keep.take(D)
    hot = keep.take(GW, P)
    windows = keep.take(GW, P)
    rel = keep.take(1)
    idx, to = keep.take(1, dt=I32), keep.take(1, dt=I32)
    missed = keep.take(1)
    s_n, s_flag = sem("edges_counted"), sem("flag_ready")
    s_x, s_e, s_g = sem("h_loaded"), sem("edges_loaded"), sem("rows_gathered")
    s_hot, s_sum, s_add, s_c, s_pc = sem("onehots_ready"), sem("windows_summed"), sem("windows_added"), sem("vector_chain"), sem("pool_ordered")

    def missing(eng):
        eng.wait_ge(s_flag, 1)
        return eng.If(eng.value_load(k["fallback"][0:1, 0:1], min_val=0, max_val=1) > 0)

    with nc.Block() as block:
        @block.sync
        def _(sp):
            with missing(sp):
                sp.dma_start(X, d["h"].rearrange("(t p) n -> p t n", p=P)).then_inc(s_x, 16)
                sp.dma_start(gbb, gb.rearrange("(a n) -> a n", a=1).broadcast_to([P, D])).then_inc(s_x, 16)
                with sp.Fori(0, blocks) as j:
                    a, b = (v[bass.ds(j * EB, EB)].rearrange("(p o) -> p o", o=1) for v in (src, dst))
                    sp.wait_ge(s_add, groups * j + 1)
                    sp.dma_start(idx[0:EB, :], a).then_inc(s_e, 16)
                    sp.dma_start(to[0:EB, :], b).then_inc(s_e, 16)

        @block.gpsimd
        def _(pool):
            with missing(pool):
                with pool.Fori(0, blocks) as j:
                    pool.wait_ge(s_e, 32 * j + 32)
                    pool.sem_inc(s_pc, 1)
                    pool.indirect_dma_start(rows[0:EB, :], None, d["h"], bass.IndirectOffsetOnAxis(ap=idx[0:EB, :], axis=0)).then_inc(s_g, 16)

        @block.vector
        def _(dve):
            link = Chain(dve, s_c)
            dve.wait_ge(s_n, 1)
            link(nc.vector.tensor_scalar(missed, banks[7][:, 0:1], float(E), None, ALU.is_lt))
            link(nc.vector.tensor_copy(k["fallback"], missed))
            dve.sem_inc(s_flag, 1)
            with missing(dve):
                for w in range(GW):
                    link.add(nc.vector.tensor_scalar(windows[:, w, :], k["iota"], float(P * w), None, ALU.add))
                dve.wait_ge(s_x, 32)
                for t in range(NT):
                    link.add(nc.vector.scalar_tensor_tensor(X[:, t, :], gbb, k["sdeg"][:, t:t + 1], X[:, t, :], ALU.mult, ALU.add))
                link.wait()
                dve.sem_inc(s_add, 1)
                with dve.Fori(0, blocks) as j:
                    dve.wait_ge(s_e, 32 * j + 32)
                    nc.vector.tensor_scalar(rel[0:EB, :], to[0:EB, :], 0.0, None, ALU.add).then_inc(s_c, 1)
                    for g in range(groups):
                        n = groups * j + g
                        if g == 0:
                            dve.wait_ge(s_c, j + link.n + 1)
                        nc.vector.tensor_tensor(hot[0:EB], rel[0:EB, :].unsqueeze(2).to_broadcast([EB, GW, P]), windows[0:EB], ALU.is_equal).then_inc(s_hot, 1)
                        dve.wait_ge(s_sum, n + 1)
                        for w in range(GW):
                            nc.vector.tensor_tensor(X[:, GW * g + w, :], X[:, GW * g + w, :], banks[w][:, :], ALU.add)
                        nc.vector.tensor_scalar(rel[0:EB, :], rel[0:EB, :], -float(GW * P), None, ALU.add).then_inc(s_add, 1)
                        dve.wait_ge(s_add, n + 2)

        @block.tensor
        def _(pe):
            nc.tensor.matmul(banks[7][:, 0:1], k["ones"], k["covered"], start=True, stop=True).then_inc(s_n, 1)
            with missing(pe):
                with pe.Fori(0, blocks) as j:
                    pe.wait_ge(s_g, 16 * j + 16)
                    for g in range(groups):
                        pe.wait_ge(s_hot, groups * j + g + 1)
                        for w in range(GW):
                            last = nc.tensor.matmul(banks[w][:, :], hot[0:EB, w, :], rows[0:EB, :], start=True, stop=True)
                        last.then_inc(s_sum, 1)


def ln_stats(nc, link, k, S, t=slice(0, NT)):
    st = k["stats"].rearrange("p t c -> p c t")
    link.add(nc.vector.tensor_tensor(S[:, 2, t], st[:, 1, t], st[:, 4, t], ALU.add))
    link.add(nc.vector.tensor_tensor(S[:, 3, t], st[:, 1, t], st[:, 4, t], ALU.subtract))
    link(nc.vector.tensor_tensor(S[:, 4, t], st[:, 2, t], st[:, 5, t], ALU.add))
    link.add(nc.vector.tensor_scalar(S[:, 2, t], S[:, 2, t], 0.5, None, ALU.mult))
    link(nc.vector.scalar_tensor_tensor(S[:, 3, t], S[:, 3, t], 0.25, S[:, 3, t], ALU.mult, ALU.mult))
    link(nc.vector.scalar_tensor_tensor(S[:, 1, t], S[:, 4, t], 1.0 / D, S[:, 3, t], ALU.mult, ALU.add))


def ln_scales(nc, link, k, S, t=slice(0, NT)):
    link(nc.vector.reciprocal(k["rstd"][:, t], S[:, 0, t]))
    link(nc.vector.scalar_tensor_tensor(k["nmr"][:, t], S[:, 2, t], -1.0, k["rstd"][:, t], ALU.mult, ALU.mult))


def schedule_vector(part, nc, dve, link, k, S, nat_s, nat_d, nat_i, iota_t, onehot, over_w, spread, block_of, banks, s_src, s_pe, s_sch):
    W = WINDOWS + 1
    col = [S[0:W, 4, i:i + 1] for i in range(12)]
    cnt, start, end, first, last_, nb, t0, t1, bm, some = col[:10]
    ints = S[0:W, 5, 0:4].bitcast(I32)
    ps = banks[5]
    if part == 0:
        dve.wait_ge(s_src, 48)
        nc.vector.memset(k["edge_src"], 0.0)
        nc.vector.memset(k["edge_dst"], -1.0)
        nc.vector.memset(k["win"], 0)
        nc.vector.tensor_copy(nat_i.bitcast(FP32), nat_s.bitcast(I32)).then_inc(s_sch, 1)
    if part == 1:
        dve.wait_ge(s_pe, 1)
        link(nc.vector.tensor_copy(cnt, ps[0:W, 0:1]))
        dve.sem_inc(s_sch, 1)
    if part == 2:
        dve.wait_ge(s_pe, 2)
        link(nc.vector.tensor_copy(start, ps[0:W, 1:2]))
        link(nc.vector.tensor_tensor(end, start, cnt, ALU.add))
        link.add(nc.vector.tensor_copy(ints[:, 0:1], start))
        link(nc.vector.tensor_scalar(ints[:, 1:2], end, -1.0, None, ALU.add))
        link(nc.vector.tensor_single_scalar(ints[:, 2:4], ints[:, 0:2], PAIR.bit_length() - 1, ALU.arith_shift_right))
        link.add(nc.vector.tensor_copy(first, ints[:, 2:3]))
        link.add(nc.vector.tensor_copy(last_, ints[:, 3:4]))
        link(nc.vector.tensor_scalar(some, cnt, 0.0, None, ALU.is_gt))
        link(nc.vector.tensor_scalar(nb, last_, first, 1.0, ALU.subtract, ALU.add))
        link(nc.vector.tensor_tensor(nb, nb, some, ALU.mult))
        dve.sem_inc(s_sch, 1)
    if part == 3:
        dve.wait_ge(s_pe, 3)
        link(nc.vector.tensor_copy(t0, ps[0:W, 2:3]))
        link.add(nc.vector.tensor_tensor(t1, t0, nb, ALU.add))
        link(nc.vector.tensor_tensor(bm, first, t0, ALU.subtract))
        link.add(nc.vector.tensor_scalar(over_w[0:W, :], iota_t[0:W, :], t0, None, ALU.is_ge))
        link.add(nc.vector.tensor_scalar(spread[0:W, 0, :], k["ones"][0:W, :], bm, None, ALU.mult))
        link(nc.vector.tensor_scalar(spread[0:W, 1, :], k["ones"][0:W, :], k["pidx"][0:W, :], None, ALU.mult))
        link(nc.vector.scalar_tensor_tensor(over_w[0:W, :], iota_t[0:W, :], t1, over_w[0:W, :], ALU.is_lt, ALU.mult))
        dve.sem_inc(s_sch, 1)
    if part == 4:
        dve.wait_ge(s_pe, 4)
        link.add(nc.vector.tensor_tensor(block_of, ps[:, 0:T], iota_t, ALU.add))
        link.add(nc.vector.tensor_copy(k["win"][:, 0:T], banks[6][:, 0:T]))
        link(nc.vector.tensor_scalar(over_w, banks[6][:, 0:T], float(P), None, ALU.mult))
        for g in range(BG):
            last = nc.vector.tensor_scalar(onehot[:, g, :], block_of, float(-P * g), k["pidx"], ALU.add, ALU.is_equal)
        last.then_inc(s_sch, 1)
    if part == 5:
        for half in range(2):
            to = k["edge_src"].rearrange("p (t h) -> p h t", h=2)[:, half, 0:T]
            dve.wait_ge(s_pe, 5 + half)
            nc.vector.tensor_copy(to, banks[5 + half][:, 0:T])
        for half in range(2):
            to = k["edge_dst"].rearrange("p (t h) -> p h t", h=2)[:, half, 0:T]
            dve.wait_ge(s_pe, 7 + half)
            nc.vector.tensor_tensor(to, banks[(7, 4)[half]][:, 0:T], over_w, ALU.subtract)


def schedule_tensor(part, nc, pe, k, S, nat_i, nat_d, onehot, over_w, spread, banks, s_pe, s_sch):
    W = WINDOWS + 1
    nat_f = nat_i.bitcast(FP32)
    ps = banks[5]
    if part == 1:
        pe.wait_ge(s_sch, 1)
        nc.tensor.matmul(ps[0:W, 0:1], S[:, 3, 0:W], k["ones"][:, 0:1], start=True, stop=True).then_inc(s_pe, 1)
    if part == 2:
        pe.wait_ge(s_sch, 2)
        nc.tensor.matmul(ps[0:W, 1:2], k["tri"][0:W, 0:W], S[0:W, 4, 0:1], start=True, stop=True).then_inc(s_pe, 1)
    if part == 3:
        pe.wait_ge(s_sch, 3)
        nc.tensor.matmul(ps[0:W, 2:3], k["tri"][0:W, 0:W], S[0:W, 4, 5:6], start=True, stop=True).then_inc(s_pe, 1)
    if part == 4:
        pe.wait_ge(s_sch, 4)
        nc.tensor.matmul(ps[:, 0:T], spread[0:W, 0, :], over_w[0:W, :], start=True, stop=True)
        nc.tensor.matmul(banks[6][:, 0:T], spread[0:W, 1, :], over_w[0:W, :], start=True, stop=True).then_inc(s_pe, 1)
    if part == 5:
        pe.wait_ge(s_sch, 5)
        for table, first in ((nat_f, (5, 6)), (nat_d, (7, 4))):
            for half in range(2):
                for g in range(BG):
                    last = nc.tensor.matmul(banks[first[half]][:, 0:T], table[:, g, half * P:(half + 1) * P], onehot[:, g, :], start=g == 0, stop=g == BG - 1)
                last.then_inc(s_pe, 1)


def route(nc, sem, d, k, X, keep, banks, rw):
    V = 5
    norm_tables(k, keep)
    g = [keep.take(D) for _ in range(V)]
    xm = [keep.take(D) for _ in range(V)]
    x2 = [keep.take(D) for _ in range(V)]
    xT = [keep.take(C, 2 * P) for _ in range(V)]
    lgT = keep.take(NT * P)[0:NX]
    lg = keep.take(NT, NX)
    pick = keep.take(NT, NX)
    below = keep.take(NX)
    low = keep.take(NT)
    S = k["small"]
    psT, psL, psG = banks[0:2], banks[2:2 + V], banks[7]
    s_lgT = sem("logits_transposed")
    s_w = sem("router_loaded")
    s_xm = [sem(f"xm_loaded{v}") for v in range(V)]
    s_g, s_x1, s_st, s_x1st = sem("gcn_ready"), sem("x1_made"), sem("stats_made"), sem("x1_stored")
    s_var, s_sq, s_ln = sem("variances"), sem("std_done"), sem("ln_ready")
    s_x2, s_T, s_xT, s_L, s_lg = (sem(n) for n in ("x2_made", "x2_transposed", "xT_copied", "logits_made", "logits_kept"))
    s_gate, s_e = sem("gate_gaps"), sem("gate_exps")
    s_x2st = [sem(f"x2_stored{v}") for v in range(V)]
    s_c, s_ac, s_vo = sem("vector_chain"), sem("act_ordered"), sem("vector_ordered")
    V2 = 2 * V

    def second(eng, turn):
        with eng.Fori(0, NT // V2 - 1) as i:
            for v in range(V2):
                turn(V2 * i + v, i, v, lambda n: True)
        for v in range(V2):
            turn(NT - V2 + v, NT // V2 - 1, v, lambda n: v + n < V2)

    with nc.Block() as block:
        @block.sync
        def _(sp):
            for v in range(V):
                sp.dma_start(xm[v], d["xm"][v * P:(v + 1) * P, :]).then_inc(s_xm[v], 16)
            sp.dma_start(k["wr"], rw.rearrange("(c p) e -> p c e", p=P)).then_inc(s_w, 16)

            def store(t):
                sp.dma_start(d["x1"][bass.ds(t * P, P), :], tile_of(X, t)).then_inc(s_x1st, 16)

            with sp.Fori(0, NT // V - 1) as i:
                for v in range(V):
                    sp.wait_ge(s_x1, V * i + v + 1)
                    store(V * i + v)
                    sp.dma_start(xm[v], d["xm"][bass.ds((V * i + V + v) * P, P), :]).then_inc(s_xm[v], 16)
            for v in range(V):
                sp.wait_ge(s_x1, NT - V + v + 1)
                store(NT - V + v)

            def store_x2(t, i, v, more):
                rows = d["x2"][bass.ds(t * P, P), :]
                sp.wait_ge(s_x2, t + 1)
                sp.dma_start(rows, x2[v % V]).then_inc(s_x2st[v % V], 16)

            second(sp, store_x2)
            sp.wait_ge(s_x1st, 16 * NT)
            for v in range(V):
                sp.wait_ge(s_x2st[v], 16 * (NT // V) + 16)

        @block.scalar
        def _(act):
            with act.Fori(0, NT // V) as i:
                for v in range(V):
                    t = V * i + v
                    act.wait_ge(s_st, t + 1)
                    act.sem_inc(s_ac, 1)
                    nc.scalar.activation(g[v], tile_of(X, t), ACT.Relu, scale=k["dinv"][:, bass.ds(t, 1)]).then_inc(s_g, 1)
            act.wait_ge(s_var, 1)
            nc.scalar.activation(S[:, 0, :], S[:, 1, :], ACT.Sqrt, bias=k["eps"]).then_inc(s_sq, 1)
            act.wait_ge(s_ln, 1)

            def normed(t, i, v):
                act.wait_ge(s_T, t + 1)
                act.wait_ge(s_x2st[v % V], 16 * (2 * i + v // V) + 16)
                act.sem_inc(s_ac, 1)
                nc.scalar.activation(x2[v % V], tile_of(X, t), ACT.Identity, bias=k["nmr"][:, bass.ds(t, 1)], scale=k["rstd"][:, bass.ds(t, 1)]).then_inc(s_x2, 1)

            def turn(t, i, v, more):
                act.wait_ge(s_T, t + 3)
                act.wait_ge(s_L, V * i + v // 2 + 1)
                nc.scalar.copy(xT[v // 2].rearrange("p c (u r) -> p u c r", r=P)[:, v % 2], psT[v % 2][:, :].rearrange("p (c r) -> p c r", r=P)).then_inc(s_xT, 1)
                if more(2):
                    normed(t + 2, i + (v + 2) // V2, (v + 2) % V2)

            normed(0, 0, 0)
            normed(1, 0, 1)
            second(act, turn)
            act.wait_ge(s_gate, 1)
            nc.scalar.activation(k["gate"][:, 1, :], k["gate"][:, 0, :], ACT.Exp).then_inc(s_e, 1)

        @block.vector
        def _(dve):
            link = Chain(dve, s_c)
            dve.sem_inc(s_st, V)
            with dve.Fori(0, NT // V) as i:
                for v in range(V + 1):
                    t = V * i + v
                    if v < V:
                        dve.wait_ge(s_g, t + 1)
                        dve.wait_ge(s_xm[v], 16 * i + 16)
                        nc.vector.tensor_tensor(tile_of(X, t), g[v], xm[v], ALU.add).then_inc(s_x1, 1)
                    if v > 0:
                        dve.wait_ge(s_x1, t)
                        dve.sem_inc(s_vo, 1)
                        nc.vector.bn_stats(k["stats"][:, bass.ds(t - 1, 1), :].rearrange("p a s -> p (a s)"), tile_of(X, t - 1)).then_inc(s_st, 1)
            dve.wait_ge(s_st, NT + V)
            ln_stats(nc, link, k, S)
            dve.sem_inc(s_var, 1)
            dve.wait_ge(s_sq, 1)
            ln_scales(nc, link, k, S)
            dve.sem_inc(s_ln, 1)
            with dve.Fori(0, NT // V2) as i:
                for j in range(V):
                    dve.wait_ge(s_L, V * i + j + V + 1)
                    nc.vector.tensor_scalar(lgT[:, bass.ds((V * i + j) * 2 * P, 2 * P)], psL[j][0:NX, 0:2 * P], 1.0, None, ALU.mult).then_inc(s_lg, 1)
            dve.wait_ge(s_lgT, 1)
            link(nc.vector.tensor_copy(flat(lg), psG[:, 0:NT * NX]))
            link(nc.vector.tensor_scalar(below, k["iota"][:, 0:NX], -float(NX), None, ALU.add))
            experts_of = below.unsqueeze(1).to_broadcast([P, NT, NX])
            for m, M in enumerate((k["M1"], k["M2"])):
                top = k["v12"][:, m, :]
                link(nc.vector.tensor_reduce(top, lg, mybir.AxisListType.X, ALU.max))
                link(nc.vector.tensor_tensor(pick, lg, top.unsqueeze(2).to_broadcast([P, NT, NX]), ALU.is_equal))
                link(nc.vector.tensor_tensor(pick, pick, experts_of, ALU.mult))
                link(nc.vector.tensor_reduce(low, pick, mybir.AxisListType.X, ALU.min))
                link(nc.vector.tensor_tensor(M, low.unsqueeze(2).to_broadcast([P, NT, NX]), experts_of, ALU.is_equal))
                if m == 0:
                    link(nc.vector.scalar_tensor_tensor(lg, M, -3e38, lg, ALU.mult, ALU.add))
            for M in (k["M1"], k["M2"]):
                link(nc.vector.tensor_tensor(M, M, k["rowmask"].unsqueeze(2).to_broadcast([P, NT, NX]), ALU.mult))
            link(nc.vector.tensor_tensor(k["gate"][:, 0, :], k["v12"][:, 1, :], k["v12"][:, 0, :], ALU.subtract))
            dve.sem_inc(s_gate, 1)
            dve.wait_ge(s_e, 1)
            link(nc.vector.tensor_scalar(S[:, 3, :], k["gate"][:, 1, :], 1.0, None, ALU.add))
            link(nc.vector.reciprocal(k["gate"][:, 0, :], S[:, 3, :]))
            link(nc.vector.tensor_tensor(k["gate"][:, 1, :], k["gate"][:, 1, :], k["gate"][:, 0, :], ALU.mult))

        @block.tensor
        def _(pe):
            pe.sem_inc(s_T, 2)
            pe.sem_inc(s_xT, 1)
            pe.sem_inc(s_L, V)
            pe.sem_inc(s_lg, V)
            for v in range(V):
                pe.sem_inc(s_x2st[v], 16)
            pe.wait_ge(s_w, 16)

            def transpose(t, v):
                pe.wait_ge(s_x2, t + 1)
                for c in range(C):
                    last = nc.tensor.transpose(psT[v % 2][:, c * P:(c + 1) * P], x2[v % V][:, c * P:(c + 1) * P], k["ident"])
                last.then_inc(s_T, 1)

            def turn(t, i, v, more):
                if more(1):
                    pe.wait_ge(s_xT, t + 1)
                    transpose(t + 1, (v + 1) % V2)
                pe.wait_ge(s_xT, t + 2)
                if v % 2 == 1:
                    j = v // 2
                    pe.wait_ge(s_lg, V * i + j + 1)
                    for c in range(C):
                        last = nc.tensor.matmul(psL[j][0:NX, 0:2 * P], k["wr"][:, c, :], xT[j][:, c, :], start=c == 0, stop=c == C - 1)
                    last.then_inc(s_L, 1)

            transpose(0, 0)
            second(pe, turn)
            pe.wait_ge(s_lg, NT // 2 + V)
            for t in range(NT):
                last = nc.tensor.transpose(psG[:, t * NX:(t + 1) * NX], lgT[:, t * P:(t + 1) * P], k["ident"][0:NX, 0:NX])
            last.then_inc(s_lgT, 1)


def dispatch(nc, sem, d, k, X, keep, banks, w1, b1, w2, b2, gamma, beta):
    both = keep.take(NT, NX)
    incl = keep.take(NT, NX)
    pos = keep.take(NT, NX)
    pick = keep.take(2, NT, NX)
    slot = keep.take(2, NT)
    zeros = keep.take(NT)
    nb, binc, bexc, base = (keep.take(NX) for _ in range(4))
    ni = keep.take(2, NX, dt=I32)
    ex = keep.take(MB)
    HB = 10
    lo_i, hi_i = keep.take(2, NT, dt=I32), keep.take(2, NT, dt=I32)
    hi_f = keep.take(2, NT)
    lo, hi = keep.take(2, NT, dt=BF16), keep.take(2, NT, dt=BF16)
    tile = keep.take(NT, dt=BF16)
    iota_b = keep.take(P, HB, dt=BF16)
    onelo = [keep.take(P, HB, dt=BF16) for _ in range(2)]
    onehi = [keep.take(2 * MB, HB, dt=BF16) for _ in range(2)]
    zero = keep.take(2 * MB)
    s_c, s_both, s_ps, s_pos = sem("vector_chain"), sem("choices_ready"), sem("ranks_made"), sem("zeros_ready")
    s_hot, s_inv = sem("onehots_made"), sem("slots_inverted")
    s_w = sem("experts_loaded")
    psI = banks[2]

    with nc.Block() as block:
        @block.sync
        def _(sp):
            with nc.allow_non_contiguous_dma("b1 by feature, once"):
                sp.dma_start(flat(k["b1T"]), b1.rearrange("e (c p) -> p (e c)", p=P)).then_inc(s_w, 16)
            for to, a in ((k["b2b"], b2), (k["gab"], gamma), (k["beb"], beta)):
                sp.dma_start(flat(to), a.rearrange("(o e) n -> o (e n)", o=1).broadcast_to([P, NX * D])).then_inc(s_w, 16)
            sp.dma_start(k["W1"], w1.rearrange("e (c p) f -> p (e c) f", p=P)).then_inc(s_w, 16)
            sp.dma_start(k["W2"], w2.rearrange("e (c p) n -> p (e c) n", p=P)).then_inc(s_w, 16)
            sp.wait_ge(s_w, 6 * 16)

        @block.vector
        def _(dve):
            link = Chain(dve, s_c)
            nc.vector.memset(zeros, 0.0)
            nc.vector.memset(zero, 0.0).then_inc(s_pos, 1)
            nc.vector.tensor_copy(iota_b, k["iota"].unsqueeze(2).to_broadcast([P, P, HB]))
            nc.vector.tensor_copy(tile, k["iota"][:, 0:NT])
            link(nc.vector.tensor_tensor(flat(both), flat(k["M1"]), flat(k["M2"]), ALU.add))
            dve.sem_inc(s_both, 1)
            dve.wait_ge(s_ps, 1)
            rank = banks[0][:, 0:NT * NX].rearrange("p (t e) -> p t e", e=NX)
            total = banks[1][:, 0:NT * NX].rearrange("p (t e) -> p t e", e=NX)
            for e in range(NX):
                link.add(nc.vector.tensor_tensor_scan(incl[:, :, e], total[:, :, e], zeros, 0.0, ALU.add, ALU.add))
            link.wait()
            link.add(nc.vector.tensor_tensor(pos, incl, rank, ALU.add))
            link(nc.vector.tensor_scalar(ni[:, 0, :], incl[:, NT - 1, :], float(P - 1), None, ALU.add))
            link.add(nc.vector.tensor_tensor(pos, pos, total, ALU.subtract))
            link(nc.vector.tensor_single_scalar(ni[:, 1, :], ni[:, 0, :], P.bit_length() - 1, ALU.arith_shift_right))
            link(nc.vector.tensor_copy(nb, ni[:, 1, :]))
            link(nc.vector.tensor_tensor_scan(binc, nb, zeros[:, 0:NX], 0.0, ALU.add, ALU.add))
            link(nc.vector.tensor_tensor(bexc, binc, nb, ALU.subtract))
            link(nc.vector.tensor_scalar(base, bexc, float(P), None, ALU.mult))
            link(nc.vector.tensor_tensor(pos, pos, base.unsqueeze(1).to_broadcast([P, NT, NX]), ALU.add))
            for m, M in enumerate((k["M1"], k["M2"])):
                link(nc.vector.tensor_tensor(pick[:, m], M, pos, ALU.mult))
                link(nc.vector.tensor_reduce(slot[:, m, :], pick[:, m], mybir.AxisListType.X, ALU.add))
            link(nc.vector.tensor_copy(flat(k["pos"]), flat(slot)))
            link.add(nc.vector.tensor_single_scalar(lo_i, k["pos"], P - 1, ALU.bitwise_and))
            link(nc.vector.tensor_single_scalar(hi_i, k["pos"], P.bit_length() - 1, ALU.arith_shift_right))
            link.add(nc.vector.tensor_copy(lo, lo_i))
            link(nc.vector.tensor_scalar(hi_f, hi_i, 1.0, None, ALU.add))
            link(nc.vector.tensor_tensor(hi_f, hi_f, k["rowmask"].unsqueeze(1).to_broadcast([P, 2, NT]), ALU.mult))
            link(nc.vector.tensor_scalar(hi, hi_f, -1.0, None, ALU.add))
            base_n = link.n
            with dve.Fori(0, NT // HB) as i:
                for m in range(2):
                    cols = bass.ds(i * HB, HB)
                    dve.wait_ge(s_inv, 2 * i + m + 1)
                    nc.vector.tensor_tensor(onelo[m], lo[:, m, cols].unsqueeze(1).to_broadcast([P, P, HB]), iota_b, ALU.is_equal)
                    nc.vector.tensor_tensor(onehi[m][:, 0:MB, :], hi[:, m, cols].unsqueeze(1).to_broadcast([P, MB, HB]), iota_b[:, 0:MB, :], ALU.is_equal).then_inc(s_c, 1)
                    dve.wait_ge(s_c, 2 * (2 * i + m) + base_n + 1)
                    nc.vector.tensor_tensor(onehi[m][:, MB:2 * MB, :], onehi[m][:, 0:MB, :], tile[:, cols].unsqueeze(1).to_broadcast([P, MB, HB]), ALU.mult).then_inc(s_c, 1)
                    dve.wait_ge(s_c, 2 * (2 * i + m) + base_n + 2)
                    nc.vector.tensor_scalar(onehi[m][:, 0:MB, :], onehi[m][:, 0:MB, :], k["pidx"], None, ALU.mult).then_inc(s_hot, 1)
            link.n = base_n + 4 * (NT // HB)
            link(nc.vector.tensor_scalar(ex, k["iota"][:, 0:MB], bexc[:, 1:2], None, ALU.is_ge))
            for e in range(2, NX):
                link(nc.vector.scalar_tensor_tensor(ex, k["iota"][:, 0:MB], bexc[:, e:e + 1], ex, ALU.is_ge, ALU.add))
            link(nc.vector.tensor_copy(k["expert"], ex))
            dve.wait_ge(s_inv, 2 * (NT // HB) + 3)
            link(nc.vector.tensor_copy(ex, psI[:, 0:MB]))
            link(nc.vector.scalar_tensor_tensor(ex, psI[:, MB:2 * MB], float(P), ex, ALU.mult, ALU.add))
            link(nc.vector.tensor_copy(k["token"], ex))

        @block.tensor
        def _(pe):
            pe.wait_ge(s_both, 1)
            nc.tensor.matmul(banks[0][:, 0:NT * NX], k["tri"], flat(both), start=True, stop=True)
            nc.tensor.matmul(banks[1][:, 0:NT * NX], k["ones"], flat(both), start=True, stop=True).then_inc(s_ps, 1)
            pe.wait_ge(s_pos, 1)
            nc.tensor.matmul(psI[:, 0:2 * MB], zero[:, 0:P], zero, start=True, stop=False).then_inc(s_inv, 2)
            with pe.Fori(0, NT // HB) as i:
                for m in range(2):
                    pe.wait_ge(s_hot, 2 * i + m + 1)
                    for j in range(HB):
                        last = nc.tensor.matmul(psI[:, 0:2 * MB], onelo[m][:, :, j], onehi[m][:, :, j], start=False, stop=False)
                    last.then_inc(s_inv, 1)
            nc.tensor.matmul(psI[:, 0:2 * MB], zero[:, 0:P], zero, start=False, stop=True).then_inc(s_inv, 1)


def experts(nc, sem, d, k, X, keep, banks):
    W1, W2, b1T, b2b, gab, beb = (k[n] for n in ("W1", "W2", "b1T", "b2b", "gab", "beb"))
    m = keep
    xs = [m.take(D) for _ in range(4)]
    idx = m.take(4, dt=I32)
    xb = [m.take(D) for _ in range(4)]
    xsT, hb, hT, r, n, g, y = ([m.take(w) for _ in range(2)] for w in (D, F, F, D, D, D, D))
    st, mv, sd, rs, nm = ([m.take(w) for _ in range(2)] for w in (6, 2, 1, 1, 1))
    psX, psH, psG, psY = banks[0:2], banks[2:4], banks[4:6], banks[6:8]
    s_xs = [sem(f"rows_loaded{u}") for u in range(4)]
    s_yst = [sem(f"y_stored{u}") for u in range(2)]
    s_T, s_xT, s_H, s_hb, s_G, s_hT, s_Y = (sem(n) for n in ("x_transposed", "xT_copied", "h_made", "h_biased", "h_transposed", "hT_copied", "y_made"))
    s_idx, s_ao = sem("tokens_ready"), sem("act_ordered")
    s_xb, s_r, s_v, s_sd, s_y, s_pc = (sem(n) for n in ("x_biased", "r_made", "var_made", "std_made", "y_ready", "pool_ordered"))
    s_st, s_rs, s_nm, s_n, s_g, s_vo = (sem(n) for n in ("stats_made", "rstd_made", "mean_scaled", "normed", "gamma_applied", "vector_ordered"))

    def pipeline(eng, turn, ahead, behind):
        lo, hi = 4 * -(-behind // 4), (MB - ahead) // 4 * 4
        for b in range(-ahead, lo):
            turn(b, b // 4, b % 4)
        with eng.Fori(lo // 4, hi // 4) as i:
            for u in range(4):
                turn(4 * i + u, i, u, middle=True)
        for b in range(hi, MB + behind):
            turn(b, b // 4, b % 4)

    def inside(b, middle):
        return middle or 0 <= b < MB

    with nc.Block() as block:
        @block.sync
        def _(sp):
            def turn(b, i, u, middle=False):
                rows = d["ys"][bass.ds(b * P, P), :]
                sp.wait_ge(s_y, b + 1)
                sp.dma_start(rows, y[u % 2]).then_inc(s_yst[u % 2], 16)

            pipeline(sp, turn, 0, 0)
            for v in range(2):
                sp.wait_ge(s_yst[v], 16 * (MB // 2) + 16)

        @block.gpsimd
        def _(pool):
            def turn(b, i, u, middle=False):
                v = u % 2
                if inside(b + 1, middle):
                    e1 = pool.value_load(k["expert"][0:1, bass.ds(b + 1, 1)], min_val=0, max_val=NX - 1)
                if inside(b - 3, middle):
                    e2 = pool.value_load(k["expert"][0:1, bass.ds(b - 3, 1)], min_val=0, max_val=NX - 1)
                if inside(b + 4, middle):
                    if middle or b >= 0:
                        pool.wait_ge(s_T, b + 3)
                        pool.wait_ge(s_xb, b + 3)
                    pool.wait_ge(s_idx, b + 5)
                    pool.sem_inc(s_pc, 1)
                    pool.indirect_dma_start(xs[u], None, d["x2"], bass.IndirectOffsetOnAxis(ap=idx[:, u:u + 1], axis=0)).then_inc(s_xs[u], 16)
                if inside(b + 1, middle):
                    w = (u + 1) % 4
                    pool.wait_ge(s_xs[w], 16 * (i + (u + 1) // 4) + 16)
                    if middle or b > 2:
                        pool.wait_ge(s_r, b)
                    pool.sem_inc(s_pc, 1)
                    nc.gpsimd.tensor_tensor(xb[w], xs[w], tile_of(b2b, e1), ALU.add).then_inc(s_xb, 1)
                if inside(b - 3, middle):
                    w = (u + 1) % 2
                    pool.wait_ge(s_g, b)
                    pool.wait_ge(s_yst[w], 16 * (2 * i + (u - 3) // 2) + 16)
                    pool.sem_inc(s_pc, 1)
                    nc.gpsimd.tensor_tensor(y[w], g[w], tile_of(beb, e2), ALU.add).then_inc(s_y, 1)

            pool.sem_inc(s_xb, 2)
            pipeline(pool, turn, 4, 3)

        @block.scalar
        def _(act):
            def turn(b, i, u, middle=False):
                v = u % 2
                if inside(b, middle):
                    e = act.value_load(k["expert"][0:1, bass.ds(b, 1)], min_val=0, max_val=NX - 1)
                if inside(b + 2, middle):
                    act.wait_ge(s_T, b + 5)
                    act.wait_ge(s_H, b + 3)
                    nc.scalar.copy(xsT[v], psX[v][:, :]).then_inc(s_xT, 1)
                if inside(b, middle):
                    act.wait_ge(s_G, b + 3)
                    act.wait_ge(s_Y, b + 1)
                    act.sem_inc(s_ao, 1)
                    for c in range(FC):
                        last = nc.scalar.activation(hT[v][:, c * P:(c + 1) * P], psG[v][:, c * P:(c + 1) * P], ACT.Relu, bias=tile_of(b1T, e)[:, c:c + 1])
                    last.then_inc(s_hT, 1)
                if inside(b - 2, middle):
                    act.wait_ge(s_v, b - 1)
                    nc.scalar.activation(sd[v], mv[v][:, 1:2], ACT.Sqrt, bias=k["epsm"]).then_inc(s_sd, 1)
                    act.wait_ge(s_nm, b - 1)
                    act.wait_ge(s_g, b - 1)
                    nc.scalar.activation(n[v], r[v], ACT.Identity, bias=nm[v], scale=rs[v]).then_inc(s_n, 1)

            pipeline(act, turn, 2, 2)

        @block.vector
        def _(dve):
            def turn(b, i, u, middle=False):
                v, w = u % 2, (u + 1) % 2
                if inside(b - 3, middle):
                    e = dve.value_load(k["expert"][0:1, bass.ds(b - 3, 1)], min_val=0, max_val=NX - 1)
                if inside(b + 5, middle):
                    if middle or b >= -1:
                        dve.wait_ge(s_xs[(u + 1) % 4], 16 * (i + (u + 1) // 4) + 16)
                    nc.vector.tensor_scalar(idx[:, (u + 1) % 4:(u + 1) % 4 + 1], k["token"][:, bass.ds(b + 5, 1)], 0.0, None, ALU.add).then_inc(s_idx, 1)
                if inside(b - 3, middle):
                    dve.wait_ge(s_n, b)
                    if middle or b >= 5:
                        dve.wait_ge(s_y, b - 4)
                    nc.vector.tensor_tensor(g[w], n[w], tile_of(gab, e), ALU.mult).then_inc(s_g, 1)
                if inside(b - 2, middle):
                    dve.wait_ge(s_Y, b + 1)
                    dve.wait_ge(s_xb, b + 1)
                    dve.wait_ge(s_n, b - 1)
                    nc.vector.tensor_tensor(r[v], psY[v][:, :], xb[(u + 2) % 4], ALU.add).then_inc(s_r, 1)
                    dve.wait_ge(s_r, b + 1)
                    nc.vector.bn_stats(st[v], r[v]).then_inc(s_st, 1)
                    dve.wait_ge(s_st, b - 1)
                    dve.sem_inc(s_vo, 1)
                    nc.vector.bn_aggr(mv[v], st[v]).then_inc(s_v, 1)
                if inside(b + 1, middle):
                    dve.wait_ge(s_H, b + 4)
                    dve.wait_ge(s_G, b + 2)
                    nc.vector.tensor_copy(hb[w], psH[w][:, 0:F]).then_inc(s_hb, 1)
                if inside(b - 2, middle):
                    dve.wait_ge(s_sd, b - 1)
                    nc.vector.reciprocal(rs[v], sd[v]).then_inc(s_rs, 1)
                    dve.wait_ge(s_rs, b - 1)
                    nc.vector.scalar_tensor_tensor(nm[v], mv[v][:, 0:1], -1.0, rs[v], ALU.mult, ALU.mult).then_inc(s_nm, 1)

            dve.sem_inc(s_r, 2)
            pipeline(dve, turn, 5, 3)

        @block.tensor
        def _(pe):
            def turn(b, i, u, middle=False):
                v, w = u % 2, (u + 1) % 2
                if inside(b + 1, middle):
                    e1 = pe.value_load(k["expert"][0:1, bass.ds(b + 1, 1)], min_val=0, max_val=NX - 1)
                if inside(b - 1, middle):
                    e2 = pe.value_load(k["expert"][0:1, bass.ds(b - 1, 1)], min_val=0, max_val=NX - 1)
                if inside(b + 2, middle):
                    j = (u + 2) % 4
                    pe.wait_ge(s_xs[j], 16 * (i + (u + 2) // 4) + 16)
                    pe.wait_ge(s_xT, b + 3)
                    for c in range(C):
                        last = nc.tensor.transpose(psX[v][:, c * P:(c + 1) * P], xs[j][:, c * P:(c + 1) * P], k["ident"])
                    last.then_inc(s_T, 1)
                if inside(b + 1, middle):
                    pe.wait_ge(s_xT, b + 4)
                    pe.wait_ge(s_hb, b + 2)
                    for c in range(C):
                        last = nc.tensor.matmul(psH[w][:, 0:F], xsT[w][:, c * P:(c + 1) * P], tile_of(W1, e1 * C + c), start=c == 0, stop=c == C - 1)
                    last.then_inc(s_H, 1)
                if inside(b, middle):
                    pe.wait_ge(s_hb, b + 3)
                    pe.wait_ge(s_hT, b + 1)
                    for c in range(FC):
                        last = nc.tensor.transpose(psG[v][:, c * P:(c + 1) * P], hb[v][:, c * P:(c + 1) * P], k["ident"])
                    last.then_inc(s_G, 1)
                if inside(b - 1, middle):
                    pe.wait_ge(s_hT, b + 2)
                    pe.wait_ge(s_r, b)
                    for c in range(FC):
                        last = nc.tensor.matmul(psY[w][:, :], hT[w][:, c * P:(c + 1) * P], tile_of(W2, e2 * FC + c), start=c == 0, stop=c == FC - 1)
                    last.then_inc(s_Y, 1)

            for s in (s_T, s_xT, s_H, s_hb, s_G, s_hT, s_Y, s_g, s_n):
                pe.sem_inc(s, 2)
            for u in range(2):
                pe.sem_inc(s_yst[u], 16)
            pipeline(pe, turn, 2, 1)


def combine(nc, sem, d, k, X, keep, out):
    R = 6
    m = Mem(X.rearrange("p t n -> p (t n)"), NT * D)
    x1, y1, y2, o1, o = ([m.take(D) for _ in range(R)] for _ in range(5))
    s_x1, s_y, s_st = ([sem(f"{n}{r}") for r in range(R)] for n in ("x1_loaded", "y_gathered", "out_stored"))
    s_o1, s_o = sem("first_added"), sem("out_made")
    turns = (REAL - 1) // R
    assert turns * R == REAL - 1

    with nc.Block() as block:
        @block.sync
        def _(sp):
            for r in range(R):
                sp.dma_start(x1[r], d["x1"][r * P:(r + 1) * P, :]).then_inc(s_x1[r], 16)
            def store(t, r):
                sp.wait_ge(s_o, t + 1)
                sp.dma_start(out[bass.ds(t * P, P), :], o[r]).then_inc(s_st[r], 16)

            with sp.Fori(0, turns - 1) as i:
                for r in range(R):
                    store(R * i + r, r)
                    sp.dma_start(x1[r], d["x1"][bass.ds((R * i + R + r) * P, P), :]).then_inc(s_x1[r], 16)
            for r in range(R):
                store(R * (turns - 1) + r, r)
                if r == 0:
                    sp.dma_start(x1[0], d["x1"][R * turns * P:(R * turns + 1) * P, :]).then_inc(s_x1[0], 16)
            sp.wait_ge(s_o, REAL)
            a = (REAL - 1) * P
            sp.dma_start(out[a:a + 96, :], o[0][0:96, :]).then_inc(s_st[0], 16)
            sp.dma_start(out[a + 96:N, :], o[0][96:LAST, :]).then_inc(s_st[0], 16)
            for r in range(R):
                sp.wait_ge(s_st[r], 16 * turns + 16 + (32 if r == 0 else 0))

        @block.gpsimd
        def _(pool):
            for t in range(REAL):
                r = t % R
                if t >= R:
                    pool.wait_ge(s_o, t - R + 1)
                rows = P if t < REAL - 1 else LAST
                for j, y in enumerate((y1, y2)):
                    pool.indirect_dma_start(y[r][0:rows, :], None, d["ys"], bass.IndirectOffsetOnAxis(ap=k["pos"][0:rows, j, t:t + 1], axis=0)).then_inc(s_y[r], 16)

        @block.vector
        def _(dve):
            def tile(t, i, r, rows):
                dve.wait_ge(s_x1[r], 16 * i + 16)
                dve.wait_ge(s_y[r], 32 * i + 32)
                nc.vector.scalar_tensor_tensor(o1[r][0:rows, :], y1[r][0:rows, :], k["gate"][0:rows, 0, bass.ds(t, 1)], x1[r][0:rows, :], ALU.mult, ALU.add).then_inc(s_o1, 1)
                dve.wait_ge(s_o1, t + 1)
                dve.wait_ge(s_st[r], 16 * i + 16)
                nc.vector.scalar_tensor_tensor(o[r][0:rows, :], y2[r][0:rows, :], k["gate"][0:rows, 1, bass.ds(t, 1)], o1[r][0:rows, :], ALU.mult, ALU.add).then_inc(s_o, 1)

            for r in range(R):
                dve.sem_inc(s_st[r], 16)
            with dve.Fori(0, turns) as i:
                for r in range(R):
                    tile(R * i + r, i, r, P)
            tile(REAL - 1, turns, 0, LAST)


_INS = ["x", "src", "dst", "L0_gnn_W", "L0_gnn_b", "L0_mix_w_qkv", "L0_mix_w_out", "L0_mix_b_out", "L0_ffn_router_w",
        "L0_ffn_w1", "L0_ffn_b1", "L0_ffn_w2", "L0_ffn_b2", "L0_ffn_gamma", "L0_ffn_beta"]


def kernel(**inputs):
    import concourse.bacc as bacc
    import numpy as np
    from concourse.bass_utils import run_bass_kernel_spmd

    nc = bacc.Bacc("TRN2", target_bir_lowering=False, num_devices=1)
    arrays, args = {}, []
    for name in _INS:
        a = np.ascontiguousarray(inputs[name])
        arrays[f"in_{name}"] = a
        args.append(nc.dram_tensor(f"in_{name}", a.shape, mybir.dt.from_np(a.dtype), kind="ExternalInput").ap())
    args.append(nc.dram_tensor("out_x", (N, D), FP32, kind="ExternalOutput").ap())
    build(nc, *args)
    r = run_bass_kernel_spmd(nc, [arrays], core_ids=[0])
    return r.results[0]["out_x"]
```
